# Optimizing a Trainium2 kernel written in Bass

```python
import numpy as np
import jax
import jax.numpy as jnp

def _softmax(x, axis=-1):
    return jax.nn.softmax(x, axis=axis)

def _gelu(x):
    return jax.nn.gelu(x, approximate=True)

def _silu(x):
    return jax.nn.silu(x)

def _sigmoid(x):
    return jax.nn.sigmoid(x)

def _layernorm(x, axis=-1, eps=1e-05):
    m = jnp.mean(x, axis=axis, keepdims=True)
    v = jnp.var(x, axis=axis, keepdims=True)
    return (x - m) / jnp.sqrt(v + eps)

def _scatter_add(tgt, idx, src, axis=0):
    return tgt.at[idx].add(src)

def _segment_sum(src, seg, n):
    return jax.ops.segment_sum(src, seg, n)
kernel_name = 'mk_audio_tower_d1_tok_audfeat1024_r4_14c40d'

def setup_inputs(seed: int=0):
    np.random.seed(seed)
    _w = jnp.asarray

    def _rec_inputs():
        import jax
        import jax.numpy as jnp
        _rk = jax.random.key(seed)
        x = -7.03837e-07 + 1.00017 * jax.random.normal(jax.random.fold_in(_rk, 1), (8, 256, 256), jnp.float32)
        return x
    x = _rec_inputs()

    def _L0_tok_setup():
        import jax, jax.numpy as jnp
        import numpy as np
        D, H, HD, P, S0, B, MEM = (256, 16, 64, 32, 504, 4, 512)

        def _ln(x, g, b, eps=1e-05):
            m = x.mean(-1, keepdims=True)
            v = ((x - m) ** 2).mean(-1, keepdims=True)
            return (x - m) / jnp.sqrt(v + eps) * g + b
        key = jax.random.key(seed)
        ks = jax.random.split(key, 20)
        sc = 0.02
        rn = lambda k, shp: jax.random.normal(k, shp, jnp.float32) * sc
        return {'x': jax.random.normal(ks[0], (B, S0, D), jnp.float32), 'persistent_memory': jax.random.normal(ks[1], (P, D), jnp.float32), 'Wq': rn(ks[2], (D, H * HD)), 'bq': jnp.zeros((H * HD,), jnp.float32), 'Wk': rn(ks[3], (D, H * HD)), 'bk': jnp.zeros((H * HD,), jnp.float32), 'Wv': rn(ks[4], (D, H * HD)), 'bv': jnp.zeros((H * HD,), jnp.float32), 'Wo': rn(ks[5], (H * HD, D)), 'bo': jnp.zeros((D,), jnp.float32), 'mWq': rn(ks[6], (D, D)), 'mbq': jnp.zeros((D,), jnp.float32), 'mWk': rn(ks[7], (D, D)), 'mbk': jnp.zeros((D,), jnp.float32), 'mWv': rn(ks[8], (D, D)), 'mbv': jnp.zeros((D,), jnp.float32), 'g1_w': jnp.ones((D,), jnp.float32), 'g1_b': jnp.zeros((D,), jnp.float32), 'g2_w': jnp.ones((D,), jnp.float32), 'g2_b': jnp.zeros((D,), jnp.float32), 'gate_W': rn(ks[9], (2 * D, D)), 'gate_b': jnp.zeros((D,), jnp.float32), 'window_size': 64}
    _L0_tok_all = _L0_tok_setup()
    _L0_tok_in = {k: v for k, v in _L0_tok_all.items() if k in ('persistent_memory', 'Wq', 'bq', 'Wk', 'bk', 'Wv', 'bv', 'Wo', 'bo', 'mWq', 'mbq', 'mWk', 'mbk', 'mWv', 'mbv', 'g1_w', 'g1_b', 'g2_w', 'g2_b', 'gate_W', 'gate_b')}
    del _L0_tok_all

    def _L0_attn_setup():
        import jax, jax.numpy as jnp
        import numpy as np
        import math
        INPUT_WIDTH = 256
        KEY_WIDTH = 64
        VALUE_WIDTH = 64
        NUM_HEADS = 16
        key = jax.random.key(seed)
        k_x, k_q, k_k, k_v, k_p = jax.random.split(key, 5)
        n, s = (2, 512)
        scale = 1.0 / math.sqrt(INPUT_WIDTH)
        X = jax.random.normal(k_x, (n, s, INPUT_WIDTH), dtype=jnp.float32)
        Wq = jax.random.uniform(k_q, (INPUT_WIDTH, NUM_HEADS * KEY_WIDTH), jnp.float32, -scale, scale)
        Wk = jax.random.uniform(k_k, (INPUT_WIDTH, NUM_HEADS * KEY_WIDTH), jnp.float32, -scale, scale)
        Wv = jax.random.uniform(k_v, (INPUT_WIDTH, NUM_HEADS * VALUE_WIDTH), jnp.float32, -scale, scale)
        p_scale = 1.0 / math.sqrt(NUM_HEADS * VALUE_WIDTH)
        Wpost = jax.random.uniform(k_p, (NUM_HEADS * VALUE_WIDTH, INPUT_WIDTH), jnp.float32, -p_scale, p_scale)
        return {'X': X, 'Wq': Wq, 'Wk': Wk, 'Wv': Wv, 'Wpost': Wpost}
    _L0_attn_all = _L0_attn_setup()
    _L0_attn_in = {k: v for k, v in _L0_attn_all.items() if k in ('Wq', 'Wk', 'Wv', 'Wpost')}
    del _L0_attn_all

    def _L0_ffn_setup():
        import jax, jax.numpy as jnp
        import numpy as np
        B, T, C = (4, 512, 256)
        NUM_EXPERTS = 8
        TOP_K = 2
        D_EXPERT = 4 * C * TOP_K // NUM_EXPERTS
        key = jax.random.key(seed)
        k0, k1, k2, k3 = jax.random.split(key, 4)
        x = jax.random.normal(k0, (B, T, C), dtype=jnp.float32)
        router_w = jax.random.normal(k1, (NUM_EXPERTS, C), dtype=jnp.float32) * 0.02
        w1_all = jax.random.normal(k2, (NUM_EXPERTS, C, D_EXPERT), dtype=jnp.float32) * 0.02
        w2_all = jax.random.normal(k3, (NUM_EXPERTS, D_EXPERT, C), dtype=jnp.float32) * 0.02
        return {'x': x, 'router_w': router_w, 'w1_all': w1_all, 'w2_all': w2_all}
    _L0_ffn_all = _L0_ffn_setup()
    _L0_ffn_in = {k: v for k, v in _L0_ffn_all.items() if k in ('router_w', 'w1_all', 'w2_all')}
    del _L0_ffn_all
    return {'x': x, 'L0_tok_persistent_memory': _L0_tok_in['persistent_memory'], 'L0_tok_Wq': _L0_tok_in['Wq'], 'L0_tok_bq': _L0_tok_in['bq'], 'L0_tok_Wk': _L0_tok_in['Wk'], 'L0_tok_bk': _L0_tok_in['bk'], 'L0_tok_Wv': _L0_tok_in['Wv'], 'L0_tok_bv': _L0_tok_in['bv'], 'L0_tok_Wo': _L0_tok_in['Wo'], 'L0_tok_bo': _L0_tok_in['bo'], 'L0_tok_mWq': _L0_tok_in['mWq'], 'L0_tok_mbq': _L0_tok_in['mbq'], 'L0_tok_mWk': _L0_tok_in['mWk'], 'L0_tok_mbk': _L0_tok_in['mbk'], 'L0_tok_mWv': _L0_tok_in['mWv'], 'L0_tok_mbv': _L0_tok_in['mbv'], 'L0_tok_g1_w': _L0_tok_in['g1_w'], 'L0_tok_g1_b': _L0_tok_in['g1_b'], 'L0_tok_g2_w': _L0_tok_in['g2_w'], 'L0_tok_g2_b': _L0_tok_in['g2_b'], 'L0_tok_gate_W': _L0_tok_in['gate_W'], 'L0_tok_gate_b': _L0_tok_in['gate_b'], 'L0_attn_Wq': _L0_attn_in['Wq'], 'L0_attn_Wk': _L0_attn_in['Wk'], 'L0_attn_Wv': _L0_attn_in['Wv'], 'L0_attn_Wpost': _L0_attn_in['Wpost'], 'L0_ffn_router_w': _L0_ffn_in['router_w'], 'L0_ffn_w1_all': _L0_ffn_in['w1_all'], 'L0_ffn_w2_all': _L0_ffn_in['w2_all']}

def reference(x, L0_tok_persistent_memory, L0_tok_Wq, L0_tok_bq, L0_tok_Wk, L0_tok_bk, L0_tok_Wv, L0_tok_bv, L0_tok_Wo, L0_tok_bo, L0_tok_mWq, L0_tok_mbq, L0_tok_mWk, L0_tok_mbk, L0_tok_mWv, L0_tok_mbv, L0_tok_g1_w, L0_tok_g1_b, L0_tok_g2_w, L0_tok_g2_b, L0_tok_gate_W, L0_tok_gate_b, L0_attn_Wq, L0_attn_Wk, L0_attn_Wv, L0_attn_Wpost, L0_ffn_router_w, L0_ffn_w1_all, L0_ffn_w2_all):
    import jax
    import jax.numpy as jnp

    def _L0_tok_ref(x, persistent_memory, Wq, bq, Wk, bk, Wv, bv, Wo, bo, mWq, mbq, mWk, mbk, mWv, mbv, g1_w, g1_b, g2_w, g2_b, gate_W, gate_b, window_size):
        import jax, jax.numpy as jnp
        import numpy as np
        D, H, HD, P, S0, B, MEM = (256, 16, 64, 32, 504, 4, 512)

        def _ln(x, g, b, eps=1e-05):
            m = x.mean(-1, keepdims=True)
            v = ((x - m) ** 2).mean(-1, keepdims=True)
            return (x - m) / jnp.sqrt(v + eps) * g + b
        b, s0, d = x.shape
        p = persistent_memory.shape[0]
        combined = jnp.concatenate([jnp.broadcast_to(persistent_memory[None], (b, p, d)), x], axis=1)
        S = p + s0

        def heads(t, W, bias):
            return (t @ W + bias).reshape(b, S, H, HD).transpose(0, 2, 1, 3)
        q = heads(combined, Wq, bq)
        k = heads(combined, Wk, bk)
        v = heads(combined, Wv, bv)
        scores = jnp.einsum('bhqd,bhkd->bhqk', q, k) / np.float32(np.sqrt(HD))
        i = jnp.arange(S)[:, None]
        j = jnp.arange(S)[None, :]
        disallow = (j > i) | (j < i - window_size)
        scores = jnp.where(disallow, -jnp.inf, scores)
        attn = jax.nn.softmax(scores, axis=-1)
        attn_out = jnp.einsum('bhqk,bhkd->bhqd', attn, v)
        attn_out = attn_out.transpose(0, 2, 1, 3).reshape(b, S, H * HD) @ Wo + bo
        mem_state = 0.1 * combined
        mq = combined @ mWq + mbq
        mk = mem_state @ mWk + mbk
        mv = mem_state @ mWv + mbv
        mscores = jnp.einsum('bqd,bkd->bqk', mq, mk) / np.float32(np.sqrt(D))
        mem_out = jnp.einsum('bqk,bkd->bqd', jax.nn.softmax(mscores, axis=-1), mv)
        na = _ln(attn_out, g1_w, g1_b)
        nm = _ln(mem_out, g2_w, g2_b)
        gate = jax.nn.sigmoid(jnp.concatenate([na, nm], axis=-1) @ gate_W + gate_b)
        return gate * na + (1.0 - gate) * nm

    def _L0_attn_ref(X, Wq, Wk, Wv, Wpost):
        import jax, jax.numpy as jnp
        import numpy as np
        import math
        INPUT_WIDTH = 256
        KEY_WIDTH = 64
        VALUE_WIDTH = 64
        NUM_HEADS = 16
        n, s, _ = X.shape
        Q = (X @ Wq).reshape(n, s, NUM_HEADS, KEY_WIDTH)
        K = (X @ Wk).reshape(n, s, NUM_HEADS, KEY_WIDTH)
        V = (X @ Wv).reshape(n, s, NUM_HEADS, VALUE_WIDTH)
        inv_sqrt_d = 1.0 / math.sqrt(KEY_WIDTH)
        raw_attn = jnp.einsum('bshe,bthe->bsth', Q, K * inv_sqrt_d)
        attn = jax.nn.softmax(raw_attn, axis=2)
        A = jnp.einsum('bsth,bthe->bshe', attn, V).reshape(n, s, NUM_HEADS * VALUE_WIDTH)
        A = jax.nn.gelu(A, approximate=False)
        P = A @ Wpost
        return X + P

    def _L0_ffn_ref(x, router_w, w1_all, w2_all):
        import jax, jax.numpy as jnp
        import numpy as np
        B, T, C = (4, 512, 256)
        NUM_EXPERTS = 8
        TOP_K = 2
        D_EXPERT = 4 * C * TOP_K // NUM_EXPERTS
        b, t, c = x.shape
        x_flat = x.reshape(-1, c)
        router_logits = x_flat @ router_w.T
        top_k_logits, top_k_idx = jax.lax.top_k(router_logits, TOP_K)
        router_probs = jax.nn.softmax(top_k_logits, axis=-1)
        hidden = jnp.einsum('nc,ecd->ned', x_flat, w1_all)
        hidden = jnp.square(jax.nn.relu(hidden))
        out_all = jnp.einsum('ned,edc->nec', hidden, w2_all)
        sel = jnp.take_along_axis(out_all, top_k_idx[:, :, None], axis=1)
        out = jnp.sum(sel * router_probs[:, :, None], axis=1)
        return out.reshape(b, t, c)
    h = _L0_tok_ref(x, L0_tok_persistent_memory, L0_tok_Wq, L0_tok_bq, L0_tok_Wk, L0_tok_bk, L0_tok_Wv, L0_tok_bv, L0_tok_Wo, L0_tok_bo, L0_tok_mWq, L0_tok_mbq, L0_tok_mWk, L0_tok_mbk, L0_tok_mWv, L0_tok_mbv, L0_tok_g1_w, L0_tok_g1_b, L0_tok_g2_w, L0_tok_g2_b, L0_tok_gate_W, L0_tok_gate_b, 64)
    h = h + _L0_attn_ref(_layernorm(h, axis=-1), L0_attn_Wq, L0_attn_Wk, L0_attn_Wv, L0_attn_Wpost)
    h = h + _L0_ffn_ref(_layernorm(h, axis=-1), L0_ffn_router_w, L0_ffn_w1_all, L0_ffn_w2_all)
    return h

_drawn_inputs = setup_inputs


def setup_inputs(seed=0):
    import zlib

    import numpy as np

    out = dict(_drawn_inputs(seed))
    spreads = {'L0_tok_bq': (0.0, 0.8),
     'L0_tok_bk': (0.0, 0.8),
     'L0_tok_bv': (0.0, 0.1),
     'L0_tok_bo': (0.0, 0.1),
     'L0_tok_mbq': (0.0, 0.8),
     'L0_tok_mbk': (0.0, 0.8),
     'L0_tok_mbv': (0.0, 0.1),
     'L0_tok_g1_w': (1.0, 0.2),
     'L0_tok_g1_b': (0.0, 0.1),
     'L0_tok_g2_w': (1.0, 0.2),
     'L0_tok_g2_b': (0.0, 0.1),
     'L0_tok_gate_b': (0.0, 0.1)}
    factors = {'L0_tok_Wq': 3.247,
     'L0_tok_Wk': 3.106,
     'L0_tok_mWq': 8.0,
     'L0_tok_mWk': 8.0,
     'L0_tok_mWv': 4.344,
     'L0_attn_Wq': 8.0,
     'L0_attn_Wk': 8.0,
     'L0_ffn_router_w': 3.96,
     'L0_ffn_w1_all': 3.728,
     'L0_ffn_w2_all': 3.394}
    for name, (base, spread) in spreads.items():
        noise = np.random.default_rng([zlib.crc32(name.encode()), seed]).standard_normal(out[name].shape)
        drawn = base * np.exp(spread * noise) if base else spread * noise
        out[name] = jnp.asarray(drawn.astype(out[name].dtype))
    for name, factor in factors.items():
        out[name] = (out[name] * factor).astype(out[name].dtype)
    return out
```

```python
from contextlib import ExitStack

import concourse.bass as bass
from concourse import mybir
from concourse.alu_op_type import AluOpType as ALU

F32 = mybir.dt.float32
F32R = mybir.dt.float32r
BF16 = mybir.dt.bfloat16
U32 = mybir.dt.uint32
ACT = mybir.ActivationFunctionType
AX = mybir.AxisListType

B, S0, D = 8, 256, 256
PM = 32
S = S0 + PM
T = 96
NT = S // T
KC = D // 128
H, HD = 16, 64
HP = H // 2
WINDOW = 64
E, DE = 8, 256
EC = DE // 128
INNER = H * HD
EPS = 1e-5
MASKED = -3.0e38
PIECE = 1024
STAGES = 8
WCOLS = 10752
WIN = [(0, 0, 1), (T, 0, 2), (3 * T, 1, 2)]
WINT = [(0, 0, 2), (2 * T, 1, 2), (4 * T, 2, 1)]
PRING = 3
PRIMED = 1
CONST_STEPS = 15
CHAIN_STEPS = [28, 8, 25]


class Ring:

    def __init__(self, sem, name, size, uses):
        self.size, self.uses = size, uses
        self.full = [sem(f"{name}{i}_full") for i in range(size)]
        self.free = [sem(f"{name}{i}_free") for i in range(size)]
        self.per = [(uses + size - 1 - i) // size for i in range(size)]

    def fills_before(self, b, n):
        return b * self.per[n % self.size] + n // self.size + PRIMED

    def wait_free(self, eng, b, n):
        eng.wait_ge(self.free[n % self.size], self.fills_before(b, n))

    def wait_full(self, eng, b, n):
        eng.wait_ge(self.full[n % self.size], self.fills_before(b, n) + 1)

    def wait_freed(self, eng, b, n):
        eng.wait_ge(self.free[n % self.size], self.fills_before(b, n) + 1)

    def wait_all_freed(self, eng, b, uses):
        for n in {n % self.size: n for n in sorted(uses)}.values():
            self.wait_freed(eng, b, n)

    def wait_last(self, eng, b):
        i = (self.uses - 1) % self.size
        eng.wait_ge(self.full[i], b * self.per[i] + PRIMED)

    def filled(self, ins, n):
        ins.then_inc(self.full[n % self.size], 1)

    def freed(self, ins, n):
        ins.then_inc(self.free[n % self.size], 1)


class Chain:

    def __init__(self, sem, eng, per):
        self.sem, self.eng, self.per, self.n = sem, eng, per, 0

    def start(self, b):
        self.b, self.n = b, 0

    def step(self, ins):
        ins.then_inc(self.sem, 1)
        self.n += 1

    def wait(self):
        self.eng.wait_ge(self.sem, self.b * self.per + self.n)

    def link(self, ins):
        self.step(ins)
        self.wait()

    def end(self):
        assert self.n == self.per, (self.n, self.per)


def weight_pieces(w):
    def rows(x, k, n, cols):
        return x[128 * k:128 * (k + n), :].rearrange("(k p) n -> p k n", p=128), n, cols

    def plain(name):
        return [rows(w[name], k, 1, INNER) for k in range(KC)]

    qk = float(HD) ** -0.5
    tok = [([d], [(PIECE, s)]) for name, s in (("L0_tok_Wq", qk), ("L0_tok_Wk", 1.0), ("L0_tok_Wv", 1.0))
           for d in plain(name)]
    tok += [([rows(w["L0_tok_Wo"], 4 * i, 4, D)], [(PIECE, 1.0)]) for i in range(2)]
    tok += [([rows(w["L0_tok_mWq"], 0, 2, D), rows(w["L0_tok_mWk"], 0, 2, D)],
             [(2 * D, float(D) ** -0.5), (2 * D, 0.1)]),
            ([rows(w["L0_tok_mWv"], 0, 2, D), rows(w["L0_tok_gate_W"], 0, 2, D)], [(2 * D, 0.1), (2 * D, 1.0)]),
            ([rows(w["L0_tok_gate_W"], 2, 2, D)], [(2 * D, 1.0)])]
    attn = [([d], [(PIECE, s)]) for name, s in (("L0_attn_Wq", 1.0), ("L0_attn_Wk", qk), ("L0_attn_Wv", 1.0))
            for d in plain(name)]
    attn += [([rows(w["L0_attn_Wpost"], 4 * i, 4, D)], [(PIECE, 1.0)]) for i in range(2)]
    ffn = []
    for name in ("L0_ffn_w1_all", "L0_ffn_w2_all"):
        for e in range(0, E, 2):
            src = w[name][e:e + 2].rearrange("e (k p) n -> p (e k) n", p=128)
            ffn.append(([(src, 2 * KC, DE)], [(PIECE, 1.0)]))
    return [tok, attn, ffn]


WQ, WK, WV, WO = 0, KC * INNER, 2 * KC * INNER, 3 * KC * INNER
WMQ = WO + HP * D
WMK, WMV = WMQ + KC * D, WMQ + 2 * KC * D
WG = WMV + KC * D
W1, W2 = 0, E * KC * DE


def wait_slot(eng, phase, b, h, done):
    m = h // 2
    eng.wait_ge(done, b * HP + max(m - 1, 0) + PRIMED)


def build(nc, out, **w):
    ctx = ExitStack()
    with ctx:
        def sb(name, shape, dt=F32):
            return ctx.enter_context(nc.sbuf_tensor(name, shape, dt))

        def sem(name):
            return ctx.enter_context(nc.semaphore(name))

        x = w["x"]
        h_tok = nc.dram_tensor("h_tok", (B, S, D), F32, kind="Internal").ap()
        h_attn = nc.dram_tensor("h_attn", (B, S, D), F32, kind="Internal").ap()
        pieces = weight_pieces(w)
        flat = [p for phase in pieces for p in phase]
        first_piece = [0, len(pieces[0]), len(pieces[0]) + len(pieces[1]), len(flat)]

        stage = sb("stage", [128, STAGES, PIECE])
        w_hi = sb("w_hi", [128, WCOLS], F32R)
        w_lo = sb("w_lo", [128, WCOLS], F32R)
        router = sb("router", [128, KC, E])
        router_hi = sb("router_hi", [128, KC, E], F32R)
        router_lo = sb("router_lo", [128, KC, E], F32R)
        ident = sb("ident", [T, T])
        ident_bf = sb("ident_bf", [T, T], BF16)
        mask_bf = sb("mask_bf", [T, 5 * T], BF16)
        col_bias = sb("col_bias", [128, 3, HP])
        mem_bias = sb("mem_bias", [128, 2, KC])
        rows_bc = sb("rows_bc", [T, 7, D])
        BO, MBV, G1W, G1B, G2W, G2B, GB = range(7)
        expert_no = sb("expert_no", [T, E])
        expert_no_i = sb("expert_no_i", [T, E], mybir.dt.int32)
        neg_half = sb("neg_half", [T, NT])
        xT_hi = sb("xT_hi", [128, KC, S], F32R)
        xT_lo = sb("xT_lo", [128, KC, S], F32R)
        q_hi = sb("q_hi", [128, 2, S], F32R)
        q_lo = sb("q_lo", [128, 2, S], F32R)
        k_hi = sb("k_hi", [128, 2, S], F32R)
        k_lo = sb("k_lo", [128, 2, S], F32R)
        oT_hi = sb("oT_hi", [128, HP, S], F32R)
        oT_lo = sb("oT_lo", [128, HP, S], F32R)
        h_in = sb("h_in", [T, NT, D])
        keep = sb("keep", [T, NT, D])
        work = sb("work", [T, NT, D])
        tmp = sb("tmp", [T, NT, D])
        mv = sb("mv", [T, NT, D])
        v = sb("v", [T, NT, INNER])
        probs = sb("probs", [T, PRING, NT * S])
        pT = sb("pT", [128, 4, NT * S])
        gelu = pT[:, :, :].rearrange("p a n -> p (a n)")[:, 0:HP * S].rearrange("p (m n) -> p m n", m=HP)
        neg_max = sb("neg_max", [T, H + 1, NT])
        sums = sb("sums", [T, H + 1, NT])
        recip = sb("recip", [T, H + 1, NT])
        bn = sb("bn", [T, NT, 6])
        mean_var = sb("mean_var", [T, NT, 2])
        rstd = sb("rstd", [T, NT])
        mv_flat = mv[:, :, :].rearrange("p t d -> p (t d)")

        def small(at, *shape):
            size = 1
            for s in shape:
                size *= s
            names = "abc"[:len(shape)]
            return mv_flat[:, at:at + size].rearrange(
                f"p ({' '.join(names)}) -> p {' '.join(names)}", **dict(zip(names, shape)))

        logits_T = mv_flat[0:E, 0:S]
        logits = small(S, NT, E)
        top = small(S + 24, NT, 8)
        top_no = small(S + 48, NT, 8).bitcast(U32)
        top_nof = small(S + 72, NT, 2)
        route = small(S + 80, NT, 4)
        gates = small(S + 96, 2, NT, E)

        def bank(name, shape=(128, 512)):
            return ctx.enter_context(nc.psum_tensor(name, list(shape), F32))

        A = [bank("bank_a0"), bank("bank_a1")]
        SC = [bank(f"bank_s{i}") for i in range(3)]
        TP = [bank("bank_t0"), bank("bank_t1")]
        OB = bank("bank_o")

        staged = [sem(f"staged{i}") for i in range(STAGES)]
        w_hi_done, w_lo_done = sem("w_hi_done"), sem("w_lo_done")
        const_in, const_made, const_ready = sem("const_in"), sem("const_made"), sem("const_ready")
        CONSTS = 16 * (12 + KC)
        entry_in = [sem(f"entry_in{i}") for i in range(3)]
        stored = [sem(f"stored{i}") for i in range(3)]
        gated = sem("gated")
        normed = [sem(f"normed{i}") for i in range(3)]
        stats = [sem(f"stats{i}") for i in range(3)]
        rooted = [sem(f"rooted{i}") for i in range(3)]
        chains = [sem(f"vector_chain{i}") for i in range(3)]

        heads_a = [f"{c}{m}" for m in range(2, HP) for c in "qk"]
        A_ORDER = [["x0", "x1", "mq0", "mk0", "mq1", "mk1"] + [f"v{i}" for i in range(2 * NT)]
                   + ["mv0", "mv1", "mv2", "q0", "k0", "q1", "k1", "mo0", "mo1", "mo2"] + heads_a
                   + ["c2", "c3", "wo0", "wo1", "wo2", "c0", "c1", "g0", "g1", "g2"],
                   ["x0", "x1", "q0", "k0"] + [f"v{i}" for i in range(2 * NT)] + ["q1", "k1"] + heads_a
                   + ["wo0", "wo1", "wo2"],
                   ["x0", "x1", "lg", "h0_0", "h0_1", "lt"] + [f"h{e}_{c}" for e in range(1, E) for c in range(EC)]]
        HI_ORDER = [[n for n in A_ORDER[0] if n[0] in "xqkc" or n[:2] in ("mq", "mk")],
                    [n for n in A_ORDER[1] if n[0] in "xqk"], ["x0", "x1"]]
        a_ring = [Ring(sem, f"a{i}_", 2, len(A_ORDER[i])) for i in range(3)]
        hi_done = [sem(f"hi_done{i}") for i in range(3)]
        UNITS = [NT + H, NT * H]
        s_ring = [Ring(sem, f"s{i}_", 3, UNITS[i]) for i in range(2)]
        t_ring = [Ring(sem, f"t{i}_", 2, UNITS[i]) for i in range(2)]
        p_ring = [Ring(sem, f"p{i}_", PRING, H + 1 - i) for i in range(2)]
        maxed = [sem(f"maxed{i}") for i in range(2)]
        inverted = [sem(f"inverted{i}") for i in range(2)]
        pv_done = [sem(f"pv_done{i}") for i in range(2)]
        o_hi_done = [sem(f"o_hi_done{i}") for i in range(2)]
        o_lo_done = [sem(f"o_lo_done{i}") for i in range(2)]
        gate_exp = sem("gate_exp")
        kept = sem("kept")
        joined, gelu_done, gelu_hi, gelu_lo = sem("joined"), sem("gelu_done"), sem("gelu_hi"), sem("gelu_lo")
        o_banks = Ring(sem, "expert_out", 6, NT * E)
        squared, hidden_hi, hidden_lo = sem("squared"), sem("hidden_hi"), sem("hidden_lo")
        margin_ready, margin_exp = sem("margin_ready"), sem("margin_exp")

        passed = {nc.vector: sem("vector_passed"), nc.gpsimd: sem("gpsimd_passed"), nc.tensor: sem("tensor_passed")}

        block = ctx.enter_context(nc.Block())

        def plain(eng):
            eng.sem_inc(passed[eng], 1)

        def parts_of(phase):
            for i, (_, parts) in enumerate(pieces[phase]):
                p, at = first_piece[phase] + i, 0
                for cols, scale in parts:
                    yield (p, stage[:, p % STAGES, at:at + cols], slice(PIECE * i + at, PIECE * i + at + cols), scale,
                           at + cols == sum(c for c, _ in parts))
                    at += cols

        PARTS = [sum(len(parts) for _, parts in phase) for phase in pieces]

        def s_use(ph, h, t=0):
            return h + NT if ph == 0 else NT * h + t

        def p_use(ph, h):
            return h + 1 - ph

        def row_of(ph, h, t):
            return (WIN[t][0], WIN[t][2] * T) if ph == 0 else (t * S, S)

        @block.sync
        def _(sp):
            def load_pieces(phase):
                for p in range(first_piece[phase], first_piece[phase + 1]):
                    if p >= STAGES:
                        sp.wait_ge(w_lo_done, p - STAGES + 1)
                    at = 0
                    for src, n, cols in flat[p][0]:
                        sp.dma_start(stage[:, p % STAGES, at:at + n * cols].rearrange("p (k n) -> p k n", k=n), src)\
                          .then_inc(staged[p % STAGES], 16)
                        at += n * cols

            def load_x(b):
                sp.dma_start(h_in[PM:T, 0, :], x[b, 0:T - PM, :]).then_inc(entry_in[0], 16)
                sp.dma_start(h_in[:, 1:NT, :], x[b, T - PM:S0, :].rearrange("(t p) d -> p t d", p=T))\
                  .then_inc(entry_in[0], 16)

            def store(phase, dst, b):
                if phase == 0:
                    sp.wait_ge(gated, b + 1)
                if phase == 1:
                    a_ring[1].wait_all_freed(sp, b, [A_ORDER[1].index(f"wo{t}") for t in range(NT)])
                if phase == 2:
                    o_banks.wait_all_freed(sp, b, [NT * (E - 1) + t for t in range(NT)])
                sp.dma_start(dst[b].rearrange("(t p) d -> p t d", p=T), tmp[:, :, :]).then_inc(stored[phase], 16)

            def load_h(phase, src, b):
                sp.dma_start(h_in[:, :, :], src[b].rearrange("(t p) d -> p t d", p=T)).then_inc(entry_in[phase], 16)

            sp.dma_start(h_in[0:PM, 0, :], w["L0_tok_persistent_memory"]).then_inc(entry_in[0], 16)
            load_x(0)
            for i, name in enumerate(("bq", "bk", "bv")):
                sp.dma_start(col_bias[:, i, :], w["L0_tok_" + name].rearrange("(m p) -> p m", p=128),
                             allow_slow_non_contiguous=True).then_inc(const_in, 16)
            for i, name in enumerate(("mbq", "mbk")):
                sp.dma_start(mem_bias[:, i, :], w["L0_tok_" + name].rearrange("(m p) -> p m", p=128),
                             allow_slow_non_contiguous=True).then_inc(const_in, 16)
            for i, name in enumerate(("bo", "mbv", "g1_w", "g1_b", "g2_w", "g2_b", "gate_b")):
                sp.dma_start(rows_bc[:, i, :], w["L0_tok_" + name].partition_broadcast(T)).then_inc(const_in, 16)
            for k in range(KC):
                sp.dma_start(router[:, k, :], w["L0_ffn_router_w"][:, 128 * k:128 * k + 128].rearrange("e p -> p e"),
                             allow_slow_non_contiguous=True).then_inc(const_in, 16)
            load_pieces(0)
            load_pieces(1)
            with sp.Fori(0, B - 1) as b:
                a_ring[0].wait_freed(sp, b, 1)
                load_x(b + 1)
                store(0, h_tok, b)
            store(0, h_tok, B - 1)
            sp.wait_ge(stored[0], 16 * B + PRIMED)
            load_h(1, h_tok, 0)
            load_pieces(2)
            with sp.Fori(0, B - 1) as b:
                sp.wait_ge(kept, b + 1)
                load_h(1, h_tok, b + 1)
                store(1, h_attn, b)
            store(1, h_attn, B - 1)
            sp.wait_ge(stored[1], 16 * B + PRIMED)
            load_h(2, h_attn, 0)
            with sp.Fori(0, B - 1) as b:
                o_banks.wait_all_freed(sp, b, range(NT))
                load_h(2, h_attn, b + 1)
                store(2, out, b)
            store(2, out, B - 1)
            sp.wait_ge(stored[2], 16 * B + PRIMED)

        @block.gpsimd
        def _(pool):
            n = 0

            def made(ins):
                nonlocal n
                n += 1
                ins.then_inc(const_made, 1)
                pool.wait_ge(const_made, n)

            made(pool.memset(ident[:, :], 0.0))
            made(pool.affine_select(out=ident[:, :], in_=ident[:, :], compare_op=ALU.not_equal, fill=1.0, base=0,
                                    pattern=[[-1, T]], channel_multiplier=1))
            made(pool.tensor_copy(ident_bf[:, :], ident[:, :]))
            made(pool.memset(tmp[:, :, :], 0.0))
            for t in range(NT):
                c, n_kt = WIN[t][0], WIN[t][2]
                off = (t - WIN[t][1]) * T
                m = tmp[:, :, :].rearrange("p t d -> p (t d)")[:, c:c + n_kt * T]
                made(pool.affine_select(out=m, in_=m, compare_op=ALU.is_ge, fill=MASKED, base=off,
                                        pattern=[[-1, n_kt * T]], channel_multiplier=1))
                made(pool.affine_select(out=m, in_=m, compare_op=ALU.is_ge, fill=MASKED, base=WINDOW - off,
                                        pattern=[[1, n_kt * T]], channel_multiplier=-1))
            made(pool.tensor_copy(mask_bf[:, :], tmp[:, :, :].rearrange("p t d -> p (t d)")[:, 0:5 * T]))
            made(pool.iota(expert_no_i[:, :], pattern=[[1, E]], base=0, channel_multiplier=0))
            made(pool.tensor_copy(expert_no[:, :], expert_no_i[:, :]))
            made(pool.memset(neg_half[:, :], -0.5))
            pool.wait_ge(const_in, CONSTS)
            made(pool.tensor_scalar(col_bias[:, 0, :], col_bias[:, 0, :], float(HD) ** -0.5, 1.0, ALU.mult, ALU.mult))
            pool.tensor_scalar(mem_bias[:, 0, :], mem_bias[:, 0, :], float(D) ** -0.5, 1.0, ALU.mult, ALU.mult)\
                .then_inc(const_ready, 1)

            def root(phase, count):
                pool.wait_ge(stats[phase], count)
                pool.tensor_tensor(rstd[:, :], rstd[:, :], neg_half[:, :], ALU.pow).then_inc(rooted[phase], 1)

            def scale_head(ph, b, h):
                pool.wait_ge(inverted[ph], b * H + h + 1)
                plain(pool)
                for t in range(NT):
                    c, cols = row_of(ph, h, t)
                    row = probs[:, p_use(ph, h) % PRING, c:c + cols]
                    ins = pool.tensor_scalar(row, row, recip[:, h, t:t + 1], 1.0, ALU.mult, ALU.mult)
                p_ring[ph].filled(ins, p_use(ph, h))

            with pool.Fori(0, B) as b:
                for h in range(H):
                    scale_head(0, b, h)
                    if h == 1:
                        root(0, 2 * b + 1)
                root(0, 2 * b + 2)
            with pool.Fori(0, B) as b:
                root(1, b + 1)
                for h in range(H):
                    scale_head(1, b, h)
                for g in range(HP // 2):
                    pool.wait_ge(gelu_hi, b * (HP // 2) + g + 1)
                    pool.tensor_tensor(oT_lo[:, 2 * g:2 * g + 2, :], gelu[:, 2 * g:2 * g + 2, :],
                                       oT_hi[:, 2 * g:2 * g + 2, :].bitcast(F32), ALU.subtract).then_inc(gelu_lo, 1)
            with pool.Fori(0, B) as b:
                root(2, b + 1)

        @block.tensor
        def _(pe):
            def product(dst, ops, start=True, stop=True):
                n = 3 * len(ops)
                i = 0
                for (l_hi, l_lo), (r_hi, r_lo) in ops:
                    for l, r in ((l_hi, r_hi), (l_hi, r_lo), (l_lo, r_hi)):
                        ins = pe.matmul(dst, l, r, start=start and i == 0, stop=stop and i == n - 1,
                                        skip_group_check=not start)
                        i += 1
                return ins

            def wcols(at, n):
                return w_hi[:, at:at + n], w_lo[:, at:at + n]

            def xcols(k, t=None):
                c = slice(0, S) if t is None else slice(t * T, t * T + T)
                return xT_hi[:, k, c], xT_lo[:, k, c]

            rings = a_ring + s_ring + t_ring + p_ring + [o_banks]
            for primed in ([s for ring in rings for s in ring.full + ring.free] + pv_done + o_lo_done + stored
                           + [squared, hidden_lo]):
                pe.sem_inc(primed, PRIMED)

            for phase in range(3):
                a, order = a_ring[phase], A_ORDER[phase]

                def fill(b, name, emit):
                    n = order.index(name)
                    a.wait_free(pe, b, n)
                    a.filled(emit(A[n % 2]), n)

                def ready(b, *names):
                    a.wait_all_freed(pe, b, [order.index(name) for name in names])

                def turn_in(b, names, src):
                    for k, name in enumerate(names):
                        def emit(bank):
                            for t in range(NT):
                                ins = pe.transpose(bank[:, t * T:t * T + T], src[:, t, 128 * k:128 * k + 128],
                                                   ident[:, :])
                            return ins
                        fill(b, name, emit)

                def chunk(b, name, at, width, m):
                    fill(b, name, lambda bank: product(bank[:, 0:S], [
                        (wcols(at + k * width + 128 * m, 128), xcols(k)) for k in range(KC)]))

                def natural(b, name, at, width, cols, t):
                    fill(b, name, lambda bank: product(bank[0:T, 0:cols.stop - cols.start], [
                        (xcols(k, t), wcols(at + k * width + cols.start, cols.stop - cols.start)) for k in range(KC)]))

                def values(b):
                    for i in range(2 * NT):
                        natural(b, f"v{i}", WV, INNER, slice(512 * (i % 2), 512 * (i % 2) + 512), i // 2)

                def scores(b, h):
                    s, half, m = s_ring[phase], 64 * (h % 2), h // 2
                    rows = slice(half, half + HD)
                    ready(b, f"q{m}", f"k{m}")
                    if phase == 0:
                        n = s_use(0, h)
                        s.wait_free(pe, b, n)
                        bank = SC[n % 3]
                        pe.matmul(bank[0:T, 0:5 * T], ident_bf[:, :], mask_bf[:, :], start=True, stop=True)
                        for t in range(NT):
                            c, kt, n_kt = WIN[t]
                            keys, mine = slice(kt * T, (kt + n_kt) * T), slice(t * T, t * T + T)
                            ins = product(bank[0:T, c:c + n_kt * T], [
                                ((q_hi[rows, m % 2, mine], q_lo[rows, m % 2, mine]),
                                 (k_hi[rows, m % 2, keys], k_lo[rows, m % 2, keys]))], start=False)
                        s.filled(ins, n)
                        return
                    for t in range(NT):
                        n, mine = s_use(1, h, t), slice(t * T, t * T + T)
                        s.wait_free(pe, b, n)
                        s.filled(product(SC[n % 3][0:T, 0:S], [
                            ((q_hi[rows, m % 2, mine], q_lo[rows, m % 2, mine]),
                             (k_hi[rows, m % 2, :], k_lo[rows, m % 2, :]))]), n)

                def turn_square(b, p_n, t_first):
                    p_ring[phase].wait_full(pe, b, p_n)
                    for kt in range(NT):
                        n = t_first + kt
                        t_ring[phase].wait_free(pe, b, n)
                        for t in range(NT):
                            ins = pe.transpose(TP[n % 2][0:T, t * T:t * T + T],
                                               probs[:, p_n % PRING, t * S + kt * T:t * S + kt * T + T], ident[:, :])
                        t_ring[phase].filled(ins, n)

                def turn_probs(b, h):
                    if phase == 1:
                        turn_square(b, p_use(1, h), NT * h)
                        return
                    n = NT + h
                    p_ring[0].wait_full(pe, b, p_use(0, h))
                    t_ring[0].wait_free(pe, b, n)
                    for kt in range(NT):
                        c, qt, n_qt = WINT[kt]
                        for i in range(n_qt):
                            src = WIN[qt + i][0] + (kt - WIN[qt + i][1]) * T
                            ins = pe.transpose(TP[n % 2][0:T, c + i * T:c + i * T + T],
                                               probs[:, p_use(0, h) % PRING, src:src + T], ident[:, :])
                    t_ring[0].filled(ins, n)

                def attend(b, m):
                    t_ring[phase].wait_all_freed(pe, b, [NT + 2 * m, NT + 2 * m + 1] if phase == 0
                                                 else range(2 * m * NT, (2 * m + 2) * NT))
                    pe.wait_ge(o_lo_done[phase], b * HP + m + PRIMED)
                    for kt in range(NT):
                        c, qt, n_qt = WINT[kt] if phase == 0 else (kt * S, 0, NT)
                        for h in (2 * m, 2 * m + 1):
                            half = 64 * (h % 2)
                            ins = pe.matmul(OB[half:half + HD, qt * T:(qt + n_qt) * T],
                                            v[:, kt, h * HD:h * HD + HD], pT[0:T, h % 4, c:c + n_qt * T],
                                            start=kt == 0, stop=kt == NT - 1, skip_group_check=True)
                    ins.then_inc(pv_done[phase], 1)

                def project_out(b):
                    for t in range(NT):
                        mine = slice(t * T, t * T + T)
                        fill(b, f"wo{t}", lambda bank: product(bank[0:T, 0:D], [
                            ((oT_hi[:, m, mine], oT_lo[:, m, mine]), wcols(WO + m * D, D)) for m in range(HP)]))

                def memory_scores(b):
                    ready(b, "mq0", "mk0", "mq1", "mk1")
                    for t in range(NT):
                        mine = slice(t * T, t * T + T)
                        s_ring[0].wait_free(pe, b, t)
                        s_ring[0].filled(product(SC[t][0:T, 0:S], [
                            ((q_hi[:, c, mine], q_lo[:, c, mine]), (k_hi[:, c, :], k_lo[:, c, :]))
                            for c in range(KC)]), t)

                def memory_attend(b):
                    t_ring[0].wait_all_freed(pe, b, range(NT))
                    ready(b, "mv2")
                    for t in range(NT):
                        def emit(bank):
                            for kt in range(NT):
                                ins = pe.matmul(bank[0:T, 0:D], pT[0:T, 2, kt * S + t * T:kt * S + t * T + T],
                                                mv[:, kt, :], start=kt == 0, stop=kt == NT - 1)
                            return ins
                        fill(b, f"mo{t}", emit)

                if phase == 0:
                    pe.wait_ge(const_made, CONST_STEPS)
                    pe.wait_ge(const_ready, 1)
                else:
                    pe.wait_ge(stored[phase - 1], 16 * B + PRIMED)
                pe.wait_ge(w_lo_done, first_piece[phase + 1] + (phase == 2))

                if phase < 2:
                    with pe.Fori(0, B) as b:
                        if phase == 0:
                            pe.wait_ge(entry_in[0], b * 32 + 48)
                            turn_in(b, ("x0", "x1"), h_in)
                            ready(b, "x0", "x1")
                            for c in range(KC):
                                chunk(b, f"mq{c}", WMQ, D, c)
                                chunk(b, f"mk{c}", WMK, D, c)
                            values(b)
                            memory_scores(b)
                            for t in range(NT):
                                natural(b, f"mv{t}", WMV, D, slice(0, D), t)
                            chunk(b, "q0", WQ, INNER, 0)
                            chunk(b, "k0", WK, INNER, 0)
                        else:
                            pe.wait_ge(normed[1], b + 1)
                            turn_in(b, ("x0", "x1"), work)
                            ready(b, "x0", "x1")
                            chunk(b, "q0", WQ, INNER, 0)
                            chunk(b, "k0", WK, INNER, 0)
                            values(b)
                        for h in range(H + 3):
                            if h % 2 == 0 and h // 2 + 1 < HP:
                                chunk(b, f"q{h // 2 + 1}", WQ, INNER, h // 2 + 1)
                                chunk(b, f"k{h // 2 + 1}", WK, INNER, h // 2 + 1)
                            if h < H:
                                scores(b, h)
                            if phase == 0 and h == 0:
                                turn_square(b, 0, 0)
                            if phase == 0 and h == 1:
                                memory_attend(b)
                            if 2 <= h < H + 2:
                                turn_probs(b, h - 2)
                            if h % 2 == 0 and h >= 4:
                                attend(b, h // 2 - 2)
                        if phase == 0:
                            pe.wait_ge(normed[0], 2 * b + 1)
                            turn_in(b, ("c2", "c3"), keep)
                            pe.wait_ge(o_lo_done[0], b * HP + HP + PRIMED)
                            project_out(b)
                            pe.wait_ge(normed[0], 2 * b + 2)
                            turn_in(b, ("c0", "c1"), work)
                            ready(b, "c0", "c1", "c2", "c3")
                            for t in range(NT):
                                mine = slice(t * T, t * T + T)
                                fill(b, f"g{t}", lambda bank: product(bank[0:T, 0:D], [
                                    ((src_hi[:, c, mine], src_lo[:, c, mine]), wcols(WG + (2 * i + c) * D, D))
                                    for i, (src_hi, src_lo) in enumerate(((q_hi, q_lo), (k_hi, k_lo)))
                                    for c in range(KC)]))
                        else:
                            pe.wait_ge(gelu_lo, b * (HP // 2) + HP // 2)
                            project_out(b)
                    continue

                with pe.Fori(0, B) as b:
                    pe.wait_ge(normed[2], b + 1)
                    turn_in(b, ("x0", "x1"), work)
                    ready(b, "x0", "x1")
                    fill(b, "lg", lambda bank: product(bank[0:E, 0:S], [
                        ((router_hi[:, k, :], router_lo[:, k, :]), xcols(k)) for k in range(KC)]))

                    def hidden(e):
                        for c in range(EC):
                            chunk(b, f"h{e}_{c}", W1 + e * KC * DE, DE, c)

                    def expert_out(e):
                        pe.wait_ge(hidden_lo, (b * E + e + 1) * EC + PRIMED)
                        for t in range(NT):
                            n, mine = NT * e + t, slice(t * T, t * T + T)
                            o_banks.wait_free(pe, b, n)
                            o_banks.filled(product((SC + TP + [OB])[n % 6][0:T, 0:D], [
                                ((oT_hi[:, 2 * (e % 2) + c, mine], oT_lo[:, 2 * (e % 2) + c, mine]),
                                 wcols(W2 + (e * EC + c) * D, D)) for c in range(EC)]), n)

                    hidden(0)
                    ready(b, "lg")

                    def emit(bank):
                        plain(pe)
                        for t in range(NT):
                            ins = pe.transpose(bank[0:T, t * E:t * E + E], logits_T[:, t * T:t * T + T], ident[0:E, 0:E])
                        return ins
                    fill(b, "lt", emit)
                    for e in range(1, E):
                        hidden(e)
                        expert_out(e - 1)
                    expert_out(E - 1)

        @block.scalar
        def _(act):
            def split_weights(phase):
                for p, src, cols, scale, _ in parts_of(phase):
                    act.wait_ge(staged[p % STAGES], 16 * sum(len(flat[n][0]) for n in range(p % STAGES, p + 1, STAGES)))
                    act.activation(w_hi[:, cols], src, ACT.Copy, scale=scale).then_inc(w_hi_done, 1)

            for phase in range(3):
                a, order = a_ring[phase], A_ORDER[phase]

                def hi(b, name, dst, bias=None):
                    n = order.index(name)
                    a.wait_full(act, b, n)
                    if bias is None:
                        ins = act.activation(dst, A[n % 2][:, 0:S], ACT.Copy)
                    else:
                        ins = act.activation(dst, A[n % 2][:, 0:S], ACT.Identity, bias=bias)
                    ins.then_inc(hi_done[phase], 1)

                def copy_out(b, name, dst, cols):
                    n = order.index(name)
                    a.wait_full(act, b, n)
                    a.freed(act.activation(dst, A[n % 2][0:dst.shape[0], 0:cols], ACT.Copy), n)

                def hi_qk(b, m):
                    if m >= 2:
                        h = 2 * m - 3
                        s_ring[phase].wait_full(act, b, s_use(phase, h, NT - 1))
                    elif phase == 0:
                        for t in range(NT):
                            s_ring[0].wait_full(act, b, t)
                    for c, dst in (("q", q_hi), ("k", k_hi)):
                        bias = col_bias[:, "qk".index(c), m:m + 1] if phase == 0 else None
                        hi(b, f"{c}{m}", dst[:, m % 2, :], bias)

                def copy_values(b):
                    for i in range(2 * NT):
                        copy_out(b, f"v{i}", v[:, i // 2, 512 * (i % 2):512 * (i % 2) + 512], 512)

                def exp_head(b, h):
                    p_n = p_use(phase, h)
                    if p_n >= PRING:
                        before = h - PRING
                        t_ring[phase].wait_full(act, b, NT * before + NT - 1 if phase else NT + before)
                    for t in range(NT):
                        n = s_use(phase, h, t)
                        c, cols = row_of(phase, h, t)
                        if phase == 1 or t == 0:
                            act.wait_ge(maxed[phase], b * UNITS[phase] + n + 1)
                        at = c if phase == 0 else 0
                        ins = act.activation(probs[:, p_n % PRING, c:c + cols], SC[n % 3][0:T, at:at + cols], ACT.Exp,
                                             bias=neg_max[:, h, t:t + 1], accum_out=sums[:, h, t:t + 1])
                        if phase == 1 or t == NT - 1:
                            s_ring[phase].freed(ins, n)

                def copy_turned(b, h):
                    for n in ([NT + h] if phase == 0 else range(NT * h, NT * h + NT)):
                        if n % 2:
                            wait_slot(act, phase, b, h, pv_done[phase])
                            t_ring[phase].wait_full(act, b, n)
                            c, cols = (0, 5 * T) if phase == 0 else ((n - NT * h) * S, S)
                            t_ring[phase].freed(act.activation(pT[0:T, h % 4, c:c + cols], TP[1][0:T, 0:cols],
                                                               ACT.Copy), n)

                def hi_out(b, m):
                    act.wait_ge(pv_done[phase], b * HP + m + 1 + PRIMED)
                    if phase == 0:
                        ins = act.activation(oT_hi[:, m, :], OB[:, 0:S], ACT.Identity, bias=col_bias[:, 2, m:m + 1])
                    else:
                        ins = act.activation(oT_hi[:, m, :], OB[:, 0:S], ACT.Copy)
                    ins.then_inc(o_hi_done[phase], 1)

                if phase == 0:
                    act.wait_ge(const_ready, 1)
                    split_weights(0)
                else:
                    act.wait_ge(stored[phase - 1], 16 * B + PRIMED)
                    if phase == 2:
                        act.activation(router_hi[:, :, :], router[:, :, :], ACT.Copy).then_inc(w_hi_done, 1)
                    split_weights(phase)

                if phase < 2:
                    with act.Fori(0, B) as b:
                        a.wait_last(act, b)
                        hi(b, "x0", xT_hi[:, 0, :])
                        hi(b, "x1", xT_hi[:, 1, :])
                        if phase == 0:
                            for c in range(KC):
                                hi(b, f"mq{c}", q_hi[:, c, :], mem_bias[:, 0, c:c + 1])
                                hi(b, f"mk{c}", k_hi[:, c, :], mem_bias[:, 1, c:c + 1])
                            copy_values(b)
                            for t in range(NT):
                                act.wait_ge(maxed[0], b * UNITS[0] + t + 1)
                                ins = act.activation(probs[:, 0, t * S:t * S + S], SC[t][0:T, 0:S], ACT.Exp,
                                                     bias=neg_max[:, H, t:t + 1], accum_out=sums[:, H, t:t + 1])
                                s_ring[0].freed(ins, t)
                            for t in range(NT):
                                copy_out(b, f"mv{t}", mv[:, t, :], D)
                            hi_qk(b, 0)
                        else:
                            hi_qk(b, 0)
                            copy_values(b)
                        for h in range(H + 3):
                            if h % 2 == 0 and h // 2 + 1 < HP:
                                hi_qk(b, h // 2 + 1)
                            if h < H:
                                exp_head(b, h)
                            if phase == 0 and h == 0:
                                t_ring[0].wait_full(act, b, 1)
                                t_ring[0].freed(act.activation(pT[0:T, 2, S:2 * S], TP[1][0:T, 0:S], ACT.Copy), 1)
                            if 2 <= h < H + 2:
                                copy_turned(b, h - 2)
                            if h % 2 == 0 and h >= 4:
                                hi_out(b, h // 2 - 2)
                        if phase == 0:
                            for name, dst in (("c2", k_hi[:, 0, :]), ("c3", k_hi[:, 1, :]), ("c0", q_hi[:, 0, :]),
                                              ("c1", q_hi[:, 1, :])):
                                hi(b, name, dst)
                            for t in range(NT):
                                a.wait_freed(act, b, order.index(f"g{t}"))
                                act.activation(tmp[:, t, :], tmp[:, t, :], ACT.Exp, scale=-1.0).then_inc(gate_exp, 1)
                        else:
                            for g in range(HP // 2):
                                act.wait_ge(joined, b * (HP // 2) + g + 1)
                                act.activation(gelu[:, 2 * g:2 * g + 2, :], gelu[:, 2 * g:2 * g + 2, :], ACT.Gelu)\
                                   .then_inc(gelu_done, 1)
                    continue

                with act.Fori(0, B) as b:
                    o_banks.wait_last(act, b)
                    hi(b, "x0", xT_hi[:, 0, :])
                    hi(b, "x1", xT_hi[:, 1, :])
                    copy_out(b, "lg", logits_T[:, :], S)

                    def relu(i):
                        e, c = i // EC, i % EC
                        n = order.index(f"h{e}_{c}")
                        a.wait_full(act, b, n)
                        act.wait_ge(squared, b * E * EC + max(i - 1, 0) + PRIMED)
                        a.freed(act.activation(pT[:, i % 2, 0:S], A[n % 2][:, 0:S], ACT.Relu), n)

                    def hi_hidden(i):
                        e, c = i // EC, i % EC
                        act.wait_ge(squared, b * E * EC + i + 1 + PRIMED)
                        if e >= 2:
                            o_banks.wait_full(act, b, NT * (e - 2) + NT - 1)
                        act.activation(oT_hi[:, 2 * (e % 2) + c, :], pT[:, 2 + i % 2, 0:S], ACT.Copy)\
                           .then_inc(hidden_hi, 1)

                    for i in range(E * EC + 1):
                        if i < E * EC:
                            relu(i)
                        if i >= 1:
                            hi_hidden(i - 1)
                        if i == 3:
                            act.wait_ge(margin_ready, b + 1)
                            act.activation(route[:, :, 1], route[:, :, 0], ACT.Exp).then_inc(margin_exp, 1)

        @block.vector
        def _(dve):
            lo_n = [0]

            def split_weights(phase):
                for p, src, cols, scale, last in parts_of(phase):
                    lo_n[0] += 1
                    dve.wait_ge(w_hi_done, lo_n[0])
                    ins = dve.scalar_tensor_tensor(out=w_lo[:, cols], in0=src, scalar=scale,
                                                   in1=w_hi[:, cols].bitcast(F32), op0=ALU.mult, op1=ALU.subtract)
                    if last:
                        ins.then_inc(w_lo_done, 1)

            for phase in range(3):
                a, order = a_ring[phase], A_ORDER[phase]
                chain = Chain(chains[phase], dve, CHAIN_STEPS[phase])

                def lo(b, name, hi_ap, dst, bias=None):
                    n = order.index(name)
                    dve.wait_ge(hi_done[phase], b * len(HI_ORDER[phase]) + HI_ORDER[phase].index(name) + 1)
                    if bias is None:
                        ins = dve.tensor_tensor(dst, A[n % 2][:, 0:S], hi_ap.bitcast(F32), ALU.subtract)
                    else:
                        ins = dve.scalar_tensor_tensor(out=dst, in0=A[n % 2][:, 0:S], scalar=bias,
                                                       in1=hi_ap.bitcast(F32), op0=ALU.add, op1=ALU.subtract)
                    a.freed(ins, n)

                def lo_qk(b, m):
                    for i, (h_ap, l_ap) in enumerate(((q_hi, q_lo), (k_hi, k_lo))):
                        lo(b, f"{'qk'[i]}{m}", h_ap[:, m % 2, :], l_ap[:, m % 2, :],
                           col_bias[:, i, m:m + 1] if phase == 0 else None)

                def max_head(b, h):
                    if phase == 0:
                        n = s_use(0, h)
                        s_ring[0].wait_full(dve, b, n)
                        dve.tensor_reduce(neg_max[:, h, 0:1], SC[n % 3][0:T, 0:T], AX.X, ALU.max, negate=True)
                        dve.tensor_reduce(neg_max[:, h, 1:NT],
                                          SC[n % 3][0:T, T:5 * T].rearrange("p (t n) -> p t n", t=2),
                                          AX.X, ALU.max, negate=True).then_inc(maxed[0], 1)
                        return
                    for t in range(NT):
                        n = s_use(1, h, t)
                        s_ring[1].wait_full(dve, b, n)
                        dve.tensor_reduce(neg_max[:, h, t:t + 1], SC[n % 3][0:T, 0:S], AX.X, ALU.max, negate=True)\
                           .then_inc(maxed[1], 1)

                def invert(b, h):
                    for t in range(NT):
                        if phase == 1 or t == NT - 1:
                            s_ring[phase].wait_freed(dve, b, s_use(phase, h, t))
                    dve.reciprocal(recip[:, h, :], sums[:, h, :]).then_inc(inverted[phase], 1)

                def copy_turned(b, h):
                    for n in ([NT + h] if phase == 0 else range(NT * h, NT * h + NT)):
                        if n % 2 == 0:
                            wait_slot(dve, phase, b, h, pv_done[phase])
                            t_ring[phase].wait_full(dve, b, n)
                            c, cols = (0, 5 * T) if phase == 0 else ((n - NT * h) * S, S)
                            t_ring[phase].freed(dve.tensor_copy(pT[0:T, h % 4, c:c + cols], TP[0][0:T, 0:cols]), n)

                def lo_out(b, m):
                    dve.wait_ge(o_hi_done[phase], b * HP + m + 1)
                    if phase == 0:
                        ins = dve.scalar_tensor_tensor(out=oT_lo[:, m, :], in0=OB[:, 0:S], scalar=col_bias[:, 2, m:m + 1],
                                                       in1=oT_hi[:, m, :].bitcast(F32), op0=ALU.add, op1=ALU.subtract)
                    else:
                        ins = dve.tensor_tensor(oT_lo[:, m, :], OB[:, 0:S], oT_hi[:, m, :].bitcast(F32), ALU.subtract)
                    ins.then_inc(o_lo_done[phase], 1)

                def norm_stats(src):
                    for t in range(NT):
                        chain.step(dve.bn_stats(bn[:, t, :], src[:, t, :]))
                    chain.wait()
                    plain(dve)
                    for t in range(NT):
                        chain.step(dve.bn_aggr(mean_var[:, t, :], bn[:, t, :]))
                    chain.wait()
                    dve.tensor_scalar(rstd[:, :], mean_var[:, :, 1], EPS, None, ALU.add).then_inc(stats[phase], 1)

                def norm_apply(count, src, dst):
                    dve.wait_ge(rooted[phase], count)
                    for t in range(NT):
                        ins = dve.tensor_scalar(dst[:, t, :], src[:, t, :], mean_var[:, t, 0:1], rstd[:, t:t + 1],
                                                ALU.subtract, ALU.mult)
                        if t < NT - 1 or phase == 0:
                            chain.step(ins)
                    if phase:
                        ins.then_inc(normed[phase], 1)

                def affine(x_ap, gain, shift):
                    chain.wait()
                    for t in range(NT):
                        chain.step(dve.tensor_tensor(x_ap[:, t, :], x_ap[:, t, :], rows_bc[:, gain, :], ALU.mult))
                    chain.wait()
                    for t in range(NT):
                        ins = dve.tensor_tensor(x_ap[:, t, :], x_ap[:, t, :], rows_bc[:, shift, :], ALU.add)
                    ins.then_inc(normed[0], 1)

                if phase:
                    dve.wait_ge(stored[phase - 1], 16 * B + PRIMED)
                if phase == 2:
                    lo_n[0] += 1
                    dve.wait_ge(w_hi_done, lo_n[0])
                    dve.tensor_tensor(router_lo[:, :, :], router[:, :, :], router_hi[:, :, :].bitcast(F32), ALU.subtract)\
                       .then_inc(w_lo_done, 1)
                split_weights(phase)

                if phase < 2:
                    with dve.Fori(0, B) as b:
                        chain.start(b)
                        if phase == 1:
                            dve.wait_ge(entry_in[1], 16 * b + 16)
                            norm_stats(h_in)
                            a.wait_last(dve, b)
                            norm_apply(b + 1, h_in, work)
                            dve.wait_ge(normed[1], b + 1)
                            dve.tensor_tensor(keep[:, :, :], h_in[:, :, :], work[:, :, :], ALU.add).then_inc(kept, 1)
                        lo(b, "x0", xT_hi[:, 0, :], xT_lo[:, 0, :])
                        lo(b, "x1", xT_hi[:, 1, :], xT_lo[:, 1, :])
                        if phase == 0:
                            for c in range(KC):
                                lo(b, f"mq{c}", q_hi[:, c, :], q_lo[:, c, :], mem_bias[:, 0, c:c + 1])
                                lo(b, f"mk{c}", k_hi[:, c, :], k_lo[:, c, :], mem_bias[:, 1, c:c + 1])
                            for t in range(NT):
                                s_ring[0].wait_full(dve, b, t)
                                dve.tensor_reduce(neg_max[:, H, t:t + 1], SC[t][0:T, 0:S], AX.X, ALU.max, negate=True)\
                                   .then_inc(maxed[0], 1)
                        lo_qk(b, 0)
                        for h in range(H + 3):
                            if h % 2 == 0 and h // 2 + 1 < HP:
                                lo_qk(b, h // 2 + 1)
                            if h < H:
                                max_head(b, h)
                            if phase == 0 and h == 0:
                                s_ring[0].wait_all_freed(dve, b, range(NT))
                                p_ring[0].filled(dve.reciprocal(recip[:, H, :], sums[:, H, :]), 0)
                                for n in (0, 2):
                                    t_ring[0].wait_full(dve, b, n)
                                    t_ring[0].freed(dve.tensor_copy(pT[0:T, 2, n * S:n * S + S], TP[0][0:T, 0:S]), n)
                            if 1 <= h <= H:
                                invert(b, h - 1)
                            if phase == 0 and h == 1:
                                p_ring[0].wait_full(dve, b, 0)
                                for t in range(NT):
                                    n = order.index(f"mo{t}")
                                    a.wait_full(dve, b, n)
                                    a.freed(dve.scalar_tensor_tensor(out=keep[:, t, :], in0=A[n % 2][0:T, 0:D],
                                                                     scalar=recip[:, H, t:t + 1], in1=rows_bc[:, MBV, :],
                                                                     op0=ALU.mult, op1=ALU.add), n)
                                a.wait_all_freed(dve, b, [order.index(f"mo{t}") for t in range(NT)])
                                norm_stats(keep)
                            if phase == 0 and h == 3:
                                norm_apply(2 * b + 1, keep, keep)
                                affine(keep, G2W, G2B)
                            if 2 <= h < H + 2:
                                copy_turned(b, h - 2)
                            if h % 2 == 0 and h >= 4:
                                lo_out(b, h // 2 - 2)
                        if phase == 0:
                            lo(b, "c2", k_hi[:, 0, :], k_lo[:, 0, :])
                            lo(b, "c3", k_hi[:, 1, :], k_lo[:, 1, :])
                            for t in range(NT):
                                n = order.index(f"wo{t}")
                                a.wait_full(dve, b, n)
                                a.freed(dve.tensor_tensor(work[:, t, :], A[n % 2][0:T, 0:D], rows_bc[:, BO, :],
                                                          ALU.add), n)
                            a.wait_all_freed(dve, b, [order.index(f"wo{t}") for t in range(NT)])
                            norm_stats(work)
                            norm_apply(2 * b + 2, work, work)
                            affine(work, G1W, G1B)
                            lo(b, "c0", q_hi[:, 0, :], q_lo[:, 0, :])
                            lo(b, "c1", q_hi[:, 1, :], q_lo[:, 1, :])
                            dve.wait_ge(stored[0], 16 * b + PRIMED)
                            for t in range(NT):
                                n = order.index(f"g{t}")
                                a.wait_full(dve, b, n)
                                a.freed(dve.tensor_tensor(tmp[:, t, :], A[n % 2][0:T, 0:D], rows_bc[:, GB, :],
                                                          ALU.add), n)
                            dve.wait_ge(normed[0], 2 * b + 2)
                            chain.step(dve.tensor_tensor(work[:, :, :], work[:, :, :], keep[:, :, :], ALU.subtract))
                            dve.wait_ge(gate_exp, NT * b + NT)
                            chain.link(dve.tensor_scalar(tmp[:, :, :], tmp[:, :, :], 1.0, None, ALU.add))
                            chain.link(dve.reciprocal(tmp[:, :, :], tmp[:, :, :]))
                            chain.link(dve.tensor_tensor(tmp[:, :, :], tmp[:, :, :], work[:, :, :], ALU.mult))
                            dve.tensor_tensor(tmp[:, :, :], tmp[:, :, :], keep[:, :, :], ALU.add).then_inc(gated, 1)
                        else:
                            dve.wait_ge(o_lo_done[1], b * HP + HP + PRIMED)
                            for g in range(HP // 2):
                                dve.tensor_tensor(gelu[:, 2 * g:2 * g + 2, :], oT_hi[:, 2 * g:2 * g + 2, :].bitcast(F32),
                                                  oT_lo[:, 2 * g:2 * g + 2, :].bitcast(F32), ALU.add).then_inc(joined, 1)
                            for g in range(HP // 2):
                                dve.wait_ge(gelu_done, b * (HP // 2) + g + 1)
                                dve.tensor_copy(oT_hi[:, 2 * g:2 * g + 2, :], gelu[:, 2 * g:2 * g + 2, :])\
                                   .then_inc(gelu_hi, 1)
                            dve.wait_ge(stored[1], 16 * b + PRIMED)
                            for t in range(NT):
                                n = order.index(f"wo{t}")
                                a.wait_full(dve, b, n)
                                a.freed(dve.tensor_tensor(tmp[:, t, :], A[n % 2][0:T, 0:D], keep[:, t, :], ALU.add), n)
                        chain.end()
                    continue

                with dve.Fori(0, B) as b:
                    chain.start(b)
                    dve.wait_ge(entry_in[2], 16 * b + 16)
                    norm_stats(h_in)
                    norm_apply(b + 1, h_in, work)
                    lo(b, "x0", xT_hi[:, 0, :], xT_lo[:, 0, :])
                    lo(b, "x1", xT_hi[:, 1, :], xT_lo[:, 1, :])

                    def square(i):
                        a.wait_freed(dve, b, order.index(f"h{i // EC}_{i % EC}"))
                        dve.wait_ge(hidden_lo, b * E * EC + max(i - 1, 0) + PRIMED)
                        r = pT[:, i % 2, 0:S]
                        dve.tensor_tensor(pT[:, 2 + i % 2, 0:S], r, r, ALU.mult).then_inc(squared, 1)

                    def lo_hidden(i):
                        dve.wait_ge(hidden_hi, b * E * EC + i + 1)
                        slot = 2 * (i // EC % 2) + i % EC
                        dve.tensor_tensor(oT_lo[:, slot, :], pT[:, 2 + i % 2, 0:S], oT_hi[:, slot, :].bitcast(F32),
                                          ALU.subtract).then_inc(hidden_lo, 1)

                    def choose():
                        n = order.index("lt")
                        a.wait_full(dve, b, n)
                        a.freed(dve.tensor_copy(logits[:, :, :].rearrange("p t e -> p (t e)"), A[n % 2][0:T, 0:NT * E]), n)
                        a.wait_freed(dve, b, n)
                        plain(dve)
                        for t in range(NT):
                            chain.step(dve.max(top[:, t, :], logits[:, t, :]))
                        chain.wait()
                        plain(dve)
                        for t in range(NT):
                            chain.step(dve.max_index(top_no[:, t, :], top[:, t, :], logits[:, t, :]))
                        dve.tensor_tensor(route[:, :, 0], top[:, :, 1], top[:, :, 0], ALU.subtract)\
                           .then_inc(margin_ready, 1)
                        chain.wait()
                        chain.step(dve.tensor_copy(top_nof[:, :, :], top_no[:, :, 0:2]))
                        dve.wait_ge(margin_exp, b + 1)
                        chain.link(dve.tensor_scalar(route[:, :, 2], route[:, :, 1], 1.0, None, ALU.add))
                        chain.link(dve.reciprocal(route[:, :, 2], route[:, :, 2]))
                        chain.link(dve.tensor_tensor(route[:, :, 3], route[:, :, 1], route[:, :, 2], ALU.mult))
                        for t in range(NT):
                            for i in range(2):
                                chain.step(dve.tensor_scalar(gates[:, i, t, :], expert_no[:, :], top_nof[:, t, i:i + 1],
                                                             route[:, t, 2 + i:3 + i], ALU.is_equal, ALU.mult))
                        chain.wait()
                        chain.link(dve.tensor_tensor(gates[:, 0, :, :], gates[:, 0, :, :], gates[:, 1, :, :], ALU.add))

                    def gather(e):
                        for t in range(NT):
                            n = NT * e + t
                            o_banks.wait_full(dve, b, n)
                            if e:
                                o_banks.wait_freed(dve, b, n - NT)
                            src = h_in if e == 0 else keep
                            dst = tmp if e == E - 1 else keep
                            o_banks.freed(dve.scalar_tensor_tensor(
                                out=dst[:, t, :], in0=(SC + TP + [OB])[n % 6][0:T, 0:D], scalar=gates[:, 0, t, e:e + 1],
                                in1=src[:, t, :], op0=ALU.mult, op1=ALU.add), n)

                    for i in range(E * EC + 1):
                        if i < E * EC:
                            square(i)
                        if i >= 1:
                            lo_hidden(i - 1)
                        if i == EC:
                            choose()
                        if i % EC == 0 and i // EC >= 2:
                            gather(i // EC - 2)
                    dve.wait_ge(stored[2], 16 * b + PRIMED)
                    gather(E - 1)
                    chain.end()


def kernel(**inputs):
    import numpy as _np
    import concourse.bacc as _bacc
    from concourse import mybir as _mybir
    from concourse.bass_utils import run_bass_kernel_spmd as _run

    nc = _bacc.Bacc("TRN2", target_bir_lowering=False, num_devices=1)
    arrays, args = {}, {}
    for name, value in inputs.items():
        a = _np.ascontiguousarray(value)
        arrays[f"in_{name}_dram"] = a
        args[name] = nc.dram_tensor(f"in_{name}_dram", a.shape, _mybir.dt.from_np(a.dtype), kind="ExternalInput").ap()
    out = nc.dram_tensor("out_0_dram", (B, S, D), F32, kind="ExternalOutput").ap()
    build(nc, out, **args)
    r = _run(nc, [arrays], core_ids=[0])
    return r.results[0]["out_0_dram"]
```

```python
from contextlib import ExitStack

import concourse.bass as bass
from concourse import mybir
from concourse.alu_op_type import AluOpType as ALU

F32 = mybir.dt.float32
F32R = mybir.dt.float32r
BF16 = mybir.dt.bfloat16
U32 = mybir.dt.uint32
ACT = mybir.ActivationFunctionType
AX = mybir.AxisListType

B, S0, D = 8, 256, 256
PM = 32
S = S0 + PM
T = 96
NT = S // T
KC = D // 128
H, HD = 16, 64
HP = H // 2
WINDOW = 64
E, DE = 8, 256
EC = DE // 128
INNER = H * HD
EPS = 1e-5
MASKED = -3.0e38
PIECE = 1024
STAGES = 8
WCOLS = 10 * PIECE + 2 * D
WIN = [(0, 0, 1), (T, 0, 2), (3 * T, 1, 2)]
WINT = [(0, 0, 2), (2 * T, 1, 2), (4 * T, 2, 1)]
PRING = 3
LATE = ((1, 1), (0, 1))
MEMORY_OUT_AT = 3
NORM_AT = 10
EXPERT_NORM_AT = 4
LAGS = [3, 2]
PRIMED = 1
CONST_STEPS = 15
CHAIN_STEPS = [19, 8, 25]
SHARES_FROM = 14


class Ring:

    def __init__(self, sem, name, size, order, early=()):
        self.order = list(order) if not isinstance(order, int) else list(range(order))
        self.size, self.early = size, set(early)
        self.full = [sem(f"{name}{i}_full") for i in range(size)]
        self.free = [sem(f"{name}{i}_free") for i in range(size)]
        self.per = [(len(self.order) + size - 1 - i) // size for i in range(size)]

    def slot(self, use):
        return self.order.index(use) % self.size

    def fills_before(self, b, use, more=0):
        n = self.order.index(use)
        per = self.per[n % self.size]
        steps = bool(self.early) - (use in self.early)
        return b * per + (steps * per + n // self.size + PRIMED + more)

    def wait_free(self, eng, b, use):
        eng.wait_ge(self.free[self.slot(use)], self.fills_before(b, use))

    def wait_full(self, eng, b, use):
        eng.wait_ge(self.full[self.slot(use)], self.fills_before(b, use, 1))

    def wait_freed(self, eng, b, use):
        eng.wait_ge(self.free[self.slot(use)], self.fills_before(b, use, 1))

    def wait_all_freed(self, eng, b, uses):
        in_time = sorted(uses, key=lambda use: (use not in self.early, self.order.index(use)))
        for use in {self.slot(use): use for use in in_time}.values():
            self.wait_freed(eng, b, use)

    def filled(self, ins, use):
        ins.then_inc(self.full[self.slot(use)], 1)

    def freed(self, ins, use):
        ins.then_inc(self.free[self.slot(use)], 1)


class Chain:

    def __init__(self, sem, eng, per):
        self.sem, self.eng, self.per, self.n = sem, eng, per, 0

    def start(self, b, n=0):
        self.b, self.n = b, n

    def step(self, ins):
        ins.then_inc(self.sem, 1)
        self.n += 1

    def wait(self):
        self.eng.wait_ge(self.sem, self.b * self.per + self.n)

    def link(self, ins):
        self.step(ins)
        self.wait()

    def end(self):
        assert self.n == self.per, (self.n, self.per)


def weight_pieces(w):
    def rows(x, k, n, cols):
        return x[128 * k:128 * (k + n), :].rearrange("(k p) n -> p k n", p=128), n, cols

    def plain(name):
        return [rows(w[name], k, 1, INNER) for k in range(KC)]

    qk = float(HD) ** -0.5
    tok = [([d], [(PIECE, 1.0)]) for d in plain("L0_tok_Wv")]
    tok += [([rows(w["L0_tok_mWq"], 0, 2, D), rows(w["L0_tok_mWk"], 0, 2, D)],
             [(2 * D, float(D) ** -0.5), (2 * D, 0.1)])]
    tok += [([d], [(PIECE, s)]) for name, s in (("L0_tok_Wq", qk), ("L0_tok_Wk", 1.0)) for d in plain(name)]
    tok += [([rows(w["L0_tok_mWv"], 0, 2, D), rows(w["L0_tok_gate_W"], 0, 2, D)], [(2 * D, 0.1), (2 * D, 1.0)])]
    tok += [([rows(w["L0_tok_Wo"], 4 * i, 4, D)], [(PIECE, 1.0)]) for i in range(2)]
    tok += [([rows(w["L0_tok_gate_W"], 2, 2, D)], [(2 * D, 1.0)])]
    attn = [([d], [(PIECE, s)]) for name, s in (("L0_attn_Wq", 1.0), ("L0_attn_Wk", qk), ("L0_attn_Wv", 1.0))
            for d in plain(name)]
    attn += [([rows(w["L0_attn_Wpost"], 4 * i, 4, D)], [(PIECE, 1.0)]) for i in range(2)]
    ffn = []
    for name in ("L0_ffn_w1_all", "L0_ffn_w2_all"):
        for e in range(0, E, 2):
            src = w[name][e:e + 2].rearrange("e (k p) n -> p (e k) n", p=128)
            ffn.append(([(src, 2 * KC, DE)], [(PIECE, 1.0)]))
    return [tok, attn, ffn]


WQ = [3 * PIECE, 0]
WK = [5 * PIECE, 2 * PIECE]
WV = [0, 4 * PIECE]
WMQ, WMK = 2 * PIECE, 2 * PIECE + KC * D
WMV = 7 * PIECE
WO = [8 * PIECE, 6 * PIECE]
WG = [7 * PIECE + KC * D, 10 * PIECE]
W1, W2 = 0, E * KC * DE
EARLY_PIECES = 6


def build(nc, out, **w):
    ctx = ExitStack()
    with ctx:
        def sb(name, shape, dt=F32):
            return ctx.enter_context(nc.sbuf_tensor(name, shape, dt))

        def sem(name):
            return ctx.enter_context(nc.semaphore(name))

        x = w["x"]
        h_tok = nc.dram_tensor("h_tok", (B, S, D), F32, kind="Internal").ap()
        h_attn = nc.dram_tensor("h_attn", (B, S, D), F32, kind="Internal").ap()
        pieces = weight_pieces(w)
        flat = [p for phase in pieces for p in phase]
        first_piece = [0, len(pieces[0]), len(pieces[0]) + len(pieces[1]), len(flat)]

        stage = sb("stage", [128, STAGES, PIECE])
        with nc.sbuf_tensor("w_hi", [128, WCOLS], F32R) as w_hi:
            pass
        sb("later_weights", [128, 8 * PIECE], F32R)
        o_raw = sb("o_raw", [128, HP, S])
        sb("behind_o_raw", [128, WCOLS - 8 * PIECE - HP * S])
        w_lo = sb("w_lo", [128, WCOLS], F32R)
        router = sb("router", [128, KC, E])
        router_hi = sb("router_hi", [128, KC, E], F32R)
        router_lo = sb("router_lo", [128, KC, E], F32R)
        ident = sb("ident", [T, T])
        ident_bf = sb("ident_bf", [T, T], BF16)
        mask_bf = sb("mask_bf", [T, 5 * T], BF16)
        col_bias = sb("col_bias", [128, 3, HP])
        mem_bias = sb("mem_bias", [128, 2, KC])
        rows_bc = sb("rows_bc", [T, 7, D])
        BO, MBV, G1W, G1B, G2W, G2B, GB = range(7)
        expert_no = sb("expert_no", [T, E])
        expert_no_i = sb("expert_no_i", [T, E], mybir.dt.int32)
        neg_half = sb("neg_half", [T, NT])
        xT_hi = sb("xT_hi", [128, KC, S], F32R)
        xT_lo = sb("xT_lo", [128, KC, S], F32R)
        q_hi = sb("q_hi", [128, 2, S], F32R)
        q_lo = sb("q_lo", [128, 2, S], F32R)
        k_hi = sb("k_hi", [128, 2, S], F32R)
        k_lo = sb("k_lo", [128, 2, S], F32R)
        oT_hi = sb("oT_hi", [128, HP, S], F32R)
        oT_lo = sb("oT_lo", [128, HP, S], F32R)
        h_in = sb("h_in", [T, NT, D])
        keep = sb("keep", [T, NT, D])
        work = sb("work", [T, NT, D])
        tmp = sb("tmp", [T, NT, D])
        mv = sb("mv", [T, NT, D])
        v = sb("v", [T, NT, INNER])
        probs = sb("probs", [T, PRING, NT * S])
        pT = sb("pT", [128, 4, NT * S])
        neg_max = sb("neg_max", [T, H + 1, NT])
        sums = sb("sums", [T, H + 1, NT])
        recip = sb("recip", [T, H + 1, NT])
        bn = sb("bn", [T, NT, 6])
        mean_var = sb("mean_var", [T, NT, 2])
        rstd = sb("rstd", [T, NT])
        mv_flat = mv[:, :, :].rearrange("p t d -> p (t d)")

        def small(at, *shape):
            size = 1
            for s in shape:
                size *= s
            names = "abc"[:len(shape)]
            return mv_flat[:, at:at + size].rearrange(
                f"p ({' '.join(names)}) -> p {' '.join(names)}", **dict(zip(names, shape)))

        logits_T = mv_flat[0:E, 0:S]
        logits = small(S, NT, E)
        top = small(S + 24, NT, 8)
        top_no = small(S + 48, NT, 8).bitcast(U32)
        top_nof = small(S + 72, NT, 2)
        route = small(S + 80, NT, 4)
        gates = small(S + 96, 2, NT, E)

        def bank(name, shape=(128, 512)):
            return ctx.enter_context(nc.psum_tensor(name, list(shape), F32))

        A = [bank("bank_a0"), bank("bank_a1")]
        SC = [bank(f"bank_s{i}") for i in range(3)]
        TP = [bank("bank_t0"), bank("bank_t1")]
        OB = bank("bank_o")

        staged = [sem(f"staged{i}") for i in range(STAGES)]
        w_hi_done, w_lo_done = sem("w_hi_done"), sem("w_lo_done")
        const_in, const_made, const_ready = sem("const_in"), sem("const_made"), sem("const_ready")
        CONSTS = 16 * (12 + KC)
        entry_in = [sem(f"entry_in{i}") for i in range(3)]
        stored = [sem(f"stored{i}") for i in range(3)]
        gated = sem("gated")
        normed = [sem(f"normed{i}") for i in range(3)]
        stats = [sem(f"stats{i}") for i in range(3)]
        rooted = [sem(f"rooted{i}") for i in range(3)]
        chains = [sem(f"vector_chain{i}") for i in range(3)]

        AHEAD = [{13: ("x0", "x1"), 14: ("v0", "v2"), 15: ("v4", "mq0", "mk0"), 16: ("mq1", "mk1"),
                  19: ("mv0", "mv1", "mv2"), "a": ("v1",), "b": ("v3", "v5"), "c": ("q0", "k0"), "d": ("q1",),
                  "e": ("k1",)},
                 {13: ("x0", "x1"), 14: ("v0", "v2"), 15: ("v4", "q0", "k0"), 16: ("q1",),
                  "a": ("v1", "v3", "v5"), "b": ("k1",)}]
        early = [[name for names in ahead.values() for name in names] for ahead in AHEAD]
        heads_a = [f"{c}{m}" for m in range(2, HP) for c in "qk"]
        wo_a = [f"wo{t}" for t in range(NT)]
        A_ORDER = [heads_a[:MEMORY_OUT_AT] + ["mo0", "mo1", "mo2"] + heads_a[MEMORY_OUT_AT:] + early[0][:-6] + wo_a + ["v3", "v5", "c2", "c3", "q0",
                   "k0", "c0", "c1", "q1", "g0", "g1", "g2", "k1"],
                   heads_a + early[1] + wo_a,
                   ["x0", "x1", "lg", "h0_0", "h0_1", "lt"] + [f"h{e}_{c}" for e in range(1, E) for c in range(EC)]]
        qk = [f"{c}{m}" for m in range(HP) for c in "qk"]
        HI_ORDER = [["x0", "x1", "mq0", "mk0", "mq1", "mk1"] + qk, ["x0", "x1"] + qk, ["x0", "x1"]]
        CAT_ORDER = ["c2", "c3", "c0", "c1"]
        a_ring = [Ring(sem, f"a{i}_", 2, A_ORDER[i], (early + [()])[i]) for i in range(3)]
        hi_done = [sem(f"hi_done{i}") for i in range(3)]
        cat_hi = sem("cat_hi")
        UNITS = [NT + H, NT * H]
        s_ring = [Ring(sem, f"s{i}_", 3, UNITS[i]) for i in range(2)]
        t_ring = [Ring(sem, f"t{i}_", 2, UNITS[i]) for i in range(2)]
        p_ring = [Ring(sem, f"p{i}_", PRING, H + 1 - i) for i in range(2)]
        maxed = [sem(f"maxed{i}") for i in range(2)]
        inverted = [sem(f"inverted{i}") for i in range(2)]
        pv_done = [sem(f"pv_done{i}") for i in range(2)]
        o_hi_done = sem("o_hi_done")
        o_lo_done = [sem(f"o_lo_done{i}") for i in range(2)]
        gate_tanh = sem("gate_tanh")
        differed = sem("differed")
        kept = sem("kept")
        gelu_done, gelu_hi, gelu_lo = sem("gelu_done"), sem("gelu_hi"), sem("gelu_lo")
        o_banks = Ring(sem, "expert_out", 6, NT * E)
        squared, hidden_hi, hidden_lo = sem("squared"), sem("hidden_hi"), sem("hidden_lo")
        margin_ready, margin_exp = sem("margin_ready"), sem("margin_exp")

        passed = {nc.vector: sem("vector_passed"), nc.gpsimd: sem("gpsimd_passed"), nc.tensor: sem("tensor_passed"),
                  nc.sync: sem("sync_passed")}

        block = ctx.enter_context(nc.Block())

        def plain(eng):
            eng.sem_inc(passed[eng], 1)

        def parts_of(phase):
            for i, (_, parts) in enumerate(pieces[phase]):
                p, at = first_piece[phase] + i, 0
                for cols, scale in parts:
                    yield (p, stage[:, p % STAGES, at:at + cols], slice(PIECE * i + at, PIECE * i + at + cols), scale,
                           at + cols == sum(c for c, _ in parts))
                    at += cols

        PARTS = [sum(len(parts) for _, parts in phase) for phase in pieces]

        def s_use(ph, h, t=0):
            return h + NT if ph == 0 else NT * h + t

        def p_use(ph, h):
            return h + 1 - ph

        def row_of(ph, h, t):
            return (WIN[t][0], WIN[t][2] * T) if ph == 0 else (t * S, S)

        FIRST = 0
        AHEAD_WEIGHTS = [{"v0": 2, "mq0": 3, "mv0": 8}, {"v0": EARLY_PIECES}]
        SPLIT_AT = 13
        MEMORY_AT = 18

        def qk_at(h):
            return [] if not 1 <= h <= H - 4 else [("k", h // 2 + 1) if h % 2 == 0 else ("q", (h + 3) // 2)]

        def turned(ph, h, tiles):
            return [NT * h + kt for kt in tiles] if ph else [NT + h] if 0 in tiles else []

        @block.sync
        def _(sp):
            def load_pieces(phase):
                for p in range(first_piece[phase], first_piece[phase + 1]):
                    if p >= STAGES:
                        sp.wait_ge(w_lo_done, p - STAGES + 1)
                    at = 0
                    for src, n, cols in flat[p][0]:
                        sp.dma_start(stage[:, p % STAGES, at:at + n * cols].rearrange("p (k n) -> p k n", k=n), src)\
                          .then_inc(staged[p % STAGES], 16)
                        at += n * cols

            def load_x(b):
                sp.dma_start(h_in[PM:T, 0, :], x[b, 0:T - PM, :]).then_inc(entry_in[0], 16)
                sp.dma_start(h_in[:, 1:NT, :], x[b, T - PM:S0, :].rearrange("(t p) d -> p t d", p=T))\
                  .then_inc(entry_in[0], 16)

            def store(phase, dst, b):
                if phase == 0:
                    sp.wait_ge(gated, b + (1 + PRIMED))
                if phase == 1:
                    a_ring[1].wait_all_freed(sp, b, wo_a)
                if phase == 2:
                    o_banks.wait_all_freed(sp, b, [NT * (E - 1) + t for t in range(NT)])
                sp.dma_start(dst[b].rearrange("(t p) d -> p t d", p=T), tmp[:, :, :]).then_inc(stored[phase], 16)

            def load_h(phase, src, b):
                sp.dma_start(h_in[:, :, :], src[b].rearrange("(t p) d -> p t d", p=T)).then_inc(entry_in[phase], 16)

            sp.dma_start(h_in[0:PM, 0, :], w["L0_tok_persistent_memory"]).then_inc(entry_in[0], 16)
            load_x(0)
            for i, name in enumerate(("bq", "bk", "bv")):
                sp.dma_start(col_bias[:, i, :], w["L0_tok_" + name].rearrange("(m p) -> p m", p=128),
                             allow_slow_non_contiguous=True).then_inc(const_in, 16)
            for i, name in enumerate(("mbq", "mbk")):
                sp.dma_start(mem_bias[:, i, :], w["L0_tok_" + name].rearrange("(m p) -> p m", p=128),
                             allow_slow_non_contiguous=True).then_inc(const_in, 16)
            for i, name in enumerate(("bo", "mbv", "g1_w", "g1_b", "g2_w", "g2_b", "gate_b")):
                sp.dma_start(rows_bc[:, i, :], w["L0_tok_" + name].partition_broadcast(T)).then_inc(const_in, 16)
            for k in range(KC):
                sp.dma_start(router[:, k, :], w["L0_ffn_router_w"][:, 128 * k:128 * k + 128].rearrange("e p -> p e"),
                             allow_slow_non_contiguous=True).then_inc(const_in, 16)
            load_pieces(0)
            load_pieces(1)
            with sp.Fori(0, B - 1) as b:
                for name in ("x0", "x1"):
                    a_ring[0].wait_freed(sp, b, name)
                    plain(sp)
                load_x(b + 1)
                store(0, h_tok, b)
            a_ring[0].wait_all_freed(sp, B - 1, ("x0", "x1"))
            sp.wait_ge(stored[0], 16 + PRIMED)
            load_h(1, h_tok, 0)
            store(0, h_tok, B - 1)
            sp.wait_ge(stored[0], 16 * B + PRIMED)
            load_pieces(2)
            with sp.Fori(0, B - 1) as b:
                sp.wait_ge(kept, b + 1)
                load_h(1, h_tok, b + 1)
                store(1, h_attn, b)
            sp.wait_ge(kept, B)
            sp.wait_ge(stored[1], 16 + PRIMED)
            load_h(2, h_attn, 0)
            store(1, h_attn, B - 1)
            sp.wait_ge(stored[1], 16 * B + PRIMED)
            with sp.Fori(0, B - 1) as b:
                o_banks.wait_all_freed(sp, b, range(NT))
                load_h(2, h_attn, b + 1)
                store(2, out, b)
            store(2, out, B - 1)
            sp.wait_ge(stored[2], 16 * B + PRIMED)

        @block.gpsimd
        def _(pool):
            n = 0

            def made(ins):
                nonlocal n
                n += 1
                ins.then_inc(const_made, 1)
                pool.wait_ge(const_made, n)

            made(pool.memset(ident[:, :], 0.0))
            made(pool.affine_select(out=ident[:, :], in_=ident[:, :], compare_op=ALU.not_equal, fill=1.0, base=0,
                                    pattern=[[-1, T]], channel_multiplier=1))
            made(pool.tensor_copy(ident_bf[:, :], ident[:, :]))
            made(pool.memset(tmp[:, :, :], 0.0))
            for t in range(NT):
                c, n_kt = WIN[t][0], WIN[t][2]
                off = (t - WIN[t][1]) * T
                m = tmp[:, :, :].rearrange("p t d -> p (t d)")[:, c:c + n_kt * T]
                made(pool.affine_select(out=m, in_=m, compare_op=ALU.is_ge, fill=MASKED, base=off,
                                        pattern=[[-1, n_kt * T]], channel_multiplier=1))
                made(pool.affine_select(out=m, in_=m, compare_op=ALU.is_ge, fill=MASKED, base=WINDOW - off,
                                        pattern=[[1, n_kt * T]], channel_multiplier=-1))
            made(pool.tensor_copy(mask_bf[:, :], tmp[:, :, :].rearrange("p t d -> p (t d)")[:, 0:5 * T]))
            made(pool.iota(expert_no_i[:, :], pattern=[[1, E]], base=0, channel_multiplier=0))
            made(pool.tensor_copy(expert_no[:, :], expert_no_i[:, :]))
            made(pool.memset(neg_half[:, :], -0.5))
            pool.wait_ge(const_in, CONSTS)
            made(pool.tensor_scalar(col_bias[:, 0, :], col_bias[:, 0, :], float(HD) ** -0.5, 1.0, ALU.mult, ALU.mult))
            pool.tensor_scalar(mem_bias[:, 0, :], mem_bias[:, 0, :], float(D) ** -0.5, 1.0, ALU.mult, ALU.mult)\
                .then_inc(const_ready, 1)

            def root(phase, count):
                pool.wait_ge(stats[phase], count)
                pool.tensor_tensor(rstd[:, :], rstd[:, :], neg_half[:, :], ALU.pow).then_inc(rooted[phase], 1)

            def scale_head(ph, b, h):
                pool.wait_ge(inverted[ph], b * H + h + 1)
                plain(pool)
                for t in range(NT):
                    c, cols = row_of(ph, h, t)
                    row = probs[:, p_use(ph, h) % PRING, c:c + cols]
                    ins = pool.tensor_scalar(row, row, recip[:, h, t:t + 1], 1.0, ALU.mult, ALU.mult)
                p_ring[ph].filled(ins, p_use(ph, h))

            def entry(ph, b, n):
                for h in range(1 - ph, H):
                    scale_head(ph, b, h)
                    if ph == 0 and h == MEMORY_OUT_AT:
                        root(0, 2 * b + 1)
                    if h == NORM_AT:
                        if n is None:
                            root(ph + 1, 1)
                        elif ph == 1:
                            root(1, n + 1)
                if ph == 0:
                    root(0, 2 * b + 2)
                    a_ring[0].wait_full(pool, b, "c1")
                    pool.tensor_tensor(work[:, :, :], work[:, :, :], keep[:, :, :], ALU.subtract).then_inc(differed, 1)
                    if n is not None:
                        scale_head(0, n, 0)
                else:
                    for g in range(HP // 2 - 1):
                        pool.wait_ge(gelu_hi, b * (HP // 2) + (g + 1))
                        pool.tensor_tensor(oT_lo[:, 2 * g:2 * g + 2, :], o_raw[:, 2 * g:2 * g + 2, :],
                                           oT_hi[:, 2 * g:2 * g + 2, :].bitcast(F32), ALU.subtract).then_inc(gelu_lo, 1)

            def lo_hidden(b, e):
                for i in range(EC * e, EC * e + EC):
                    pool.wait_ge(hidden_hi, b * (E * EC) + (i + 1))
                    slot = i % (4 * EC)
                    pool.tensor_tensor(oT_lo[:, slot, :], pT[:, i % 4, 0:S], oT_hi[:, slot, :].bitcast(F32),
                                       ALU.subtract).then_inc(hidden_lo, 1)

            scale_head(0, FIRST, 0)
            for phase in range(2):
                with pool.Fori(0, B - 1) as b:
                    entry(phase, b, b + 1)
                entry(phase, B - 1, None)

            def experts(b, n):
                for e in range(2, E):
                    lo_hidden(b, e)
                    if e == EXPERT_NORM_AT and n is not None:
                        root(2, n + 1)
                if n is not None:
                    lo_hidden(n, 0)
                    lo_hidden(n, 1)

            lo_hidden(0, 0)
            lo_hidden(0, 1)
            with pool.Fori(0, B - 1) as b:
                experts(b, b + 1)
            experts(B - 1, None)

        @block.tensor
        def _(pe):
            def product(dst, ops, start=True, stop=True):
                n = 3 * len(ops)
                i = 0
                for (l_hi, l_lo), (r_hi, r_lo) in ops:
                    for l, r in ((l_hi, r_hi), (l_hi, r_lo), (l_lo, r_hi)):
                        ins = pe.matmul(dst, l, r, start=start and i == 0, stop=stop and i == n - 1,
                                        skip_group_check=not start)
                        i += 1
                return ins

            def wcols(at, n):
                return w_hi[:, at:at + n], w_lo[:, at:at + n]

            def xcols(k, t=None):
                c = slice(0, S) if t is None else slice(t * T, t * T + T)
                return xT_hi[:, k, c], xT_lo[:, k, c]

            rings = a_ring + s_ring + t_ring + p_ring + [o_banks]
            for primed in ([s for ring in rings for s in ring.full + ring.free] + o_lo_done + stored + [gated]):
                pe.sem_inc(primed, PRIMED)

            for phase in range(3):
                a, order = a_ring[phase], A_ORDER[phase]
                LAG = LAGS[phase] if phase < 2 else 0

                def pass_over(name):
                    early_use = name in a.early
                    a.wait_free(pe, step[0] + 1 if early_use else step[0], name)
                    pe.sem_inc(a.full[a.slot(name)], 1)
                    pe.sem_inc(a.free[a.slot(name)], 1)

                def fill(b, name, emit):
                    while order[cursor[0] % len(order)] != name:
                        pass_over(order[cursor[0] % len(order)])
                        cursor[0] += 1
                    cursor[0] += 1
                    a.wait_free(pe, b, name)
                    a.filled(emit(A[a.slot(name)]), name)

                def ready(b, *names):
                    a.wait_all_freed(pe, b, names)

                def turn_in(b, name, src, k):
                    def emit(bank):
                        for t in range(NT):
                            ins = pe.transpose(bank[:, t * T:t * T + T], src[:, t, 128 * k:128 * k + 128], ident[:, :])
                        return ins
                    fill(b, name, emit)

                def chunk(b, name, at, width, m):
                    fill(b, name, lambda bank: product(bank[:, 0:S], [
                        (wcols(at + k * width + 128 * m, 128), xcols(k)) for k in range(KC)]))

                def project(b, c, m):
                    chunk(b, f"{c}{m}", {"q": WQ, "k": WK}[c][phase], INNER, m)

                def natural(b, name, at, width, cols, t):
                    fill(b, name, lambda bank: product(bank[0:T, 0:cols.stop - cols.start], [
                        (xcols(k, t), wcols(at + k * width + cols.start, cols.stop - cols.start)) for k in range(KC)]))

                def ahead(b, name):
                    kind, i = name[:-1], int(name[-1])
                    if name in AHEAD_WEIGHTS[phase] and b is FIRST:
                        pe.wait_ge(w_lo_done, first_piece[phase] + AHEAD_WEIGHTS[phase][name])
                    if name == "x0":
                        if phase == 0:
                            pe.wait_ge(entry_in[0], b * 32 + 48)
                        else:
                            pe.wait_ge(normed[phase], b + 1)
                    if name == "v0":
                        ready(b, "x0", "x1")
                    if kind == "x":
                        turn_in(b, name, h_in if phase == 0 else mv, i)
                    elif kind == "v":
                        natural(b, name, WV[phase], INNER, slice(512 * (i % 2), 512 * (i % 2) + 512), i // 2)
                    elif kind == "mv":
                        natural(b, name, WMV, D, slice(0, D), i)
                    elif kind in ("mq", "mk"):
                        chunk(b, name, WMQ if kind == "mq" else WMK, D, i)
                    else:
                        project(b, kind, i)

                def scores(b, h):
                    s, half, m = s_ring[phase], 64 * (h % 2), h // 2
                    rows = slice(half, half + HD)
                    ready(b, f"q{m}", f"k{m}")
                    if phase == 0:
                        n = s_use(0, h)
                        s.wait_free(pe, b, n)
                        bank = SC[n % 3]
                        pe.matmul(bank[0:T, 0:5 * T], ident_bf[:, :], mask_bf[:, :], start=True, stop=True)
                        for t in range(NT):
                            c, kt, n_kt = WIN[t]
                            keys, mine = slice(kt * T, (kt + n_kt) * T), slice(t * T, t * T + T)
                            ins = product(bank[0:T, c:c + n_kt * T], [
                                ((q_hi[rows, m % 2, mine], q_lo[rows, m % 2, mine]),
                                 (k_hi[rows, m % 2, keys], k_lo[rows, m % 2, keys]))], start=False)
                        s.filled(ins, n)
                        return
                    for t in range(NT):
                        n, mine = s_use(1, h, t), slice(t * T, t * T + T)
                        s.wait_free(pe, b, n)
                        s.filled(product(SC[n % 3][0:T, 0:S], [
                            ((q_hi[rows, m % 2, mine], q_lo[rows, m % 2, mine]),
                             (k_hi[rows, m % 2, :], k_lo[rows, m % 2, :]))]), n)

                def turn_square(b, p_n, t_first, tiles=range(NT)):
                    if 0 in tiles:
                        p_ring[phase].wait_full(pe, b, p_n)
                    for kt in tiles:
                        n = t_first + kt
                        t_ring[phase].wait_free(pe, b, n)
                        for t in range(NT):
                            ins = pe.transpose(TP[n % 2][0:T, t * T:t * T + T],
                                               probs[:, p_n % PRING, t * S + kt * T:t * S + kt * T + T], ident[:, :])
                        t_ring[phase].filled(ins, n)

                def turn_probs(b, h, tiles):
                    if phase == 1:
                        turn_square(b, p_use(1, h), NT * h, tiles)
                        return
                    if 0 not in tiles:
                        return
                    n = NT + h
                    p_ring[0].wait_full(pe, b, p_use(0, h))
                    t_ring[0].wait_free(pe, b, n)
                    for kt in range(NT):
                        c, qt, n_qt = WINT[kt]
                        for i in range(n_qt):
                            src = WIN[qt + i][0] + (kt - WIN[qt + i][1]) * T
                            ins = pe.transpose(TP[n % 2][0:T, c + i * T:c + i * T + T],
                                               probs[:, p_use(0, h) % PRING, src:src + T], ident[:, :])
                    t_ring[0].filled(ins, n)

                def attend(b, m):
                    t_ring[phase].wait_all_freed(pe, b, [NT + 2 * m, NT + 2 * m + 1] if phase == 0
                                                 else range(2 * m * NT, (2 * m + 2) * NT))
                    pe.wait_ge(o_lo_done[phase], b * HP + (m + PRIMED))
                    for kt in range(NT):
                        c, qt, n_qt = WINT[kt] if phase == 0 else (kt * S, 0, NT)
                        for h in (2 * m, 2 * m + 1):
                            half = 64 * (h % 2)
                            ins = pe.matmul(OB[half:half + HD, qt * T:(qt + n_qt) * T],
                                            v[:, kt, h * HD:h * HD + HD], pT[0:T, h % 4, c:c + n_qt * T],
                                            start=kt == 0, stop=kt == NT - 1, skip_group_check=True)
                    ins.then_inc(pv_done[phase], 1)

                def project_out(b):
                    for t in range(NT):
                        mine = slice(t * T, t * T + T)
                        fill(b, f"wo{t}", lambda bank: product(bank[0:T, 0:D], [
                            ((oT_hi[:, m, mine], oT_lo[:, m, mine]), wcols(WO[phase] + m * D, D)) for m in range(HP)]))

                def memory_scores(b):
                    ready(b, "mq0", "mk0", "mq1", "mk1")
                    for t in range(NT):
                        mine = slice(t * T, t * T + T)
                        s_ring[0].wait_free(pe, b, t)
                        s_ring[0].filled(product(SC[t][0:T, 0:S], [
                            ((q_hi[:, c, mine], q_lo[:, c, mine]), (k_hi[:, c, :], k_lo[:, c, :]))
                            for c in range(KC)]), t)

                def memory_attend(b):
                    t_ring[0].wait_all_freed(pe, b, range(NT))
                    ready(b, "mv2")
                    for t in range(NT):
                        def emit(bank):
                            for kt in range(NT):
                                ins = pe.matmul(bank[0:T, 0:D], pT[0:T, 2, kt * S + t * T:kt * S + t * T + T],
                                                mv[:, kt, :], start=kt == 0, stop=kt == NT - 1)
                            return ins
                        fill(b, f"mo{t}", emit)

                def entry(b, n):
                    def between(at):
                        if n is not None:
                            for name in AHEAD[phase].get(at, ()):
                                ahead(n, name)

                    step[0] = b
                    for h in range(1, H + LAG + 1):
                        if LAG <= h < H + LAG:
                            turn_probs(b, h - LAG, (0, 1))
                        if 1 <= h < H:
                            scores(b, h)
                        if LAG <= h < H + LAG:
                            turn_probs(b, h - LAG, (2,))
                        for c, m in qk_at(h):
                            project(b, c, m)
                        if phase == 0 and h == 1:
                            turn_square(b, 0, 0, (2,))
                        if phase == 0 and h == MEMORY_OUT_AT:
                            memory_attend(b)
                        between(h)
                        if phase == 0 and h == MEMORY_AT and n is not None:
                            memory_scores(n)
                        if (h - LAG) % 2 == 0 and h > LAG:
                            attend(b, (h - LAG) // 2 - 1)
                    between("a")
                    if phase == 0:
                        pe.wait_ge(o_lo_done[0], b * HP + (HP + PRIMED))
                        project_out(b)
                        between("b")
                        pe.wait_ge(normed[0], 2 * b + 1)
                        turn_in(b, "c2", keep, 0)
                        turn_in(b, "c3", keep, 1)
                        between("c")
                        pe.wait_ge(normed[0], 2 * b + 2)
                        turn_in(b, "c0", work, 0)
                        turn_in(b, "c1", work, 1)
                        between("d")
                        if n is not None:
                            scores(n, 0)
                        ready(b, "c0", "c1")
                        for t in range(NT):
                            mine = slice(t * T, t * T + T)
                            fill(b, f"g{t}", lambda bank: product(bank[0:T, 0:D], [
                                ((oT_hi[:, c, mine], oT_lo[:, c, mine]), wcols(WG[c // KC] + c % KC * D, D))
                                for c in range(2 * KC)]))
                        between("e")
                        if n is not None:
                            turn_square(n, 0, 0, (0, 1))
                    else:
                        if n is not None:
                            scores(n, 0)
                        between("b")
                        pe.wait_ge(gelu_lo, b * (HP // 2) + HP // 2)
                        project_out(b)

                if phase == 0:
                    pe.wait_ge(const_made, CONST_STEPS)
                    pe.wait_ge(const_ready, 1)
                else:
                    a_ring[phase - 1].wait_all_freed(pe, B - 1, ("g1", "g2") if phase == 1 else ("wo1", "wo2"))
                step, cursor = [-1], [0]

                if phase < 2:
                    for name in early[phase]:
                        if name == "mv0":
                            memory_scores(FIRST)
                        if name == "k1":
                            scores(FIRST, 0)
                        ahead(FIRST, name)
                    if phase == 0:
                        turn_square(FIRST, 0, 0, (0, 1))
                    while cursor[0] < len(order):
                        pass_over(order[cursor[0]])
                        cursor[0] += 1
                    pe.wait_ge(w_lo_done, first_piece[phase + 1])
                    with pe.Fori(0, B - 1) as b:
                        entry(b, b + 1)
                    entry(B - 1, None)
                    continue

                def hidden(b, e):
                    for c in range(EC):
                        chunk(b, f"h{e}_{c}", W1 + e * KC * DE, DE, c)

                def expert_out(b, e):
                    pe.wait_ge(hidden_lo, b * (E * EC) + (e + 1) * EC)
                    for t in range(NT):
                        n, mine = NT * e + t, slice(t * T, t * T + T)
                        o_banks.wait_free(pe, b, n)
                        o_banks.filled(product((SC + TP + [OB])[n % 6][0:T, 0:D], [
                            ((oT_hi[:, EC * (e % 4) + c, mine], oT_lo[:, EC * (e % 4) + c, mine]),
                             wcols(W2 + (e * EC + c) * D, D)) for c in range(EC)]), n)

                def inputs(b):
                    pe.wait_ge(normed[2], b + 1)
                    turn_in(b, "x0", work, 0)
                    turn_in(b, "x1", work, 1)

                def route_and_first(b):
                    ready(b, "x0", "x1")
                    fill(b, "lg", lambda bank: product(bank[0:E, 0:S], [
                        ((router_hi[:, k, :], router_lo[:, k, :]), xcols(k)) for k in range(KC)]))
                    hidden(b, 0)

                def logits_and_second(b):
                    ready(b, "lg")

                    def emit(bank):
                        plain(pe)
                        for t in range(NT):
                            ins = pe.transpose(bank[0:T, t * E:t * E + E], logits_T[:, t * T:t * T + T], ident[0:E, 0:E])
                        return ins
                    fill(b, "lt", emit)
                    hidden(b, 1)

                def experts(b, n):
                    for e in range(2, E):
                        hidden(b, e)
                        expert_out(b, e - 2)
                    if n is not None:
                        inputs(n)
                    expert_out(b, E - 2)
                    if n is not None:
                        route_and_first(n)
                    expert_out(b, E - 1)
                    if n is not None:
                        logits_and_second(n)

                inputs(FIRST)
                pe.wait_ge(w_lo_done, first_piece[3] + 1)
                route_and_first(FIRST)
                logits_and_second(FIRST)
                with pe.Fori(0, B - 1) as b:
                    experts(b, b + 1)
                experts(B - 1, None)

        @block.scalar
        def _(act):
            def split(phase, first, last):
                for p, src, cols, scale, _ in parts_of(phase):
                    if first <= p - first_piece[phase] < last:
                        act.wait_ge(staged[p % STAGES],
                                    16 * sum(len(flat[n][0]) for n in range(p % STAGES, p + 1, STAGES)))
                        act.activation(w_hi[:, cols], src, ACT.Copy, scale=scale).then_inc(w_hi_done, 1)

            for phase in range(3):
                a, order = a_ring[phase], A_ORDER[phase]
                LAG = LAGS[phase] if phase < 2 else 0

                def hi(b, name, dst, bias=None):
                    a.wait_full(act, b, name)
                    if bias is None:
                        ins = act.activation(dst, A[a.slot(name)][:, 0:S], ACT.Copy)
                    else:
                        ins = act.activation(dst, A[a.slot(name)][:, 0:S], ACT.Identity, bias=bias)
                    ins.then_inc(cat_hi if name[0] == "c" else hi_done[phase], 1)

                def copy_out(b, name, dst, cols):
                    a.wait_full(act, b, name)
                    a.freed(act.activation(dst, A[a.slot(name)][0:dst.shape[0], 0:cols], ACT.Copy), name)

                def hi_qk(b, c, m):
                    hi(b, f"{c}{m}", {"q": q_hi, "k": k_hi}[c][:, m % 2, :],
                       col_bias[:, "qk".index(c), m:m + 1] if phase == 0 else None)

                def ahead(b, name):
                    kind, i = name[:-1], int(name[-1])
                    if kind == "x":
                        hi(b, name, xT_hi[:, i, :])
                    elif kind == "v":
                        copy_out(b, name, v[:, i // 2, 512 * (i % 2):512 * (i % 2) + 512], 512)
                    elif kind == "mv":
                        copy_out(b, name, mv[:, i, :], D)
                    elif kind in ("mq", "mk"):
                        hi(b, name, {"mq": q_hi, "mk": k_hi}[kind][:, i, :],
                           mem_bias[:, ("mq", "mk").index(kind), i:i + 1])
                    else:
                        hi_qk(b, kind, i)

                def turned_memory(b):
                    t_ring[0].wait_full(act, b, 1)
                    t_ring[0].freed(act.activation(pT[0:T, 2, S:2 * S], TP[1][0:T, 0:S], ACT.Copy), 1)

                def exp_memory(b):
                    for t in range(NT):
                        act.wait_ge(maxed[0], b * UNITS[0] + (t + 1))
                        ins = act.activation(probs[:, 0, t * S:t * S + S], SC[t][0:T, 0:S], ACT.Exp,
                                             bias=neg_max[:, H, t:t + 1], accum_out=sums[:, H, t:t + 1])
                        s_ring[0].freed(ins, t)

                def exp_head(b, h):
                    p_n = p_use(phase, h)
                    if phase == 1 and LAG == PRING and h >= PRING:
                        t_ring[1].wait_full(act, b, NT * (h - PRING) + NT - 1)
                    for t in range(NT):
                        n = s_use(phase, h, t)
                        c, cols = row_of(phase, h, t)
                        if phase == 1 or t == 0:
                            act.wait_ge(maxed[phase], b * UNITS[phase] + (n + 1))
                        at = c if phase == 0 else 0
                        ins = act.activation(probs[:, p_n % PRING, c:c + cols], SC[n % 3][0:T, at:at + cols], ACT.Exp,
                                             bias=neg_max[:, h, t:t + 1], accum_out=sums[:, h, t:t + 1])
                        if phase == 1 or t == NT - 1:
                            s_ring[phase].freed(ins, n)

                def copy_turned(b, h, tiles):
                    for n in turned(phase, h, tiles):
                        if n % 2:
                            t_ring[phase].wait_full(act, b, n)
                            c, cols = (0, 5 * T) if phase == 0 else ((n - NT * h) * S, S)
                            t_ring[phase].freed(act.activation(pT[0:T, h % 4, c:c + cols], TP[1][0:T, 0:cols],
                                                               ACT.Copy), n)

                def hi_out(b, m):
                    act.wait_ge(pv_done[phase], b * HP + (m + 1))
                    if phase == 0:
                        act.activation(oT_hi[:, m, :], OB[:, 0:S], ACT.Identity, bias=col_bias[:, 2, m:m + 1])\
                           .then_inc(o_hi_done, 1)
                    else:
                        act.activation(o_raw[:, m, :], OB[:, 0:S], ACT.Copy).then_inc(o_lo_done[1], 1)

                def activate(b, g):
                    if g in (0, HP // 2 - 1):
                        act.wait_ge(o_lo_done[1], b * HP + ((HP - 2 if g == 0 else HP) + PRIMED))
                    act.activation(o_raw[:, 2 * g:2 * g + 2, :], o_raw[:, 2 * g:2 * g + 2, :], ACT.Gelu)\
                       .then_inc(gelu_done, 1)

                def entry(b, n):
                    def between(at):
                        if n is not None:
                            for name in AHEAD[phase].get(at, ()):
                                ahead(n, name)

                    for h in range(1, H + LAG + 1):
                        if LAG <= h < H + LAG:
                            copy_turned(b, h - LAG, (0, 1))
                        if h < H:
                            exp_head(b, h)
                        if LAG <= h < H + LAG:
                            copy_turned(b, h - LAG, (2,))
                        for c, m in qk_at(h):
                            hi_qk(b, c, m)
                        between(h)
                        if phase == 0 and h == MEMORY_AT and n is not None:
                            exp_memory(n)
                        if n is None and SPLIT_AT <= h < SPLIT_AT + EARLY_PIECES:
                            if phase == 1 and h == SPLIT_AT:
                                act.activation(router_hi[:, :, :], router[:, :, :], ACT.Copy).then_inc(w_hi_done, 1)
                            split(phase + 1, h - SPLIT_AT, h - SPLIT_AT + 1)
                        if (h - LAG) % 2 == 0 and h > LAG:
                            hi_out(b, (h - LAG) // 2 - 1)
                        if phase == 1 and h == H:
                            for g in range(HP // 2 - 1):
                                activate(b, g)
                    if phase:
                        activate(b, HP // 2 - 1)
                    between("a")
                    if phase == 0:
                        between("b")
                        hi(b, "c2", oT_hi[:, 2, :])
                        hi(b, "c3", oT_hi[:, 3, :])
                        between("c")
                        hi(b, "c0", oT_hi[:, 0, :])
                        hi(b, "c1", oT_hi[:, 1, :])
                        between("d")
                        if n is not None:
                            exp_head(n, 0)
                        for t in range(NT):
                            a.wait_freed(act, b, f"g{t}")
                            act.activation(tmp[:, t, :], tmp[:, t, :], ACT.Tanh, scale=0.5).then_inc(gate_tanh, 1)
                        between("e")
                        if n is not None:
                            turned_memory(n)
                    else:
                        if n is not None:
                            exp_head(n, 0)
                        between("b")

                if phase == 0:
                    act.wait_ge(const_ready, 1)
                    hi(FIRST, "x0", xT_hi[:, 0, :])
                    hi(FIRST, "x1", xT_hi[:, 1, :])
                    split(0, 0, 3)
                if phase < 2:
                    if phase == 1:
                        split(1, EARLY_PIECES, len(pieces[1]))
                    for name in early[phase]:
                        if phase == 0 and name == "mq0":
                            split(0, 3, 8)
                        if name == "mv0":
                            exp_memory(FIRST)
                        if name == "k1":
                            exp_head(FIRST, 0)
                        if (phase, name[0]) != (0, "x"):
                            ahead(FIRST, name)
                        if phase == 0 and name == "mk1":
                            split(0, 8, len(pieces[0]))
                    if phase == 0:
                        turned_memory(FIRST)
                    with act.Fori(0, B - 1) as b:
                        entry(b, b + 1)
                    entry(B - 1, None)
                    continue

                a_ring[1].wait_full(act, B - 1, "wo2")
                split(2, EARLY_PIECES, len(pieces[2]))

                def hi_hidden(b, e):
                    for i in range(EC * e, EC * e + EC):
                        n = f"h{e}_{i % EC}"
                        a.wait_full(act, b, n)
                        if i >= 4 or b is not FIRST:
                            act.wait_ge(squared, b * (E * EC) + (i - 3))
                        a.freed(act.activation(pT[:, i % 4, S:2 * S], A[a.slot(n)][:, 0:S], ACT.Relu), n)
                    for i in range(EC * e, EC * e + EC):
                        act.wait_ge(squared, b * (E * EC) + (i + 1))
                        act.activation(oT_hi[:, i % (4 * EC), :], pT[:, i % 4, 0:S], ACT.Copy).then_inc(hidden_hi, 1)

                def inputs(b):
                    hi(b, "x0", xT_hi[:, 0, :])
                    hi(b, "x1", xT_hi[:, 1, :])
                    copy_out(b, "lg", logits_T[:, :], S)
                    hi_hidden(b, 0)

                def second(b):
                    hi_hidden(b, 1)
                    act.wait_ge(margin_ready, b + 1)
                    act.activation(route[:, :, 1], route[:, :, 0], ACT.Exp).then_inc(margin_exp, 1)

                def experts(b, n):
                    for e in range(2, E):
                        hi_hidden(b, e)
                    if n is not None:
                        inputs(n)
                        second(n)

                inputs(FIRST)
                second(FIRST)
                with act.Fori(0, B - 1) as b:
                    experts(b, b + 1)
                experts(B - 1, None)

        @block.vector
        def _(dve):
            lo_n = [0]

            def split(phase, first, last_piece):
                for p, src, cols, scale, last in parts_of(phase):
                    if not first <= p - first_piece[phase] < last_piece:
                        continue
                    lo_n[0] += 1
                    dve.wait_ge(w_hi_done, lo_n[0])
                    ins = dve.scalar_tensor_tensor(out=w_lo[:, cols], in0=src, scalar=scale,
                                                   in1=w_hi[:, cols].bitcast(F32), op0=ALU.mult, op1=ALU.subtract)
                    if last:
                        ins.then_inc(w_lo_done, 1)

            vector_chains = [Chain(chains[ph], dve, CHAIN_STEPS[ph]) for ph in range(3)]

            for phase in range(3):
                a, order = a_ring[phase], A_ORDER[phase]
                LAG = LAGS[phase] if phase < 2 else 0
                chain = vector_chains[phase]

                def lo(b, name, hi_ap, dst, bias=None):
                    n = a.slot(name)
                    if name[0] == "c":
                        dve.wait_ge(cat_hi, b * len(CAT_ORDER) + (CAT_ORDER.index(name) + 1))
                    else:
                        dve.wait_ge(hi_done[phase], b * len(HI_ORDER[phase]) + (HI_ORDER[phase].index(name) + 1))
                    if bias is None:
                        ins = dve.tensor_tensor(dst, A[n][:, 0:S], hi_ap.bitcast(F32), ALU.subtract)
                    else:
                        ins = dve.scalar_tensor_tensor(out=dst, in0=A[n][:, 0:S], scalar=bias,
                                                       in1=hi_ap.bitcast(F32), op0=ALU.add, op1=ALU.subtract)
                    a.freed(ins, name)

                def lo_qk(b, c, m):
                    h_ap, l_ap = {"q": (q_hi, q_lo), "k": (k_hi, k_lo)}[c]
                    lo(b, f"{c}{m}", h_ap[:, m % 2, :], l_ap[:, m % 2, :],
                       col_bias[:, "qk".index(c), m:m + 1] if phase == 0 else None)

                def max_head(b, h):
                    if phase == 0:
                        n = s_use(0, h)
                        s_ring[0].wait_full(dve, b, n)
                        dve.tensor_reduce(neg_max[:, h, 0:1], SC[n % 3][0:T, 0:T], AX.X, ALU.max, negate=True)
                        dve.tensor_reduce(neg_max[:, h, 1:NT],
                                          SC[n % 3][0:T, T:5 * T].rearrange("p (t n) -> p t n", t=2),
                                          AX.X, ALU.max, negate=True).then_inc(maxed[0], 1)
                        return
                    for t in range(NT):
                        n = s_use(1, h, t)
                        s_ring[1].wait_full(dve, b, n)
                        dve.tensor_reduce(neg_max[:, h, t:t + 1], SC[n % 3][0:T, 0:S], AX.X, ALU.max, negate=True)\
                           .then_inc(maxed[1], 1)

                def invert(b, h):
                    for t in range(NT):
                        if phase == 1 or t == NT - 1:
                            s_ring[phase].wait_freed(dve, b, s_use(phase, h, t))
                    dve.reciprocal(recip[:, h, :], sums[:, h, :]).then_inc(inverted[phase], 1)

                def copy_turned(b, h, tiles):
                    for n in turned(phase, h, tiles):
                        if n % 2 == 0:
                            t_ring[phase].wait_full(dve, b, n)
                            c, cols = (0, 5 * T) if phase == 0 else ((n - NT * h) * S, S)
                            t_ring[phase].freed(dve.tensor_copy(pT[0:T, h % 4, c:c + cols], TP[0][0:T, 0:cols]), n)

                def lo_out(b, m):
                    dve.wait_ge(o_hi_done, b * HP + (m + 1))
                    dve.scalar_tensor_tensor(out=oT_lo[:, m, :], in0=OB[:, 0:S], scalar=col_bias[:, 2, m:m + 1],
                                             in1=oT_hi[:, m, :].bitcast(F32), op0=ALU.add, op1=ALU.subtract)\
                       .then_inc(o_lo_done[0], 1)

                def tile_stats(src, t):
                    chain.step(dve.bn_stats(bn[:, t, :], src[:, t, :]))

                def norm_stats(ph, src):
                    steps = vector_chains[ph]
                    for t in range(NT if src is not None else 0):
                        steps.step(dve.bn_stats(bn[:, t, :], src[:, t, :]))
                    steps.wait()
                    plain(dve)
                    for t in range(NT):
                        steps.step(dve.bn_aggr(mean_var[:, t, :], bn[:, t, :]))
                    steps.wait()
                    dve.tensor_scalar(rstd[:, :], mean_var[:, :, 1], EPS, None, ALU.add).then_inc(stats[ph], 1)

                def norm_apply(ph, count, src, dst):
                    dve.wait_ge(rooted[ph], count)
                    for t in range(NT):
                        ins = dve.tensor_scalar(dst[:, t, :], src[:, t, :], mean_var[:, t, 0:1], rstd[:, t:t + 1],
                                                ALU.subtract, ALU.mult)
                        if t < NT - 1:
                            vector_chains[ph].step(ins)
                    ins.then_inc(normed[ph], 1)

                def input_stats(ph, b):
                    dve.wait_ge(entry_in[ph], 16 * b + 16)
                    vector_chains[ph].start(b)
                    norm_stats(ph, h_in)

                def input_apply(ph, b):
                    norm_apply(ph, b + 1, h_in, mv if ph == 1 else work)

                def centre(x_ap, tiles, gain):
                    for t in tiles:
                        chain.step(dve.scalar_tensor_tensor(out=x_ap[:, t, :], in0=x_ap[:, t, :],
                                                            scalar=mean_var[:, t, 0:1], in1=rows_bc[:, gain, :],
                                                            op0=ALU.subtract, op1=ALU.mult))

                def spread(x_ap, tiles, shift):
                    chain.wait()
                    for t in tiles:
                        ins = dve.scalar_tensor_tensor(out=x_ap[:, t, :], in0=x_ap[:, t, :], scalar=rstd[:, t:t + 1],
                                                       in1=rows_bc[:, shift, :], op0=ALU.mult, op1=ALU.add)
                    if NT - 1 in tiles:
                        ins.then_inc(normed[0], 1)

                def ahead(b, name):
                    kind, i = name[:-1], int(name[-1])
                    if kind == "x":
                        lo(b, name, xT_hi[:, i, :], xT_lo[:, i, :])
                    elif kind == "mq":
                        lo(b, name, q_hi[:, i, :], q_lo[:, i, :], mem_bias[:, 0, i:i + 1])
                    elif kind == "mk":
                        lo(b, name, k_hi[:, i, :], k_lo[:, i, :], mem_bias[:, 1, i:i + 1])
                    elif kind in ("q", "k"):
                        lo_qk(b, kind, i)

                def max_memory(b):
                    for t in range(NT):
                        s_ring[0].wait_full(dve, b, t)
                        dve.tensor_reduce(neg_max[:, H, t:t + 1], SC[t][0:T, 0:S], AX.X, ALU.max, negate=True)\
                           .then_inc(maxed[0], 1)

                def keep_input(b):
                    dve.wait_ge(normed[1], b + 1)
                    dve.tensor_tensor(keep[:, :, :], h_in[:, :, :], mv[:, :, :], ALU.add).then_inc(kept, 1)

                def gate_sum(b):
                    dve.wait_ge(stored[0], 16 * b + PRIMED)
                    for t in range(NT):
                        n = f"g{t}"
                        a.wait_full(dve, b, n)
                        a.freed(dve.tensor_tensor(tmp[:, t, :], A[a.slot(n)][0:T, 0:D], rows_bc[:, GB, :], ALU.add), n)

                def gate_mix(b):
                    dve.wait_ge(gate_tanh, NT * b + NT)
                    dve.wait_ge(differed, b + 1)
                    chain.link(dve.scalar_tensor_tensor(out=tmp[:, :, :], in0=tmp[:, :, :], scalar=1.0, in1=work[:, :, :],
                                                        op0=ALU.add, op1=ALU.mult))
                    dve.scalar_tensor_tensor(out=tmp[:, :, :], in0=tmp[:, :, :], scalar=0.5, in1=keep[:, :, :],
                                             op0=ALU.mult, op1=ALU.add).then_inc(gated, 1)
                    chain.end()

                def memory_sums(b):
                    s_ring[0].wait_all_freed(dve, b, range(NT))
                    p_ring[0].filled(dve.reciprocal(recip[:, H, :], sums[:, H, :]), 0)

                def turned_memory(b, t):
                    t_ring[0].wait_full(dve, b, t)
                    t_ring[0].freed(dve.tensor_copy(pT[0:T, 2, t * S:t * S + S], TP[0][0:T, 0:S]), t)

                def entry(b, n):
                    def between(at):
                        if n is not None:
                            for name in AHEAD[phase].get(at, ()):
                                ahead(n, name)

                    if phase == 0:
                        chain.start(b)
                    normed_next = (phase + 1, FIRST) if n is None else (1, n) if phase else None
                    for h in range(1, H + LAG + 1):
                        if LAG <= h < H + LAG:
                            copy_turned(b, h - LAG, (0, 1))
                        if h < H:
                            max_head(b, h)
                        if LAG <= h < H + LAG:
                            copy_turned(b, h - LAG, (2,))
                        if LATE[phase][0]:
                            if 2 <= h <= H:
                                invert(b, h - 1)
                        if LATE[phase][1]:
                            late = ([] if phase == 0 and h == MEMORY_OUT_AT + 1 else qk_at(h - 1)) + (
                                qk_at(h) if phase == 0 and h == MEMORY_OUT_AT else [])
                            for c, m in late:
                                lo_qk(b, c, m)
                        else:
                            for c, m in qk_at(h):
                                lo_qk(b, c, m)
                        if not LATE[phase][0]:
                            if h < H:
                                invert(b, h)
                        if phase == 0 and h == 1:
                            turned_memory(b, 2)
                        if phase == 0 and h == MEMORY_OUT_AT:
                            p_ring[0].wait_full(dve, b, 0)
                            dve.wait_ge(gated, b + PRIMED)
                            for t in range(NT):
                                name = f"mo{t}"
                                a.wait_full(dve, b, name)
                                a.freed(dve.scalar_tensor_tensor(out=keep[:, t, :], in0=A[a.slot(name)][0:T, 0:D],
                                                                 scalar=recip[:, H, t:t + 1], in1=rows_bc[:, MBV, :],
                                                                 op0=ALU.mult, op1=ALU.add), name)
                                a.wait_freed(dve, b, name)
                                tile_stats(keep, t)
                            norm_stats(0, None)
                        if phase == 0 and MEMORY_OUT_AT + 2 <= h < MEMORY_OUT_AT + 2 + NT:
                            t = h - MEMORY_OUT_AT - 2
                            if t == 0:
                                dve.wait_ge(rooted[0], 2 * b + 1)
                            centre(keep, (t,), G2W)
                            spread(keep, (t,), G2B)
                        between(h)
                        if normed_next and h == NORM_AT:
                            input_stats(*normed_next)
                        if normed_next and h == NORM_AT + 2:
                            input_apply(*normed_next)
                        if phase == 0 and h == MEMORY_AT and n is not None:
                            max_memory(n)
                        if n is None and SPLIT_AT <= h < SPLIT_AT + EARLY_PIECES:
                            if phase == 1 and h == SPLIT_AT:
                                lo_n[0] += 1
                                dve.wait_ge(w_hi_done, lo_n[0])
                                dve.tensor_tensor(router_lo[:, :, :], router[:, :, :], router_hi[:, :, :].bitcast(F32),
                                                  ALU.subtract).then_inc(w_lo_done, 1)
                            split(phase + 1, h - SPLIT_AT, h - SPLIT_AT + 1)
                        if phase == 0 and (h - LAG) % 2 == 0 and h > LAG:
                            lo_out(b, (h - LAG) // 2 - 1)
                        if phase == 1 and h == H + 1:
                            for g in range(HP // 2 - 1):
                                gelu_high(b, g)
                    if phase:
                        g = HP // 2 - 1
                        gelu_high(b, g)
                        dve.wait_ge(gelu_hi, b * (HP // 2) + (g + 1))
                        dve.tensor_tensor(oT_lo[:, 2 * g:2 * g + 2, :], o_raw[:, 2 * g:2 * g + 2, :],
                                          oT_hi[:, 2 * g:2 * g + 2, :].bitcast(F32), ALU.subtract).then_inc(gelu_lo, 1)
                    between("a")
                    if phase == 0:
                        for t in range(NT):
                            name = f"wo{t}"
                            a.wait_full(dve, b, name)
                            a.freed(dve.tensor_tensor(work[:, t, :], A[a.slot(name)][0:T, 0:D], rows_bc[:, BO, :],
                                                      ALU.add), name)
                            a.wait_freed(dve, b, name)
                            tile_stats(work, t)
                        norm_stats(0, None)
                        centre(work, range(NT), G1W)
                        between("b")
                        lo(b, "c2", oT_hi[:, 2, :], oT_lo[:, 2, :])
                        lo(b, "c3", oT_hi[:, 3, :], oT_lo[:, 3, :])
                        dve.wait_ge(rooted[0], 2 * b + 2)
                        spread(work, range(NT), G1B)
                        between("c")
                        lo(b, "c0", oT_hi[:, 0, :], oT_lo[:, 0, :])
                        lo(b, "c1", oT_hi[:, 1, :], oT_lo[:, 1, :])
                        between("d")
                        if n is not None:
                            max_head(n, 0)
                            memory_sums(n)
                        gate_sum(b)
                        between("e")
                        if n is not None:
                            invert(n, 0)
                            turned_memory(n, 0)
                        gate_mix(b)
                    else:
                        if n is not None:
                            max_head(n, 0)
                        between("b")
                        if n is not None:
                            invert(n, 0)
                        dve.wait_ge(stored[1], 16 * b + PRIMED)
                        for t in range(NT):
                            name = f"wo{t}"
                            a.wait_full(dve, b, name)
                            a.freed(dve.tensor_tensor(tmp[:, t, :], A[a.slot(name)][0:T, 0:D], keep[:, t, :], ALU.add),
                                    name)
                        if n is not None:
                            a.wait_all_freed(dve, b, wo_a)
                            keep_input(n)

                def gelu_high(b, g):
                    dve.wait_ge(gelu_done, b * (HP // 2) + (g + 1))
                    dve.tensor_copy(oT_hi[:, 2 * g:2 * g + 2, :], o_raw[:, 2 * g:2 * g + 2, :]).then_inc(gelu_hi, 1)

                if phase < 2:
                    if phase == 1:
                        split(1, EARLY_PIECES, len(pieces[1]))
                        dve.wait_ge(gated, B + PRIMED)
                        keep_input(FIRST)
                    for name in early[phase]:
                        if phase == 0 and name == "v0":
                            split(0, 0, 3)
                        if name == "mv0":
                            max_memory(FIRST)
                        if name == "k1":
                            if phase == 0:
                                memory_sums(FIRST)
                            max_head(FIRST, 0)
                        ahead(FIRST, name)
                        if phase == 0 and name == "mk1":
                            split(0, 3, 8)
                        if phase == 0 and name == "v5":
                            split(0, 8, len(pieces[0]))
                    invert(FIRST, 0)
                    if phase == 0:
                        turned_memory(FIRST, 0)
                    else:
                        dve.wait_ge(stored[0], 16 * B + PRIMED)
                    with dve.Fori(0, B - 1) as b:
                        entry(b, b + 1)
                    entry(B - 1, None)
                    continue

                def square(b, e):
                    for i in range(EC * e, EC * e + EC):
                        a.wait_freed(dve, b, f"h{e}_{i % EC}")
                        if i >= 4 or b is not FIRST:
                            dve.wait_ge(hidden_lo, b * (E * EC) + (i - 3))
                        rectified = pT[:, i % 4, S:2 * S]
                        dve.tensor_tensor(pT[:, i % 4, 0:S], rectified, rectified, ALU.mult).then_inc(squared, 1)

                def best_two(b):
                    a.wait_full(dve, b, "lt")
                    a.freed(dve.tensor_copy(logits[:, :, :].rearrange("p t e -> p (t e)"),
                                            A[a.slot("lt")][0:T, 0:NT * E]), "lt")
                    square(b, 1)
                    a.wait_freed(dve, b, "lt")
                    plain(dve)
                    for t in range(NT):
                        chain.step(dve.max(top[:, t, :], logits[:, t, :]))
                    chain.wait()
                    plain(dve)
                    for t in range(NT):
                        chain.step(dve.max_index(top_no[:, t, :], top[:, t, :], logits[:, t, :]))
                    dve.tensor_tensor(route[:, :, 0], top[:, :, 1], top[:, :, 0], ALU.subtract)\
                       .then_inc(margin_ready, 1)

                def shares(b):
                    chain.start(b, SHARES_FROM)
                    chain.wait()
                    chain.step(dve.tensor_copy(top_nof[:, :, :], top_no[:, :, 0:2]))
                    dve.wait_ge(margin_exp, b + 1)
                    chain.link(dve.tensor_scalar(route[:, :, 2], route[:, :, 1], 1.0, None, ALU.add))
                    chain.link(dve.reciprocal(route[:, :, 2], route[:, :, 2]))
                    chain.link(dve.tensor_tensor(route[:, :, 3], route[:, :, 1], route[:, :, 2], ALU.mult))
                    for t in range(NT):
                        for i in range(2):
                            chain.step(dve.tensor_scalar(gates[:, i, t, :], expert_no[:, :], top_nof[:, t, i:i + 1],
                                                         route[:, t, 2 + i:3 + i], ALU.is_equal, ALU.mult))
                    chain.wait()
                    chain.link(dve.tensor_tensor(gates[:, 0, :, :], gates[:, 0, :, :], gates[:, 1, :, :], ALU.add))
                    chain.end()

                def gather(b, e):
                    for t in range(NT):
                        n = NT * e + t
                        o_banks.wait_full(dve, b, n)
                        if e:
                            o_banks.wait_freed(dve, b, n - NT)
                        src = h_in if e == 0 else keep
                        dst = tmp if e == E - 1 else keep
                        o_banks.freed(dve.scalar_tensor_tensor(
                            out=dst[:, t, :], in0=(SC + TP + [OB])[n % 6][0:T, 0:D], scalar=gates[:, 0, t, e:e + 1],
                            in1=src[:, t, :], op0=ALU.mult, op1=ALU.add), n)

                def inputs(b):
                    lo(b, "x0", xT_hi[:, 0, :], xT_lo[:, 0, :])
                    lo(b, "x1", xT_hi[:, 1, :], xT_lo[:, 1, :])

                def experts(b, n):
                    for e in range(2, E):
                        square(b, e)
                        if e == 2:
                            shares(b)
                        gather(b, e - 2)
                        if e == EXPERT_NORM_AT and n is not None:
                            input_stats(2, n)
                        if e == EXPERT_NORM_AT + 1 and n is not None:
                            input_apply(2, n)
                    if n is not None:
                        inputs(n)
                    gather(b, E - 2)
                    if n is not None:
                        square(n, 0)
                    dve.wait_ge(stored[2], 16 * b + PRIMED)
                    gather(b, E - 1)
                    if n is not None:
                        best_two(n)

                split(2, EARLY_PIECES, len(pieces[2]))
                inputs(FIRST)
                square(FIRST, 0)
                best_two(FIRST)
                dve.wait_ge(stored[1], 16 * B + PRIMED)
                with dve.Fori(0, B - 1) as b:
                    experts(b, b + 1)
                experts(B - 1, None)


def kernel(**inputs):
    import numpy as _np
    import concourse.bacc as _bacc
    from concourse import mybir as _mybir
    from concourse.bass_utils import run_bass_kernel_spmd as _run

    nc = _bacc.Bacc("TRN2", target_bir_lowering=False, num_devices=1)
    arrays, args = {}, {}
    for name, value in inputs.items():
        a = _np.ascontiguousarray(value)
        arrays[f"in_{name}_dram"] = a
        args[name] = nc.dram_tensor(f"in_{name}_dram", a.shape, _mybir.dt.from_np(a.dtype), kind="ExternalInput").ap()
    out = nc.dram_tensor("out_0_dram", (B, S, D), F32, kind="ExternalOutput").ap()
    build(nc, out, **args)
    r = _run(nc, [arrays], core_ids=[0])
    return r.results[0]["out_0_dram"]
```

```python
from contextlib import ExitStack

import concourse.bass as bass
from concourse import mybir
from concourse.alu_op_type import AluOpType as ALU

F32 = mybir.dt.float32
F32R = mybir.dt.float32r
BF16 = mybir.dt.bfloat16
U32 = mybir.dt.uint32
ACT = mybir.ActivationFunctionType
AX = mybir.AxisListType

B, S0, D = 8, 256, 256
PM = 32
S = S0 + PM
T = 96
NT = S // T
KC = D // 128
H, HD = 16, 64
HP = H // 2
WINDOW = 64
E, DE = 8, 256
EC = DE // 128
INNER = H * HD
EPS = 1e-5
MASKED = -3.0e38
PIECE = 1024
STAGES = 8
WCOLS = 10 * PIECE + 2 * D
WIN = [(0, 0, 1), (T, 0, 2), (3 * T, 1, 2)]
WINT = [(0, 0, 2), (2 * T, 1, 2), (4 * T, 2, 1)]
PRING = 3
SCALAR_TILE = 0
MEMORY_OUT_AT = 3
NORM_AT = 8
EXPERT_NORM_AT = 4
LAGS = [3, 2]
PRIMED = 1
CONST_STEPS = 15
CHAIN_STEPS = [18, 8, 25]
SHARES_FROM = 14


class Ring:

    def __init__(self, sem, name, size, order, early=()):
        self.order = list(order) if not isinstance(order, int) else list(range(order))
        self.size, self.early = size, set(early)
        self.full = [sem(f"{name}{i}_full") for i in range(size)]
        self.free = [sem(f"{name}{i}_free") for i in range(size)]
        self.primed = 0 if self.early else PRIMED
        self.per = [(len(self.order) + size - 1 - i) // size for i in range(size)]

    def slot(self, use):
        return self.order.index(use) % self.size

    def fills(self, b, use, more):
        n = self.order.index(use)
        per = self.per[n % self.size]
        steps = bool(self.early) - (use in self.early)
        return b * per + (steps * per + n // self.size + more)

    def wait_free(self, eng, b, use):
        eng.wait_ge(self.free[self.slot(use)], self.fills(b, use, self.primed))

    def wait_full(self, eng, b, use):
        eng.wait_ge(self.full[self.slot(use)], self.fills(b, use, 1))

    def wait_freed(self, eng, b, use):
        eng.wait_ge(self.free[self.slot(use)], self.fills(b, use, 1 + self.primed))

    def wait_all_freed(self, eng, b, uses):
        in_time = sorted(uses, key=lambda use: (use not in self.early, self.order.index(use)))
        for use in {self.slot(use): use for use in in_time}.values():
            self.wait_freed(eng, b, use)

    def filled(self, ins, use):
        ins.then_inc(self.full[self.slot(use)], 1)

    def freed(self, ins, use):
        ins.then_inc(self.free[self.slot(use)], 1)


class Chain:

    def __init__(self, sem, eng, per):
        self.sem, self.eng, self.per, self.n = sem, eng, per, 0

    def start(self, b, n=0):
        self.b, self.n = b, n

    def step(self, ins):
        ins.then_inc(self.sem, 1)
        self.n += 1

    def wait(self):
        self.eng.wait_ge(self.sem, self.b * self.per + self.n)

    def link(self, ins):
        self.step(ins)
        self.wait()

    def end(self):
        assert self.n == self.per, (self.n, self.per)


def weight_pieces(w):
    def rows(x, k, n, cols):
        return x[128 * k:128 * (k + n), :].rearrange("(k p) n -> p k n", p=128), n, cols

    def plain(name):
        return [rows(w[name], k, 1, INNER) for k in range(KC)]

    qk = float(HD) ** -0.5
    tok = [([d], [(PIECE, 1.0)]) for d in plain("L0_tok_Wv")]
    tok += [([rows(w["L0_tok_mWq"], 0, 2, D), rows(w["L0_tok_mWk"], 0, 2, D)],
             [(2 * D, float(D) ** -0.5), (2 * D, 0.1)])]
    tok += [([d], [(PIECE, s)]) for name, s in (("L0_tok_Wq", qk), ("L0_tok_Wk", 1.0)) for d in plain(name)]
    tok += [([rows(w["L0_tok_mWv"], 0, 2, D), rows(w["L0_tok_gate_W"], 0, 2, D)], [(2 * D, 0.1), (2 * D, 1.0)])]
    tok += [([rows(w["L0_tok_Wo"], 4 * i, 4, D)], [(PIECE, 1.0)]) for i in range(2)]
    tok += [([rows(w["L0_tok_gate_W"], 2, 2, D)], [(2 * D, 1.0)])]
    attn = [([d], [(PIECE, s)]) for name, s in (("L0_attn_Wq", 1.0), ("L0_attn_Wk", qk), ("L0_attn_Wv", 1.0))
            for d in plain(name)]
    attn += [([rows(w["L0_attn_Wpost"], 4 * i, 4, D)], [(PIECE, 1.0)]) for i in range(2)]
    ffn = []
    for name in ("L0_ffn_w1_all", "L0_ffn_w2_all"):
        for e in range(0, E, 2):
            src = w[name][e:e + 2].rearrange("e (k p) n -> p (e k) n", p=128)
            ffn.append(([(src, 2 * KC, DE)], [(PIECE, 1.0)]))
    return [tok, attn, ffn]


WQ = [3 * PIECE, 0]
WK = [5 * PIECE, 2 * PIECE]
WV = [0, 4 * PIECE]
WMQ, WMK = 2 * PIECE, 2 * PIECE + KC * D
WMV = 7 * PIECE
WO = [8 * PIECE, 6 * PIECE]
WG = [7 * PIECE + KC * D, 10 * PIECE]
W1, W2 = 0, E * KC * DE
EARLY_PIECES = 6


def build(nc, out, **w):
    ctx = ExitStack()
    with ctx:
        def sb(name, shape, dt=F32):
            return ctx.enter_context(nc.sbuf_tensor(name, shape, dt))

        def sem(name):
            return ctx.enter_context(nc.semaphore(name))

        x = w["x"]
        h_tok = nc.dram_tensor("h_tok", (B, S, D), F32, kind="Internal").ap()
        h_attn = nc.dram_tensor("h_attn", (B, S, D), F32, kind="Internal").ap()
        pieces = weight_pieces(w)
        flat = [p for phase in pieces for p in phase]
        first_piece = [0, len(pieces[0]), len(pieces[0]) + len(pieces[1]), len(flat)]

        stage = sb("stage", [128, STAGES, PIECE])
        with nc.sbuf_tensor("w_hi", [128, WCOLS], F32R) as w_hi:
            pass
        sb("later_weights", [128, 8 * PIECE], F32R)
        o_raw = sb("o_raw", [128, HP, S])
        sb("behind_o_raw", [128, WCOLS - 8 * PIECE - HP * S])
        w_lo = sb("w_lo", [128, WCOLS], F32R)
        router = sb("router", [128, KC, E])
        router_hi = sb("router_hi", [128, KC, E], F32R)
        router_lo = sb("router_lo", [128, KC, E], F32R)
        ident = sb("ident", [T, T])
        ident_bf = sb("ident_bf", [T, T], BF16)
        mask_bf = sb("mask_bf", [T, 5 * T], BF16)
        col_bias = sb("col_bias", [128, 3, HP])
        mem_bias = sb("mem_bias", [128, 2, KC])
        rows_bc = sb("rows_bc", [T, 7, D])
        BO, MBV, G1W, G1B, G2W, G2B, GB = range(7)
        expert_no = sb("expert_no", [T, E])
        expert_no_i = sb("expert_no_i", [T, E], mybir.dt.int32)
        neg_half = sb("neg_half", [T, NT])
        xT_hi = sb("xT_hi", [128, KC, S], F32R)
        xT_lo = sb("xT_lo", [128, KC, S], F32R)
        q_hi = sb("q_hi", [128, 2, S], F32R)
        q_lo = sb("q_lo", [128, 2, S], F32R)
        k_hi = sb("k_hi", [128, 2, S], F32R)
        k_lo = sb("k_lo", [128, 2, S], F32R)
        oT_hi = sb("oT_hi", [128, HP, S], F32R)
        oT_lo = sb("oT_lo", [128, HP, S], F32R)
        h_in = sb("h_in", [T, NT, D])
        keep = sb("keep", [T, NT, D])
        work = sb("work", [T, NT, D])
        tmp = sb("tmp", [T, NT, D])
        mv = sb("mv", [T, NT, D])
        v = sb("v", [T, NT, INNER])
        probs = sb("probs", [T, PRING, NT * S])
        pT = sb("pT", [128, 4, NT * S])
        neg_max = sb("neg_max", [T, H + 1, NT])
        sums = sb("sums", [T, H + 1, NT])
        recip = sb("recip", [T, H + 1, NT])
        bn = sb("bn", [T, NT, 6])
        mean_var = sb("mean_var", [T, NT, 2])
        rstd = sb("rstd", [T, NT])
        mv_flat = mv[:, :, :].rearrange("p t d -> p (t d)")

        def small(at, *shape):
            size = 1
            for s in shape:
                size *= s
            names = "abc"[:len(shape)]
            return mv_flat[:, at:at + size].rearrange(
                f"p ({' '.join(names)}) -> p {' '.join(names)}", **dict(zip(names, shape)))

        logits_T = mv_flat[0:E, 0:S]
        logits = small(S, NT, E)
        top = small(S + 24, NT, 8)
        top_no = small(S + 48, NT, 8).bitcast(U32)
        top_nof = small(S + 72, NT, 2)
        route = small(S + 80, NT, 4)
        gates = small(S + 96, 2, NT, E)

        def bank(name, shape=(128, 512)):
            return ctx.enter_context(nc.psum_tensor(name, list(shape), F32))

        A = [bank("bank_a0"), bank("bank_a1")]
        SC = [bank(f"bank_s{i}") for i in range(3)]
        TP = [bank("bank_t0"), bank("bank_t1")]
        OB = bank("bank_o")

        staged = [sem(f"staged{i}") for i in range(STAGES)]
        w_hi_done, w_lo_done = sem("w_hi_done"), sem("w_lo_done")
        const_in, const_made, const_ready = sem("const_in"), sem("const_made"), sem("const_ready")
        CONSTS = 16 * (12 + KC)
        entry_in = [sem(f"entry_in{i}") for i in range(3)]
        stored = [sem(f"stored{i}") for i in range(3)]
        gated = sem("gated")
        normed = [sem(f"normed{i}") for i in range(3)]
        stats = [sem(f"stats{i}") for i in range(3)]
        rooted = [sem(f"rooted{i}") for i in range(3)]
        chains = [sem(f"vector_chain{i}") for i in range(3)]

        AHEAD = [{13: ("x0", "x1"), 14: ("v0", "v2"), 15: ("v4",), 16: ("mq0", "mk0"), 17: ("mq1", "mk1"),
                  19: ("mv0", "mv1", "mv2"), "a": ("v1",), "b": ("v3", "v5"), "c": ("q0", "k0"), "d": ("q1",),
                  "e": ("k1",)},
                 {13: ("x0", "x1"), 14: ("v0",), 15: ("v2", "q0"), 16: ("v4", "k0"), 17: ("q1",),
                  "a": ("v1",), "b": ("v3", "v5"), "c": ("k1",)}]
        early = [[name for names in ahead.values() for name in names] for ahead in AHEAD]
        heads_a = [f"{c}{m}" for m in range(2, HP) for c in "qk"]
        wo_a = [f"wo{t}" for t in range(NT)]
        A_ORDER = [heads_a[:MEMORY_OUT_AT] + ["mo0", "mo1", "mo2"] + heads_a[MEMORY_OUT_AT:] +
                   early[0][:-6] + wo_a + ["v3", "v5", "q0", "k0", "q1",
                   "g0", "g1", "g2", "k1"],
                   heads_a + early[1] + wo_a,
                   ["x0", "x1", "lg", "h0_0", "h0_1", "lt"] + [f"h{e}_{c}" for e in range(1, E) for c in range(EC)]]
        qk = [f"{c}{m}" for m in range(HP) for c in "qk"]
        HI_ORDER = [["x0", "x1", "mq0", "mk0", "mq1", "mk1"] + qk, ["x0", "x1"] + qk, ["x0", "x1"]]
        CAT_ORDER = ["c2", "c3", "c0", "c1"]
        a_ring = [Ring(sem, f"a{i}_", 2, A_ORDER[i], (early + [()])[i]) for i in range(3)]
        hi_done = [sem(f"hi_done{i}") for i in range(3)]
        cat_hi = sem("cat_hi")
        UNITS = [NT + H, NT * H]
        s_ring = [Ring(sem, f"s{i}_", 3, UNITS[i]) for i in range(2)]
        t_ring = [Ring(sem, "t0_", 2, list(range(UNITS[0])) + CAT_ORDER), Ring(sem, "t1_", 2, UNITS[1])]
        p_ring = [Ring(sem, f"p{i}_", PRING, H + 1 - i) for i in range(2)]
        maxed = [sem(f"maxed{i}") for i in range(2)]
        inverted = [sem(f"inverted{i}") for i in range(2)]
        pv_done = [sem(f"pv_done{i}") for i in range(2)]
        o_hi_done = sem("o_hi_done")
        o_lo_done = [sem(f"o_lo_done{i}") for i in range(2)]
        gate_tanh = sem("gate_tanh")
        gate_ready = sem("gate_ready")
        differed = sem("differed")
        kept = sem("kept")
        gelu_done, gelu_hi = sem("gelu_done"), sem("gelu_hi")
        gelu_lo = [sem("gelu_lo_gpsimd"), sem("gelu_lo_vector")]
        o_banks = Ring(sem, "expert_out", 6, NT * E)
        squared, hidden_hi, hidden_lo = sem("squared"), sem("hidden_hi"), sem("hidden_lo")
        margin_ready, margin_exp = sem("margin_ready"), sem("margin_exp")

        passed = {nc.vector: sem("vector_passed"), nc.gpsimd: sem("gpsimd_passed"), nc.tensor: sem("tensor_passed"),
                  nc.sync: sem("sync_passed")}

        block = ctx.enter_context(nc.Block())

        def plain(eng):
            eng.sem_inc(passed[eng], 1)

        def parts_of(phase):
            for i, (_, parts) in enumerate(pieces[phase]):
                p, at = first_piece[phase] + i, 0
                for cols, scale in parts:
                    yield (p, stage[:, p % STAGES, at:at + cols], slice(PIECE * i + at, PIECE * i + at + cols), scale,
                           at + cols == sum(c for c, _ in parts))
                    at += cols

        PARTS = [sum(len(parts) for _, parts in phase) for phase in pieces]

        def s_use(ph, h, t=0):
            return h + NT if ph == 0 else NT * h + t

        def p_use(ph, h):
            return h + 1 - ph

        def row_of(ph, h, t):
            return (WIN[t][0], WIN[t][2] * T) if ph == 0 else (t * S, S)

        LEAD_IN = -1
        FIRST = 0
        AHEAD_WEIGHTS = [{"v0": 2, "mq0": 3, "mv0": 8}, {"v0": EARLY_PIECES}]
        SPLIT_AT, HEAD_SPLITS = 13, [0, 1]
        HEAD_0_BEFORE = ["k1", "q1"]
        FIRST_SCORES_AT = 17
        START_SPLITS = {"x1": (0, 3), "v0": (3, 4), "v2": (4, 5), "v4": (5, 6), "mk0": (6, 7), "mk1": (7, 8),
                        "mv0": (8, 9), "mv1": (9, 10), "mv2": (10, 11)}
        LATE_SPLITS = {"v1": (6, 7), "v3": (7, 8)}
        MEMORY_AT = 18

        def qk_at(h):
            return [] if not 1 <= h <= H - 4 else [("k", h // 2 + 1) if h % 2 == 0 else ("q", (h + 3) // 2)]

        def low_at(ph, h):
            at_once = {H - 4, MEMORY_OUT_AT} if ph == 0 else {H - 4}
            return (qk_at(h - 1) if h - 1 not in at_once else []) + (qk_at(h) if h in at_once else [])

        def scalar_copies(ph, h, n):
            return n % 2 == 1 if ph == 0 else n == NT * h + SCALAR_TILE

        def turned(ph, h, tiles):
            return [NT * h + kt for kt in tiles] if ph else [NT + h] if 0 in tiles else []

        @block.sync
        def _(sp):
            def load_pieces(phase, first=0, last=None):
                for p in range(first_piece[phase], first_piece[phase + 1])[first:last]:
                    if p >= STAGES:
                        sp.wait_ge(w_lo_done, p - STAGES + 1)
                    at = 0
                    for src, n, cols in flat[p][0]:
                        sp.dma_start(stage[:, p % STAGES, at:at + n * cols].rearrange("p (k n) -> p k n", k=n), src)\
                          .then_inc(staged[p % STAGES], 16)
                        at += n * cols

            def load_x(b):
                sp.dma_start(h_in[PM:T, 0, :], x[b, 0:T - PM, :]).then_inc(entry_in[0], 16)
                sp.dma_start(h_in[:, 1:NT, :], x[b, T - PM:S0, :].rearrange("(t p) d -> p t d", p=T))\
                  .then_inc(entry_in[0], 16)

            def store(phase, dst, b):
                if phase == 0:
                    sp.wait_ge(gated, b + (1 + PRIMED))
                if phase == 1:
                    a_ring[1].wait_all_freed(sp, b, wo_a)
                if phase == 2:
                    o_banks.wait_all_freed(sp, b, [NT * (E - 1) + t for t in range(NT)])
                sp.dma_start(dst[b].rearrange("(t p) d -> p t d", p=T), tmp[:, :, :]).then_inc(stored[phase], 16)

            def load_h(phase, src, b):
                sp.dma_start(h_in[:, :, :], src[b].rearrange("(t p) d -> p t d", p=T)).then_inc(entry_in[phase], 16)

            sp.dma_start(h_in[0:PM, 0, :], w["L0_tok_persistent_memory"]).then_inc(entry_in[0], 16)
            load_x(0)
            load_pieces(0, 0, 3)
            for i, name in enumerate(("bq", "bk", "bv")):
                sp.dma_start(col_bias[:, i, :], w["L0_tok_" + name].rearrange("(m p) -> p m", p=128),
                             allow_slow_non_contiguous=True).then_inc(const_in, 16)
            for i, name in enumerate(("mbq", "mbk")):
                sp.dma_start(mem_bias[:, i, :], w["L0_tok_" + name].rearrange("(m p) -> p m", p=128),
                             allow_slow_non_contiguous=True).then_inc(const_in, 16)
            for i, name in enumerate(("bo", "mbv", "g1_w", "g1_b", "g2_w", "g2_b", "gate_b")):
                sp.dma_start(rows_bc[:, i, :], w["L0_tok_" + name].partition_broadcast(T)).then_inc(const_in, 16)
            for k in range(KC):
                sp.dma_start(router[:, k, :], w["L0_ffn_router_w"][:, 128 * k:128 * k + 128].rearrange("e p -> p e"),
                             allow_slow_non_contiguous=True).then_inc(const_in, 16)
            load_pieces(0, 3)
            load_pieces(1)
            with sp.Fori(0, B - 1) as b:
                for name in ("x0", "x1"):
                    a_ring[0].wait_freed(sp, b, name)
                    plain(sp)
                load_x(b + 1)
                store(0, h_tok, b)
            a_ring[0].wait_all_freed(sp, B - 1, ("x0", "x1"))
            sp.wait_ge(stored[0], 16 + PRIMED)
            load_h(1, h_tok, 0)
            store(0, h_tok, B - 1)
            sp.wait_ge(stored[0], 16 * B + PRIMED)
            load_pieces(2)
            with sp.Fori(0, B - 1) as b:
                sp.wait_ge(kept, b + 1)
                load_h(1, h_tok, b + 1)
                store(1, h_attn, b)
            sp.wait_ge(kept, B)
            sp.wait_ge(stored[1], 16 + PRIMED)
            load_h(2, h_attn, 0)
            store(1, h_attn, B - 1)
            sp.wait_ge(stored[1], 16 * B + PRIMED)
            with sp.Fori(0, B - 1) as b:
                o_banks.wait_all_freed(sp, b, range(NT))
                load_h(2, h_attn, b + 1)
                store(2, out, b)
            store(2, out, B - 1)
            sp.wait_ge(stored[2], 16 * B + PRIMED)

        @block.gpsimd
        def _(pool):
            n = 0

            def made(ins):
                nonlocal n
                n += 1
                ins.then_inc(const_made, 1)
                pool.wait_ge(const_made, n)

            made(pool.memset(ident[:, :], 0.0))
            made(pool.affine_select(out=ident[:, :], in_=ident[:, :], compare_op=ALU.not_equal, fill=1.0, base=0,
                                    pattern=[[-1, T]], channel_multiplier=1))
            made(pool.tensor_copy(ident_bf[:, :], ident[:, :]))
            made(pool.memset(tmp[:, :, :], 0.0))
            for t in range(NT):
                c, n_kt = WIN[t][0], WIN[t][2]
                off = (t - WIN[t][1]) * T
                m = tmp[:, :, :].rearrange("p t d -> p (t d)")[:, c:c + n_kt * T]
                made(pool.affine_select(out=m, in_=m, compare_op=ALU.is_ge, fill=MASKED, base=off,
                                        pattern=[[-1, n_kt * T]], channel_multiplier=1))
                made(pool.affine_select(out=m, in_=m, compare_op=ALU.is_ge, fill=MASKED, base=WINDOW - off,
                                        pattern=[[1, n_kt * T]], channel_multiplier=-1))
            made(pool.tensor_copy(mask_bf[:, :], tmp[:, :, :].rearrange("p t d -> p (t d)")[:, 0:5 * T]))
            made(pool.iota(expert_no_i[:, :], pattern=[[1, E]], base=0, channel_multiplier=0))
            made(pool.tensor_copy(expert_no[:, :], expert_no_i[:, :]))
            made(pool.memset(neg_half[:, :], -0.5))
            pool.wait_ge(const_in, CONSTS)
            made(pool.tensor_scalar(col_bias[:, 0, :], col_bias[:, 0, :], float(HD) ** -0.5, 1.0, ALU.mult, ALU.mult))
            pool.tensor_scalar(mem_bias[:, 0, :], mem_bias[:, 0, :], float(D) ** -0.5, 1.0, ALU.mult, ALU.mult)\
                .then_inc(const_ready, 1)

            def root(phase, count):
                pool.wait_ge(stats[phase], count)
                pool.tensor_tensor(rstd[:, :], rstd[:, :], neg_half[:, :], ALU.pow).then_inc(rooted[phase], 1)

            def scale_head(ph, b, h):
                pool.wait_ge(inverted[ph], b * H + h + 1)
                plain(pool)
                for t in range(NT):
                    c, cols = row_of(ph, h, t)
                    row = probs[:, p_use(ph, h) % PRING, c:c + cols]
                    ins = pool.tensor_scalar(row, row, recip[:, h, t:t + 1], 1.0, ALU.mult, ALU.mult)
                p_ring[ph].filled(ins, p_use(ph, h))

            def entry(ph, b, n):
                for h in range(1 - ph, H):
                    scale_head(ph, b, h)
                    if ph == 0 and h == MEMORY_OUT_AT:
                        root(0, 2 * b + 1)
                    if h == NORM_AT:
                        if n is None:
                            root(ph + 1, 1)
                        elif ph == 1:
                            root(1, n + 1)
                if ph == 0:
                    root(0, 2 * b + 2)
                    t_ring[0].wait_full(pool, b, "c1")
                    pool.tensor_tensor(work[:, :, :], work[:, :, :], keep[:, :, :], ALU.subtract).then_inc(differed, 1)
                    if n is not None:
                        scale_head(0, n, 0)
                    pool.wait_ge(gate_ready, b + 1)
                    pool.wait_ge(differed, 2 * b + 1)
                    pool.tensor_tensor(tmp[:, :, :], tmp[:, :, :], work[:, :, :], ALU.mult).then_inc(differed, 1)
                    pool.wait_ge(differed, 2 * b + 2)
                    pool.tensor_tensor(tmp[:, :, :], tmp[:, :, :], keep[:, :, :], ALU.add).then_inc(gated, 1)
                else:
                    for g in (0, 2):
                        pool.wait_ge(gelu_hi, b * (HP // 2) + (g + 1))
                        pool.tensor_tensor(oT_lo[:, 2 * g:2 * g + 2, :], o_raw[:, 2 * g:2 * g + 2, :],
                                           oT_hi[:, 2 * g:2 * g + 2, :].bitcast(F32), ALU.subtract)\
                            .then_inc(gelu_lo[0], 1)

            def lo_hidden(b, e):
                for i in range(EC * e, EC * e + EC):
                    pool.wait_ge(hidden_hi, b * (E * EC) + (i + 1))
                    slot = i % (4 * EC)
                    pool.tensor_tensor(oT_lo[:, slot, :], pT[:, i % 4, 0:S], oT_hi[:, slot, :].bitcast(F32),
                                       ALU.subtract).then_inc(hidden_lo, 1)

            scale_head(0, FIRST, 0)
            for phase in range(2):
                with pool.Fori(0, B - 1) as b:
                    entry(phase, b, b + 1)
                entry(phase, B - 1, None)

            def experts(b, n):
                for e in range(2, E):
                    lo_hidden(b, e)
                    if e == EXPERT_NORM_AT and n is not None:
                        root(2, n + 1)
                if n is not None:
                    lo_hidden(n, 0)
                    lo_hidden(n, 1)

            lo_hidden(0, 0)
            lo_hidden(0, 1)
            with pool.Fori(0, B - 1) as b:
                experts(b, b + 1)
            experts(B - 1, None)

        @block.tensor
        def _(pe):
            def product(dst, ops, start=True, stop=True, onto=False):
                n = 3 * len(ops)
                i = 0
                for (l_hi, l_lo), (r_hi, r_lo) in ops:
                    for l, r in ((l_hi, r_hi), (l_hi, r_lo), (l_lo, r_hi)):
                        ins = pe.matmul(dst, l, r, start=start and i == 0, stop=stop and i == n - 1,
                                        skip_group_check=onto)
                        i += 1
                return ins

            def wcols(at, n):
                return w_hi[:, at:at + n], w_lo[:, at:at + n]

            def xcols(k, t=None):
                c = slice(0, S) if t is None else slice(t * T, t * T + T)
                return xT_hi[:, k, c], xT_lo[:, k, c]

            for phase in range(3):
                a, order = a_ring[phase], A_ORDER[phase]
                LAG = LAGS[phase] if phase < 2 else 0
                primed = [s_ring[phase], t_ring[phase]] if phase < 2 else [a, o_banks]
                for started in ([s for ring in primed for s in ring.free] + [stored[phase]] + o_lo_done[phase:phase + 1]
                                + ([gated] if phase == 0 else [])):
                    pe.sem_inc(started, PRIMED)

                def pass_over(until):
                    passed_names = order[cursor[0]:until]
                    cursor[0] = until
                    for slot in range(a.size):
                        names = [name for name in passed_names if a.slot(name) == slot]
                        if names:
                            if step[0] is not LEAD_IN or order.index(names[0]) >= a.size:
                                a.wait_free(pe, step[0] + (names[0] in a.early), names[0])
                            pe.sem_inc(a.full[slot], len(names))
                            pe.sem_inc(a.free[slot], len(names))

                def fill(b, name, emit):
                    cursor[0] %= len(order)
                    if order[cursor[0]] != name:
                        pass_over(order.index(name))
                    cursor[0] += 1
                    a.wait_free(pe, b, name)
                    a.filled(emit(A[a.slot(name)]), name)

                def ready(b, *names):
                    a.wait_all_freed(pe, b, names)

                def turn_branch(b, name, src, k):
                    t_ring[0].wait_free(pe, b, name)
                    for t in range(NT):
                        ins = pe.transpose(TP[t_ring[0].slot(name)][:, t * T:t * T + T],
                                           src[:, t, 128 * k:128 * k + 128], ident[:, :])
                    t_ring[0].filled(ins, name)

                def turn_in(b, name, src, k):
                    def emit(bank):
                        for t in range(NT):
                            ins = pe.transpose(bank[:, t * T:t * T + T], src[:, t, 128 * k:128 * k + 128], ident[:, :])
                        return ins
                    fill(b, name, emit)

                def chunk(b, name, at, width, m):
                    fill(b, name, lambda bank: product(bank[:, 0:S], [
                        (wcols(at + k * width + 128 * m, 128), xcols(k)) for k in range(KC)]))

                def project(b, c, m):
                    chunk(b, f"{c}{m}", {"q": WQ, "k": WK}[c][phase], INNER, m)

                def natural(b, name, at, width, cols, t):
                    fill(b, name, lambda bank: product(bank[0:T, 0:cols.stop - cols.start], [
                        (xcols(k, t), wcols(at + k * width + cols.start, cols.stop - cols.start)) for k in range(KC)]))

                def ahead(b, name):
                    kind, i = name[:-1], int(name[-1])
                    if name in AHEAD_WEIGHTS[phase] and b is FIRST:
                        pe.wait_ge(w_lo_done, first_piece[phase] + AHEAD_WEIGHTS[phase][name])
                    if name == "x0":
                        if phase == 0:
                            pe.wait_ge(entry_in[0], b * 32 + 48)
                        else:
                            pe.wait_ge(normed[phase], b + 1)
                    if name == "v0":
                        ready(b, "x0", "x1")
                    if kind == "x":
                        turn_in(b, name, h_in if phase == 0 else mv, i)
                    elif kind == "v":
                        natural(b, name, WV[phase], INNER, slice(512 * (i % 2), 512 * (i % 2) + 512), i // 2)
                    elif kind == "mv":
                        natural(b, name, WMV, D, slice(0, D), i)
                    elif kind in ("mq", "mk"):
                        chunk(b, name, WMQ if kind == "mq" else WMK, D, i)
                    else:
                        project(b, kind, i)

                def scores(b, h):
                    s, half, m = s_ring[phase], 64 * (h % 2), h // 2
                    rows = slice(half, half + HD)
                    ready(b, f"q{m}", f"k{m}")
                    if phase == 0:
                        n = s_use(0, h)
                        s.wait_free(pe, b, n)
                        bank = SC[n % 3]
                        pe.matmul(bank[0:T, 0:5 * T], ident_bf[:, :], mask_bf[:, :], start=True, stop=True)
                        for t in range(NT):
                            c, kt, n_kt = WIN[t]
                            keys, mine = slice(kt * T, (kt + n_kt) * T), slice(t * T, t * T + T)
                            ins = product(bank[0:T, c:c + n_kt * T], [
                                ((q_hi[rows, m % 2, mine], q_lo[rows, m % 2, mine]),
                                 (k_hi[rows, m % 2, keys], k_lo[rows, m % 2, keys]))], start=False, onto=True)
                        s.filled(ins, n)
                        return
                    for t in range(NT):
                        n, mine = s_use(1, h, t), slice(t * T, t * T + T)
                        s.wait_free(pe, b, n)
                        s.filled(product(SC[n % 3][0:T, 0:S], [
                            ((q_hi[rows, m % 2, mine], q_lo[rows, m % 2, mine]),
                             (k_hi[rows, m % 2, :], k_lo[rows, m % 2, :]))]), n)

                def turn_square(b, p_n, t_first, tiles=range(NT)):
                    if 0 in tiles:
                        p_ring[phase].wait_full(pe, b, p_n)
                    for kt in tiles:
                        n = t_first + kt
                        t_ring[phase].wait_free(pe, b, n)
                        for t in range(NT):
                            ins = pe.transpose(TP[n % 2][0:T, t * T:t * T + T],
                                               probs[:, p_n % PRING, t * S + kt * T:t * S + kt * T + T], ident[:, :])
                        t_ring[phase].filled(ins, n)

                def turn_probs(b, h, tiles):
                    if phase == 1:
                        turn_square(b, p_use(1, h), NT * h, tiles)
                        return
                    if 0 not in tiles:
                        return
                    n = NT + h
                    p_ring[0].wait_full(pe, b, p_use(0, h))
                    t_ring[0].wait_free(pe, b, n)
                    for kt in range(NT):
                        c, qt, n_qt = WINT[kt]
                        for i in range(n_qt):
                            src = WIN[qt + i][0] + (kt - WIN[qt + i][1]) * T
                            ins = pe.transpose(TP[n % 2][0:T, c + i * T:c + i * T + T],
                                               probs[:, p_use(0, h) % PRING, src:src + T], ident[:, :])
                    t_ring[0].filled(ins, n)

                def attend(b, m):
                    t_ring[phase].wait_all_freed(pe, b, [NT + 2 * m, NT + 2 * m + 1] if phase == 0
                                                 else range(2 * m * NT, (2 * m + 2) * NT))
                    pe.wait_ge(o_lo_done[phase], b * HP + (m + PRIMED))
                    for kt in range(NT):
                        c, qt, n_qt = WINT[kt] if phase == 0 else (kt * S, 0, NT)
                        for h in (2 * m, 2 * m + 1):
                            half = 64 * (h % 2)
                            ins = pe.matmul(OB[half:half + HD, qt * T:(qt + n_qt) * T],
                                            v[:, kt, h * HD:h * HD + HD], pT[0:T, h % 4, c:c + n_qt * T],
                                            start=kt == 0, stop=kt == NT - 1, skip_group_check=True)
                    ins.then_inc(pv_done[phase], 1)

                def project_out(b):
                    for t in range(NT):
                        mine = slice(t * T, t * T + T)

                        def emit(bank):
                            for m in range(HP):
                                if phase == 1 and t == 0 and m % 2 == 0:
                                    g = m // 2
                                    pe.wait_ge(gelu_lo[g % 2], 2 * b + (g // 2 + 1))
                                ins = product(bank[0:T, 0:D], [
                                    ((oT_hi[:, m, mine], oT_lo[:, m, mine]), wcols(WO[phase] + m * D, D))],
                                    start=m == 0, stop=m == HP - 1)
                            return ins
                        fill(b, f"wo{t}", emit)

                def memory_scores(b):
                    ready(b, "mq0", "mk0", "mq1", "mk1")
                    for t in range(NT):
                        mine = slice(t * T, t * T + T)
                        s_ring[0].wait_free(pe, b, t)
                        s_ring[0].filled(product(SC[t][0:T, 0:S], [
                            ((q_hi[:, c, mine], q_lo[:, c, mine]), (k_hi[:, c, :], k_lo[:, c, :]))
                            for c in range(KC)]), t)

                def memory_attend(b):
                    t_ring[0].wait_all_freed(pe, b, range(NT))
                    ready(b, "mv2")
                    for t in range(NT):
                        def emit(bank):
                            for kt in range(NT):
                                ins = pe.matmul(bank[0:T, 0:D], pT[0:T, 2, kt * S + t * T:kt * S + t * T + T],
                                                mv[:, kt, :], start=kt == 0, stop=kt == NT - 1)
                            return ins
                        fill(b, f"mo{t}", emit)

                def entry(b, n):
                    def between(at):
                        if n is not None:
                            for name in AHEAD[phase].get(at, ()):
                                ahead(n, name)

                    step[0] = b
                    for h in range(1, H + LAG + 1):
                        if LAG <= h < H + LAG:
                            turn_probs(b, h - LAG, (0, 1))
                        if 1 <= h < H:
                            scores(b, h)
                        if LAG <= h < H + LAG:
                            turn_probs(b, h - LAG, (2,))
                        for c, m in qk_at(h):
                            project(b, c, m)
                        if phase == 0 and h == 1:
                            turn_square(b, 0, 0, (2,))
                        if phase == 0 and h == MEMORY_OUT_AT:
                            memory_attend(b)
                        if phase == 1 and h == FIRST_SCORES_AT and n is not None:
                            scores(n, 0)
                        between(h)
                        if phase == 0 and h == MEMORY_AT and n is not None:
                            memory_scores(n)
                        if (h - LAG) % 2 == 0 and h > LAG:
                            attend(b, (h - LAG) // 2 - 1)
                    between("a")
                    if phase == 0:
                        pe.wait_ge(o_lo_done[0], b * HP + (HP + PRIMED))
                        project_out(b)
                        between("b")
                        pe.wait_ge(normed[0], 2 * b + 1)
                        turn_branch(b, "c2", keep, 0)
                        turn_branch(b, "c3", keep, 1)
                        between("c")
                        pe.wait_ge(normed[0], 2 * b + 2)
                        turn_branch(b, "c0", work, 0)
                        turn_branch(b, "c1", work, 1)
                        between("d")
                        if n is not None:
                            scores(n, 0)
                        t_ring[0].wait_all_freed(pe, b, CAT_ORDER)
                        for t in range(NT):
                            mine = slice(t * T, t * T + T)
                            fill(b, f"g{t}", lambda bank: product(bank[0:T, 0:D], [
                                ((oT_hi[:, c, mine], oT_lo[:, c, mine]), wcols(WG[c // KC] + c % KC * D, D))
                                for c in range(2 * KC)]))
                        between("e")
                        if n is not None:
                            turn_square(n, 0, 0, (0, 1))
                    else:
                        between("b")
                        between("c")
                        project_out(b)

                if phase == 0:
                    pe.wait_ge(const_made, 2)
                else:
                    a_ring[phase - 1].wait_all_freed(pe, B - 1, ("g1", "g2") if phase == 1 else ("wo1", "wo2"))
                step, cursor = [LEAD_IN], [0]

                if phase < 2:
                    for name in early[phase]:
                        if name == "mv0":
                            memory_scores(FIRST)
                        if name == HEAD_0_BEFORE[phase]:
                            if phase == 0:
                                pe.wait_ge(const_made, CONST_STEPS)
                            scores(FIRST, 0)
                        ahead(FIRST, name)
                    if phase == 0:
                        turn_square(FIRST, 0, 0, (0, 1))
                    pass_over(len(order))
                    pe.wait_ge(w_lo_done, first_piece[phase + 1])
                    with pe.Fori(0, B - 1) as b:
                        entry(b, b + 1)
                    entry(B - 1, None)
                    continue

                def hidden(b, e):
                    for c in range(EC):
                        chunk(b, f"h{e}_{c}", W1 + e * KC * DE, DE, c)

                def expert_out(b, e):
                    pe.wait_ge(hidden_lo, b * (E * EC) + (e + 1) * EC)
                    for t in range(NT):
                        n, mine = NT * e + t, slice(t * T, t * T + T)
                        o_banks.wait_free(pe, b, n)
                        o_banks.filled(product((SC + TP + [OB])[n % 6][0:T, 0:D], [
                            ((oT_hi[:, EC * (e % 4) + c, mine], oT_lo[:, EC * (e % 4) + c, mine]),
                             wcols(W2 + (e * EC + c) * D, D)) for c in range(EC)]), n)

                def inputs(b):
                    pe.wait_ge(normed[2], b + 1)
                    turn_in(b, "x0", work, 0)
                    turn_in(b, "x1", work, 1)

                def route_and_first(b):
                    ready(b, "x0", "x1")
                    fill(b, "lg", lambda bank: product(bank[0:E, 0:S], [
                        ((router_hi[:, k, :], router_lo[:, k, :]), xcols(k)) for k in range(KC)]))
                    hidden(b, 0)

                def logits_and_second(b):
                    ready(b, "lg")

                    def emit(bank):
                        plain(pe)
                        for t in range(NT):
                            ins = pe.transpose(bank[0:T, t * E:t * E + E], logits_T[:, t * T:t * T + T], ident[0:E, 0:E])
                        return ins
                    fill(b, "lt", emit)
                    hidden(b, 1)

                def experts(b, n):
                    for e in range(2, E):
                        hidden(b, e)
                        expert_out(b, e - 2)
                    if n is not None:
                        inputs(n)
                    expert_out(b, E - 2)
                    if n is not None:
                        route_and_first(n)
                    expert_out(b, E - 1)
                    if n is not None:
                        logits_and_second(n)

                inputs(FIRST)
                pe.wait_ge(w_lo_done, first_piece[2] + 1 + EARLY_PIECES)
                route_and_first(FIRST)
                logits_and_second(FIRST)
                pe.wait_ge(w_lo_done, first_piece[3] + 1)
                with pe.Fori(0, B - 1) as b:
                    experts(b, b + 1)
                experts(B - 1, None)

        @block.scalar
        def _(act):
            def split(phase, first, last):
                for p, src, cols, scale, _ in parts_of(phase):
                    if first <= p - first_piece[phase] < last:
                        act.wait_ge(staged[p % STAGES],
                                    16 * sum(len(flat[n][0]) for n in range(p % STAGES, p + 1, STAGES)))
                        act.activation(w_hi[:, cols], src, ACT.Copy, scale=scale).then_inc(w_hi_done, 1)

            for phase in range(3):
                a, order = a_ring[phase], A_ORDER[phase]
                LAG = LAGS[phase] if phase < 2 else 0

                def hi(b, name, dst, bias=None):
                    if name[0] == "c":
                        t_ring[0].wait_full(act, b, name)
                        act.activation(dst, TP[t_ring[0].slot(name)][:, 0:S], ACT.Copy).then_inc(cat_hi, 1)
                        return
                    a.wait_full(act, b, name)
                    if bias is None:
                        ins = act.activation(dst, A[a.slot(name)][:, 0:S], ACT.Copy)
                    else:
                        ins = act.activation(dst, A[a.slot(name)][:, 0:S], ACT.Identity, bias=bias)
                    ins.then_inc(hi_done[phase], 1)

                def copy_out(b, name, dst, cols):
                    a.wait_full(act, b, name)
                    a.freed(act.activation(dst, A[a.slot(name)][0:dst.shape[0], 0:cols], ACT.Copy), name)

                def hi_qk(b, c, m):
                    hi(b, f"{c}{m}", {"q": q_hi, "k": k_hi}[c][:, m % 2, :],
                       col_bias[:, "qk".index(c), m:m + 1] if phase == 0 else None)

                def ahead(b, name):
                    kind, i = name[:-1], int(name[-1])
                    if kind == "x":
                        hi(b, name, xT_hi[:, i, :])
                    elif kind == "v":
                        copy_out(b, name, v[:, i // 2, 512 * (i % 2):512 * (i % 2) + 512], 512)
                    elif kind == "mv":
                        copy_out(b, name, mv[:, i, :], D)
                    elif kind in ("mq", "mk"):
                        hi(b, name, {"mq": q_hi, "mk": k_hi}[kind][:, i, :],
                           mem_bias[:, ("mq", "mk").index(kind), i:i + 1])
                    else:
                        hi_qk(b, kind, i)

                def turned_memory(b):
                    t_ring[0].wait_full(act, b, 1)
                    t_ring[0].freed(act.activation(pT[0:T, 2, S:2 * S], TP[1][0:T, 0:S], ACT.Copy), 1)

                def exp_memory(b):
                    for t in range(NT):
                        act.wait_ge(maxed[0], b * UNITS[0] + (t + 1))
                        ins = act.activation(probs[:, 0, t * S:t * S + S], SC[t][0:T, 0:S], ACT.Exp,
                                             bias=neg_max[:, H, t:t + 1], accum_out=sums[:, H, t:t + 1])
                        s_ring[0].freed(ins, t)

                def exp_head(b, h):
                    p_n = p_use(phase, h)
                    if phase == 1 and LAG == PRING and h >= PRING:
                        t_ring[1].wait_full(act, b, NT * (h - PRING) + NT - 1)
                    for t in range(NT):
                        n = s_use(phase, h, t)
                        c, cols = row_of(phase, h, t)
                        if phase == 1 or t == 0:
                            act.wait_ge(maxed[phase], b * UNITS[phase] + (n + 1))
                        at = c if phase == 0 else 0
                        ins = act.activation(probs[:, p_n % PRING, c:c + cols], SC[n % 3][0:T, at:at + cols], ACT.Exp,
                                             bias=neg_max[:, h, t:t + 1], accum_out=sums[:, h, t:t + 1])
                        if phase == 1 or t == NT - 1:
                            s_ring[phase].freed(ins, n)

                def copy_turned(b, h, tiles):
                    for n in turned(phase, h, tiles):
                        if scalar_copies(phase, h, n):
                            t_ring[phase].wait_full(act, b, n)
                            c, cols = (0, 5 * T) if phase == 0 else ((n - NT * h) * S, S)
                            t_ring[phase].freed(act.activation(pT[0:T, h % 4, c:c + cols], TP[n % 2][0:T, 0:cols],
                                                               ACT.Copy), n)

                def hi_out(b, m):
                    act.wait_ge(pv_done[phase], b * HP + (m + 1))
                    if phase == 0:
                        act.activation(oT_hi[:, m, :], OB[:, 0:S], ACT.Identity, bias=col_bias[:, 2, m:m + 1])\
                           .then_inc(o_hi_done, 1)
                    else:
                        act.activation(o_raw[:, m, :], OB[:, 0:S], ACT.Copy).then_inc(o_lo_done[1], 1)

                def activate(b, g):
                    if g in (0, HP // 2 - 1):
                        act.wait_ge(o_lo_done[1], b * HP + ((HP - 2 if g == 0 else HP) + PRIMED))
                    act.activation(o_raw[:, 2 * g:2 * g + 2, :], o_raw[:, 2 * g:2 * g + 2, :], ACT.Gelu)\
                       .then_inc(gelu_done, 1)

                def entry(b, n):
                    def between(at):
                        if n is not None:
                            for name in AHEAD[phase].get(at, ()):
                                ahead(n, name)

                    for h in range(1, H + LAG + 1):
                        if LAG <= h < H + LAG:
                            copy_turned(b, h - LAG, (0, 1))
                        if h < H:
                            exp_head(b, h)
                        if LAG <= h < H + LAG:
                            copy_turned(b, h - LAG, (2,))
                        for c, m in qk_at(h):
                            hi_qk(b, c, m)
                        if phase == 1 and h == FIRST_SCORES_AT and n is not None:
                            exp_head(n, 0)
                        between(h)
                        if phase == 0 and h == MEMORY_AT and n is not None:
                            exp_memory(n)
                        if n is None and SPLIT_AT <= h < SPLIT_AT + HEAD_SPLITS[phase]:
                            if phase == 1 and h == SPLIT_AT:
                                act.activation(router_hi[:, :, :], router[:, :, :], ACT.Copy).then_inc(w_hi_done, 1)
                            split(phase + 1, h - SPLIT_AT, h - SPLIT_AT + 1)
                        if (h - LAG) % 2 == 0 and h > LAG:
                            hi_out(b, (h - LAG) // 2 - 1)
                        if phase == 1 and h == H + 1:
                            for g in range(HP // 2 - 1):
                                activate(b, g)
                    between("a")
                    if phase:
                        activate(b, HP // 2 - 1)
                    if n is None:
                        split(phase + 1, HEAD_SPLITS[phase], EARLY_PIECES)
                    if phase == 0:
                        between("b")
                        hi(b, "c2", oT_hi[:, 2, :])
                        hi(b, "c3", oT_hi[:, 3, :])
                        between("c")
                        hi(b, "c0", oT_hi[:, 0, :])
                        hi(b, "c1", oT_hi[:, 1, :])
                        between("d")
                        if n is not None:
                            exp_head(n, 0)
                        for t in range(NT):
                            a.wait_freed(act, b, f"g{t}")
                            act.activation(tmp[:, t, :], tmp[:, t, :], ACT.Tanh, scale=0.5).then_inc(gate_tanh, 1)
                        act.wait_ge(gate_tanh, NT * b + NT)
                        act.activation(tmp[:, :, :], tmp[:, :, :], ACT.Copy, scale=0.5, bias=0.5).then_inc(gate_ready, 1)
                        between("e")
                        if n is not None:
                            turned_memory(n)
                    else:
                        between("b")
                        between("c")

                if phase < 2:
                    for name in early[phase]:
                        if name == "mv0":
                            exp_memory(FIRST)
                        if name == HEAD_0_BEFORE[phase]:
                            exp_head(FIRST, 0)
                        if name == "mq0":
                            act.wait_ge(const_ready, 1)
                        ahead(FIRST, name)
                        if phase == 0 and name in START_SPLITS:
                            split(0, *START_SPLITS[name])
                        if phase == 1 and name in LATE_SPLITS:
                            split(1, *LATE_SPLITS[name])
                    if phase == 0:
                        turned_memory(FIRST)
                    with act.Fori(0, B - 1) as b:
                        entry(b, b + 1)
                    entry(B - 1, None)
                    continue

                def hi_hidden(b, e):
                    for i in range(EC * e, EC * e + EC):
                        n = f"h{e}_{i % EC}"
                        a.wait_full(act, b, n)
                        if i >= 4 or b is not FIRST:
                            act.wait_ge(squared, b * (E * EC) + (i - 3))
                        a.freed(act.activation(pT[:, i % 4, S:2 * S], A[a.slot(n)][:, 0:S], ACT.Relu), n)
                    for i in range(EC * e, EC * e + EC):
                        act.wait_ge(squared, b * (E * EC) + (i + 1))
                        act.activation(oT_hi[:, i % (4 * EC), :], pT[:, i % 4, 0:S], ACT.Copy).then_inc(hidden_hi, 1)

                def inputs(b):
                    hi(b, "x0", xT_hi[:, 0, :])
                    hi(b, "x1", xT_hi[:, 1, :])
                    if b is FIRST:
                        split(2, EARLY_PIECES, len(pieces[2]))
                    copy_out(b, "lg", logits_T[:, :], S)
                    hi_hidden(b, 0)

                def second(b):
                    hi_hidden(b, 1)
                    act.wait_ge(margin_ready, b + 1)
                    act.activation(route[:, :, 1], route[:, :, 0], ACT.Exp).then_inc(margin_exp, 1)

                def experts(b, n):
                    for e in range(2, E):
                        hi_hidden(b, e)
                    if n is not None:
                        inputs(n)
                        second(n)

                inputs(FIRST)
                second(FIRST)
                with act.Fori(0, B - 1) as b:
                    experts(b, b + 1)
                experts(B - 1, None)

        @block.vector
        def _(dve):
            lo_n = [0]

            def split(phase, first, last_piece):
                for p, src, cols, scale, last in parts_of(phase):
                    if not first <= p - first_piece[phase] < last_piece:
                        continue
                    lo_n[0] += 1
                    dve.wait_ge(w_hi_done, lo_n[0])
                    ins = dve.scalar_tensor_tensor(out=w_lo[:, cols], in0=src, scalar=scale,
                                                   in1=w_hi[:, cols].bitcast(F32), op0=ALU.mult, op1=ALU.subtract)
                    if last:
                        ins.then_inc(w_lo_done, 1)

            vector_chains = [Chain(chains[ph], dve, CHAIN_STEPS[ph]) for ph in range(3)]

            for phase in range(3):
                a, order = a_ring[phase], A_ORDER[phase]
                LAG = LAGS[phase] if phase < 2 else 0
                chain = vector_chains[phase]

                def lo(b, name, hi_ap, dst, bias=None):
                    if name[0] == "c":
                        dve.wait_ge(cat_hi, b * len(CAT_ORDER) + (CAT_ORDER.index(name) + 1))
                        t_ring[0].freed(dve.tensor_tensor(dst, TP[t_ring[0].slot(name)][:, 0:S], hi_ap.bitcast(F32),
                                                          ALU.subtract), name)
                        return
                    n = a.slot(name)
                    dve.wait_ge(hi_done[phase], b * len(HI_ORDER[phase]) + (HI_ORDER[phase].index(name) + 1))
                    if bias is None:
                        ins = dve.tensor_tensor(dst, A[n][:, 0:S], hi_ap.bitcast(F32), ALU.subtract)
                    else:
                        ins = dve.scalar_tensor_tensor(out=dst, in0=A[n][:, 0:S], scalar=bias,
                                                       in1=hi_ap.bitcast(F32), op0=ALU.add, op1=ALU.subtract)
                    a.freed(ins, name)

                def lo_qk(b, c, m):
                    h_ap, l_ap = {"q": (q_hi, q_lo), "k": (k_hi, k_lo)}[c]
                    lo(b, f"{c}{m}", h_ap[:, m % 2, :], l_ap[:, m % 2, :],
                       col_bias[:, "qk".index(c), m:m + 1] if phase == 0 else None)

                def max_head(b, h):
                    if phase == 0:
                        n = s_use(0, h)
                        s_ring[0].wait_full(dve, b, n)
                        dve.tensor_reduce(neg_max[:, h, 0:1], SC[n % 3][0:T, 0:T], AX.X, ALU.max, negate=True)
                        dve.tensor_reduce(neg_max[:, h, 1:NT],
                                          SC[n % 3][0:T, T:5 * T].rearrange("p (t n) -> p t n", t=2),
                                          AX.X, ALU.max, negate=True).then_inc(maxed[0], 1)
                        return
                    for t in range(NT):
                        n = s_use(1, h, t)
                        s_ring[1].wait_full(dve, b, n)
                        dve.tensor_reduce(neg_max[:, h, t:t + 1], SC[n % 3][0:T, 0:S], AX.X, ALU.max, negate=True)\
                           .then_inc(maxed[1], 1)

                def invert(b, h):
                    for t in range(NT):
                        if phase == 1 or t == NT - 1:
                            s_ring[phase].wait_freed(dve, b, s_use(phase, h, t))
                    dve.reciprocal(recip[:, h, :], sums[:, h, :]).then_inc(inverted[phase], 1)

                def copy_turned(b, h, tiles):
                    for n in turned(phase, h, tiles):
                        if not scalar_copies(phase, h, n):
                            t_ring[phase].wait_full(dve, b, n)
                            c, cols = (0, 5 * T) if phase == 0 else ((n - NT * h) * S, S)
                            t_ring[phase].freed(dve.tensor_copy(pT[0:T, h % 4, c:c + cols], TP[n % 2][0:T, 0:cols]), n)

                def lo_out(b, m):
                    dve.wait_ge(o_hi_done, b * HP + (m + 1))
                    dve.scalar_tensor_tensor(out=oT_lo[:, m, :], in0=OB[:, 0:S], scalar=col_bias[:, 2, m:m + 1],
                                             in1=oT_hi[:, m, :].bitcast(F32), op0=ALU.add, op1=ALU.subtract)\
                       .then_inc(o_lo_done[0], 1)

                def tile_stats(src, t):
                    chain.step(dve.bn_stats(bn[:, t, :], src[:, t, :]))

                def norm_stats(ph, src):
                    steps = vector_chains[ph]
                    for t in range(NT if src is not None else 0):
                        steps.step(dve.bn_stats(bn[:, t, :], src[:, t, :]))
                    steps.wait()
                    plain(dve)
                    for t in range(NT):
                        steps.step(dve.bn_aggr(mean_var[:, t, :], bn[:, t, :]))
                    steps.wait()
                    dve.tensor_scalar(rstd[:, :], mean_var[:, :, 1], EPS, None, ALU.add).then_inc(stats[ph], 1)

                def norm_apply(ph, count, src, dst):
                    dve.wait_ge(rooted[ph], count)
                    for t in range(NT):
                        ins = dve.tensor_scalar(dst[:, t, :], src[:, t, :], mean_var[:, t, 0:1], rstd[:, t:t + 1],
                                                ALU.subtract, ALU.mult)
                        if t < NT - 1:
                            vector_chains[ph].step(ins)
                    ins.then_inc(normed[ph], 1)

                def input_stats(ph, b):
                    dve.wait_ge(entry_in[ph], 16 * b + 16)
                    vector_chains[ph].start(b)
                    norm_stats(ph, h_in)

                def input_apply(ph, b):
                    norm_apply(ph, b + 1, h_in, mv if ph == 1 else work)

                def centre(x_ap, tiles, gain):
                    for t in tiles:
                        chain.step(dve.scalar_tensor_tensor(out=x_ap[:, t, :], in0=x_ap[:, t, :],
                                                            scalar=mean_var[:, t, 0:1], in1=rows_bc[:, gain, :],
                                                            op0=ALU.subtract, op1=ALU.mult))

                def spread(x_ap, tiles, shift):
                    chain.wait()
                    for t in tiles:
                        ins = dve.scalar_tensor_tensor(out=x_ap[:, t, :], in0=x_ap[:, t, :], scalar=rstd[:, t:t + 1],
                                                       in1=rows_bc[:, shift, :], op0=ALU.mult, op1=ALU.add)
                    if NT - 1 in tiles:
                        ins.then_inc(normed[0], 1)

                def ahead(b, name):
                    kind, i = name[:-1], int(name[-1])
                    if kind == "x":
                        lo(b, name, xT_hi[:, i, :], xT_lo[:, i, :])
                    elif kind == "mq":
                        lo(b, name, q_hi[:, i, :], q_lo[:, i, :], mem_bias[:, 0, i:i + 1])
                    elif kind == "mk":
                        lo(b, name, k_hi[:, i, :], k_lo[:, i, :], mem_bias[:, 1, i:i + 1])
                    elif kind in ("q", "k"):
                        lo_qk(b, kind, i)

                def max_memory(b):
                    for t in range(NT):
                        s_ring[0].wait_full(dve, b, t)
                        dve.tensor_reduce(neg_max[:, H, t:t + 1], SC[t][0:T, 0:S], AX.X, ALU.max, negate=True)\
                           .then_inc(maxed[0], 1)

                def keep_input(b):
                    dve.wait_ge(normed[1], b + 1)
                    dve.tensor_tensor(keep[:, :, :], h_in[:, :, :], mv[:, :, :], ALU.add).then_inc(kept, 1)

                def gate_sum(b, n_entry):
                    dve.wait_ge(stored[0], 16 * b + PRIMED)
                    for t in range(NT):
                        n = f"g{t}"
                        a.wait_full(dve, b, n)
                        a.freed(dve.tensor_tensor(tmp[:, t, :], A[a.slot(n)][0:T, 0:D], rows_bc[:, GB, :], ALU.add), n)
                        if t == 0 and n_entry is not None:
                            invert(n_entry, 0)

                def memory_sums(b):
                    s_ring[0].wait_all_freed(dve, b, range(NT))
                    p_ring[0].filled(dve.reciprocal(recip[:, H, :], sums[:, H, :]), 0)

                def turned_memory(b, t):
                    t_ring[0].wait_full(dve, b, t)
                    t_ring[0].freed(dve.tensor_copy(pT[0:T, 2, t * S:t * S + S], TP[0][0:T, 0:S]), t)

                def entry(b, n):
                    def between(at):
                        if n is not None:
                            for name in AHEAD[phase].get(at, ()):
                                ahead(n, name)

                    if phase == 0:
                        chain.start(b)
                    normed_next = (phase + 1, FIRST) if n is None else (1, n) if phase else None
                    for h in range(1, H + LAG + 1):
                        if LAG <= h < H + LAG:
                            copy_turned(b, h - LAG, (0, 1))
                        if h < H:
                            max_head(b, h)
                        if LAG <= h < H + LAG:
                            copy_turned(b, h - LAG, (2,))
                        if phase == 0 and (h - 1 - LAG) % 2 == 0 and h - 1 > LAG:
                            lo_out(b, (h - 1 - LAG) // 2 - 1)
                        if phase == 0 and 2 <= h <= H:
                            invert(b, h - 1)
                        for c, m in low_at(phase, h):
                            lo_qk(b, c, m)
                        if phase == 1 and h < H:
                            invert(b, h)
                        if phase == 0 and h == 1:
                            turned_memory(b, 2)
                        if phase == 0 and h == MEMORY_OUT_AT:
                            p_ring[0].wait_full(dve, b, 0)
                            dve.wait_ge(gated, b + PRIMED)
                            for t in range(NT):
                                name = f"mo{t}"
                                a.wait_full(dve, b, name)
                                a.freed(dve.scalar_tensor_tensor(out=keep[:, t, :], in0=A[a.slot(name)][0:T, 0:D],
                                                                 scalar=recip[:, H, t:t + 1], in1=rows_bc[:, MBV, :],
                                                                 op0=ALU.mult, op1=ALU.add), name)
                                a.wait_freed(dve, b, name)
                                tile_stats(keep, t)
                            norm_stats(0, None)
                        if phase == 0 and MEMORY_OUT_AT + 2 <= h < MEMORY_OUT_AT + 2 + NT:
                            t = h - MEMORY_OUT_AT - 2
                            if t == 0:
                                dve.wait_ge(rooted[0], 2 * b + 1)
                            centre(keep, (t,), G2W)
                            spread(keep, (t,), G2B)
                        if phase == 1 and h == FIRST_SCORES_AT and n is not None:
                            max_head(n, 0)
                        between(h)
                        if phase == 1 and h == FIRST_SCORES_AT and n is not None:
                            invert(n, 0)
                        if normed_next and h == NORM_AT:
                            input_stats(*normed_next)
                        if normed_next and h == NORM_AT + 2:
                            input_apply(*normed_next)
                        if phase == 0 and h == MEMORY_AT and n is not None:
                            max_memory(n)
                        if n is None and SPLIT_AT <= h < SPLIT_AT + HEAD_SPLITS[phase]:
                            if phase == 1 and h == SPLIT_AT:
                                lo_n[0] += 1
                                dve.wait_ge(w_hi_done, lo_n[0])
                                dve.tensor_tensor(router_lo[:, :, :], router[:, :, :], router_hi[:, :, :].bitcast(F32),
                                                  ALU.subtract).then_inc(w_lo_done, 1)
                            split(phase + 1, h - SPLIT_AT, h - SPLIT_AT + 1)
                    if phase == 0:
                        lo_out(b, HP - 1)
                    if phase:
                        for g in range(HP // 2):
                            gelu_high(b, g)
                            if g % 2:
                                dve.wait_ge(gelu_hi, b * (HP // 2) + (g + 1))
                                dve.tensor_tensor(oT_lo[:, 2 * g:2 * g + 2, :], o_raw[:, 2 * g:2 * g + 2, :],
                                                  oT_hi[:, 2 * g:2 * g + 2, :].bitcast(F32), ALU.subtract)\
                                   .then_inc(gelu_lo[1], 1)
                    if n is None:
                        split(phase + 1, HEAD_SPLITS[phase], EARLY_PIECES)
                    between("a")
                    if phase == 0:
                        for t in range(NT):
                            name = f"wo{t}"
                            a.wait_full(dve, b, name)
                            a.freed(dve.tensor_tensor(work[:, t, :], A[a.slot(name)][0:T, 0:D], rows_bc[:, BO, :],
                                                      ALU.add), name)
                            a.wait_freed(dve, b, name)
                            tile_stats(work, t)
                        norm_stats(0, None)
                        centre(work, range(NT), G1W)
                        between("b")
                        dve.wait_ge(rooted[0], 2 * b + 2)
                        spread(work, range(NT), G1B)
                        lo(b, "c2", oT_hi[:, 2, :], oT_lo[:, 2, :])
                        lo(b, "c3", oT_hi[:, 3, :], oT_lo[:, 3, :])
                        between("c")
                        lo(b, "c0", oT_hi[:, 0, :], oT_lo[:, 0, :])
                        lo(b, "c1", oT_hi[:, 1, :], oT_lo[:, 1, :])
                        between("d")
                        if n is not None:
                            max_head(n, 0)
                            memory_sums(n)
                        gate_sum(b, n)
                        between("e")
                        if n is not None:
                            turned_memory(n, 0)
                        chain.end()
                    else:
                        between("b")
                        between("c")
                        dve.wait_ge(stored[1], 16 * b + PRIMED)
                        for t in range(NT):
                            name = f"wo{t}"
                            a.wait_full(dve, b, name)
                            a.freed(dve.tensor_tensor(tmp[:, t, :], A[a.slot(name)][0:T, 0:D], keep[:, t, :], ALU.add),
                                    name)
                        if n is not None:
                            a.wait_all_freed(dve, b, wo_a)
                            keep_input(n)

                def gelu_high(b, g):
                    dve.wait_ge(gelu_done, b * (HP // 2) + (g + 1))
                    dve.tensor_copy(oT_hi[:, 2 * g:2 * g + 2, :], o_raw[:, 2 * g:2 * g + 2, :]).then_inc(gelu_hi, 1)

                if phase < 2:
                    for name in early[phase]:
                        if name == "mv0":
                            max_memory(FIRST)
                        if name == HEAD_0_BEFORE[phase]:
                            if phase == 0:
                                memory_sums(FIRST)
                            max_head(FIRST, 0)
                        ahead(FIRST, name)
                        if phase == 0 and name in START_SPLITS:
                            split(0, *START_SPLITS[name])
                        if phase == 1 and name in LATE_SPLITS:
                            split(1, *LATE_SPLITS[name])
                        if phase == 1 and name == "v0":
                            dve.wait_ge(gated, B + PRIMED)
                            keep_input(FIRST)
                    invert(FIRST, 0)
                    if phase == 0:
                        turned_memory(FIRST, 0)
                    else:
                        dve.wait_ge(stored[0], 16 * B + PRIMED)
                    with dve.Fori(0, B - 1) as b:
                        entry(b, b + 1)
                    entry(B - 1, None)
                    continue

                def square(b, e):
                    for i in range(EC * e, EC * e + EC):
                        a.wait_freed(dve, b, f"h{e}_{i % EC}")
                        if i >= 4 or b is not FIRST:
                            dve.wait_ge(hidden_lo, b * (E * EC) + (i - 3))
                        rectified = pT[:, i % 4, S:2 * S]
                        dve.tensor_tensor(pT[:, i % 4, 0:S], rectified, rectified, ALU.mult).then_inc(squared, 1)

                def best_two(b):
                    a.wait_full(dve, b, "lt")
                    a.freed(dve.tensor_copy(logits[:, :, :].rearrange("p t e -> p (t e)"),
                                            A[a.slot("lt")][0:T, 0:NT * E]), "lt")
                    square(b, 1)
                    a.wait_freed(dve, b, "lt")
                    plain(dve)
                    for t in range(NT):
                        chain.step(dve.max(top[:, t, :], logits[:, t, :]))
                    chain.wait()
                    plain(dve)
                    for t in range(NT):
                        chain.step(dve.max_index(top_no[:, t, :], top[:, t, :], logits[:, t, :]))
                    dve.tensor_tensor(route[:, :, 0], top[:, :, 1], top[:, :, 0], ALU.subtract)\
                       .then_inc(margin_ready, 1)

                def shares(b):
                    chain.start(b, SHARES_FROM)
                    chain.wait()
                    chain.step(dve.tensor_copy(top_nof[:, :, :], top_no[:, :, 0:2]))
                    dve.wait_ge(margin_exp, b + 1)
                    chain.link(dve.tensor_scalar(route[:, :, 2], route[:, :, 1], 1.0, None, ALU.add))
                    chain.link(dve.reciprocal(route[:, :, 2], route[:, :, 2]))
                    chain.link(dve.tensor_tensor(route[:, :, 3], route[:, :, 1], route[:, :, 2], ALU.mult))
                    for t in range(NT):
                        for i in range(2):
                            chain.step(dve.tensor_scalar(gates[:, i, t, :], expert_no[:, :], top_nof[:, t, i:i + 1],
                                                         route[:, t, 2 + i:3 + i], ALU.is_equal, ALU.mult))
                    chain.wait()
                    chain.link(dve.tensor_tensor(gates[:, 0, :, :], gates[:, 0, :, :], gates[:, 1, :, :], ALU.add))
                    chain.end()

                def gather(b, e):
                    for t in range(NT):
                        n = NT * e + t
                        o_banks.wait_full(dve, b, n)
                        if e:
                            o_banks.wait_freed(dve, b, n - NT)
                        src = h_in if e == 0 else keep
                        dst = tmp if e == E - 1 else keep
                        o_banks.freed(dve.scalar_tensor_tensor(
                            out=dst[:, t, :], in0=(SC + TP + [OB])[n % 6][0:T, 0:D], scalar=gates[:, 0, t, e:e + 1],
                            in1=src[:, t, :], op0=ALU.mult, op1=ALU.add), n)

                def inputs(b):
                    lo(b, "x0", xT_hi[:, 0, :], xT_lo[:, 0, :])
                    lo(b, "x1", xT_hi[:, 1, :], xT_lo[:, 1, :])

                def experts(b, n):
                    for e in range(2, E):
                        square(b, e)
                        if e == 2:
                            shares(b)
                        gather(b, e - 2)
                        if e == EXPERT_NORM_AT and n is not None:
                            input_stats(2, n)
                        if e == EXPERT_NORM_AT + 1 and n is not None:
                            input_apply(2, n)
                    if n is not None:
                        inputs(n)
                    gather(b, E - 2)
                    if n is not None:
                        square(n, 0)
                    dve.wait_ge(stored[2], 16 * b + PRIMED)
                    gather(b, E - 1)
                    if n is not None:
                        best_two(n)

                inputs(FIRST)
                split(2, EARLY_PIECES, len(pieces[2]))
                square(FIRST, 0)
                best_two(FIRST)
                dve.wait_ge(stored[1], 16 * B + PRIMED)
                with dve.Fori(0, B - 1) as b:
                    experts(b, b + 1)
                experts(B - 1, None)


def kernel(**inputs):
    import numpy as _np
    import concourse.bacc as _bacc
    from concourse import mybir as _mybir
    from concourse.bass_utils import run_bass_kernel_spmd as _run

    nc = _bacc.Bacc("TRN2", target_bir_lowering=False, num_devices=1)
    arrays, args = {}, {}
    for name, value in inputs.items():
        a = _np.ascontiguousarray(value)
        arrays[f"in_{name}_dram"] = a
        args[name] = nc.dram_tensor(f"in_{name}_dram", a.shape, _mybir.dt.from_np(a.dtype), kind="ExternalInput").ap()
    out = nc.dram_tensor("out_0_dram", (B, S, D), F32, kind="ExternalOutput").ap()
    build(nc, out, **args)
    r = _run(nc, [arrays], core_ids=[0])
    return r.results[0]["out_0_dram"]
```
